# Optimizing a Trainium2 kernel written in Bass

```python
import numpy as np
import jax
import jax.numpy as jnp

def _softmax(x, axis=-1):
    return jax.nn.softmax(x, axis=axis)

def _gelu(x):
    return jax.nn.gelu(x, approximate=True)

def _silu(x):
    return jax.nn.silu(x)

def _sigmoid(x):
    return jax.nn.sigmoid(x)

def _layernorm(x, axis=-1, eps=1e-05):
    m = jnp.mean(x, axis=axis, keepdims=True)
    v = jnp.var(x, axis=axis, keepdims=True)
    return (x - m) / jnp.sqrt(v + eps)

def _scatter_add(tgt, idx, src, axis=0):
    return tgt.at[idx].add(src)

def _segment_sum(src, seg, n):
    return jax.ops.segment_sum(src, seg, n)
kernel_name = 'mk_decoder_preln_d1_seqx_r8_8889a7'

def setup_inputs(seed: int=0):
    np.random.seed(seed)
    _w = jnp.asarray

    def _rec_inputs():
        import jax
        import jax.numpy as jnp
        _rk = jax.random.key(seed)
        x = -0.000125 + 0.9999 * jax.random.normal(jax.random.fold_in(_rk, 1), (8, 256, 256), jnp.float32)
        _lenS = 256 - jax.random.randint(jax.random.fold_in(_rk, 7), (8,), 0, max(1, 256 // 4) + 1, jnp.int32)
        _lenS2 = 1601 - jax.random.randint(jax.random.fold_in(_rk, 8), (8,), 0, max(1, 1601 // 4) + 1, jnp.int32)
        _ctx_2048P = jax.random.normal(jax.random.fold_in(_rk, 11), (8, 16, 256), jnp.float32)
        _ctx_2048c = jax.random.dirichlet(jax.random.fold_in(_rk, 511), 0.3 * jnp.ones((16,), jnp.float32), (8, 1601))
        _ctx_2048t = jnp.einsum('bsk,bkd->bsd', _ctx_2048c, _ctx_2048P)
        _ctx_2048t = _ctx_2048t * jax.lax.rsqrt(jnp.mean(jnp.square(_ctx_2048t)) + 1e-12) * 0.953939
        ctx_2048 = 1.72703e-05 + 1.00003 * (_ctx_2048t + 0.3 * jax.random.normal(jax.random.fold_in(_rk, 611), (8, 1601, 256), jnp.float32))
        return (x, ctx_2048)
    x, ctx_2048 = _rec_inputs()

    def _L0_attn_setup():
        import jax, jax.numpy as jnp
        import numpy as np
        HQ, HKV, HD, WIN = (16, 4, 128, 64)

        def _sliding_window_attention(q, k, v, win):
            B, H, S, hd = q.shape
            W = win
            nb = S // W
            qb = q.reshape(B, H, nb, W, hd)
            kpad = jnp.pad(k, ((0, 0), (0, 0), (W, 0), (0, 0)))
            vpad = jnp.pad(v, ((0, 0), (0, 0), (W, 0), (0, 0)))
            kb = jnp.concatenate([kpad[:, :, :S].reshape(B, H, nb, W, hd), k.reshape(B, H, nb, W, hd)], axis=3)
            vb = jnp.concatenate([vpad[:, :, :S].reshape(B, H, nb, W, hd), v.reshape(B, H, nb, W, hd)], axis=3)
            scores = jnp.einsum('bhnqd,bhnkd->bhnqk', qb, kb) / jnp.asarray(hd, qb.dtype)
            qi = jnp.arange(W)[:, None]
            ki = jnp.arange(2 * W)[None, :]
            band = (ki >= qi + 1) & (ki <= qi + W)
            blk = jnp.arange(nb)[:, None, None]
            valid = band[None] & ((blk > 0) | (ki[None] >= W))
            neg = jnp.finfo(scores.dtype).min
            scores = jnp.where(valid[None, None], scores, neg)
            probs = jax.nn.softmax(scores, axis=-1)
            out = jnp.einsum('bhnqk,bhnkd->bhnqd', probs, vb)
            return out.reshape(B, H, S, hd)
        key = jax.random.key(seed)
        k0, k1, k2, k3, k4 = jax.random.split(key, 5)
        B, S, D = (1, 1024, 256)
        std = 0.02
        hidden_states = jax.random.normal(k0, (B, S, D), jnp.float32)
        Wq = jax.random.normal(k1, (D, HQ * HD), jnp.float32) * std
        Wk = jax.random.normal(k2, (D, HKV * HD), jnp.float32) * std
        Wv = jax.random.normal(k3, (D, HKV * HD), jnp.float32) * std
        Wo = jax.random.normal(k4, (HQ * HD, D), jnp.float32) * std
        return {'hidden_states': hidden_states, 'Wq': Wq, 'Wk': Wk, 'Wv': Wv, 'Wo': Wo}
    _L0_attn_all = _L0_attn_setup()
    _L0_attn_in = {k: v for k, v in _L0_attn_all.items() if k in ('Wq', 'Wk', 'Wv', 'Wo')}
    del _L0_attn_all

    def _L0_xattn_setup():
        import jax, jax.numpy as jnp
        import numpy as np
        DIM = 256
        NH = 16
        HD = DIM // NH
        EPS = 1e-06
        IMG_LEN = 257

        def rms_norm(x, w, eps=EPS):
            xf = x.astype(jnp.float32)
            y = xf * jax.lax.rsqrt(jnp.mean(xf * xf, axis=-1, keepdims=True) + eps)
            return y.astype(x.dtype) * w

        def linear(x, w, b):
            return jnp.einsum('blc,oc->blo', x, w) + b

        def attention(q, k, v):
            scale = 1.0 / jnp.sqrt(jnp.asarray(HD, q.dtype))
            scores = jnp.einsum('bqhd,bkhd->bhqk', q, k) * scale
            probs = jax.nn.softmax(scores, axis=-1)
            return jnp.einsum('bhqk,bkhd->bqhd', probs, v)
        key = jax.random.key(seed)
        ks = jax.random.split(key, 12)
        B, L = (2, 1024)
        s = 0.02
        inp = {'x': jax.random.normal(ks[0], (B, L, DIM), jnp.float32), 'context': jax.random.normal(ks[1], (B, 769, DIM), jnp.float32), 'q_w': jax.random.normal(ks[2], (DIM, DIM), jnp.float32) * s, 'q_b': jnp.zeros((DIM,), jnp.float32), 'k_w': jax.random.normal(ks[3], (DIM, DIM), jnp.float32) * s, 'k_b': jnp.zeros((DIM,), jnp.float32), 'v_w': jax.random.normal(ks[4], (DIM, DIM), jnp.float32) * s, 'v_b': jnp.zeros((DIM,), jnp.float32), 'k_img_w': jax.random.normal(ks[5], (DIM, DIM), jnp.float32) * s, 'k_img_b': jnp.zeros((DIM,), jnp.float32), 'v_img_w': jax.random.normal(ks[6], (DIM, DIM), jnp.float32) * s, 'v_img_b': jnp.zeros((DIM,), jnp.float32), 'o_w': jax.random.normal(ks[7], (DIM, DIM), jnp.float32) * s, 'o_b': jnp.zeros((DIM,), jnp.float32), 'norm_q_w': jnp.ones((DIM,), jnp.float32), 'norm_k_w': jnp.ones((DIM,), jnp.float32), 'norm_k_img_w': jnp.ones((DIM,), jnp.float32)}
        return inp
    _L0_xattn_all = _L0_xattn_setup()
    _L0_xattn_in = {k: v for k, v in _L0_xattn_all.items() if k in ('q_w', 'q_b', 'k_w', 'k_b', 'v_w', 'v_b', 'k_img_w', 'k_img_b', 'v_img_w', 'v_img_b', 'o_w', 'o_b', 'norm_q_w', 'norm_k_w', 'norm_k_img_w')}
    del _L0_xattn_all

    def _L0_ffn_setup():
        import jax, jax.numpy as jnp
        import numpy as np
        B, T, D = (4, 256, 256)
        E = 8
        K = 2
        F = 1024 // (E // 2)
        key = jax.random.key(seed)
        ks = jax.random.split(key, 5)
        s_in = 1.0 / np.sqrt(D)
        s_mid = 1.0 / np.sqrt(F)
        x = jax.random.normal(ks[0], (B, T, D), dtype=jnp.float32)
        Wr = jax.random.normal(ks[1], (D, E), dtype=jnp.float32) * s_in
        Wg = jax.random.normal(ks[2], (E, D, F), dtype=jnp.float32) * s_in
        Wu = jax.random.normal(ks[3], (E, D, F), dtype=jnp.float32) * s_in
        Wd = jax.random.normal(ks[4], (E, F, D), dtype=jnp.float32) * s_mid
        return {'x': x, 'Wr': Wr, 'Wg': Wg, 'Wu': Wu, 'Wd': Wd}
    _L0_ffn_all = _L0_ffn_setup()
    _L0_ffn_in = {k: v for k, v in _L0_ffn_all.items() if k in ('Wr', 'Wg', 'Wu', 'Wd')}
    del _L0_ffn_all
    return {'x': x, 'ctx_2048': ctx_2048, 'L0_attn_Wq': _L0_attn_in['Wq'], 'L0_attn_Wk': _L0_attn_in['Wk'], 'L0_attn_Wv': _L0_attn_in['Wv'], 'L0_attn_Wo': _L0_attn_in['Wo'], 'L0_xattn_q_w': _L0_xattn_in['q_w'], 'L0_xattn_q_b': _L0_xattn_in['q_b'], 'L0_xattn_k_w': _L0_xattn_in['k_w'], 'L0_xattn_k_b': _L0_xattn_in['k_b'], 'L0_xattn_v_w': _L0_xattn_in['v_w'], 'L0_xattn_v_b': _L0_xattn_in['v_b'], 'L0_xattn_k_img_w': _L0_xattn_in['k_img_w'], 'L0_xattn_k_img_b': _L0_xattn_in['k_img_b'], 'L0_xattn_v_img_w': _L0_xattn_in['v_img_w'], 'L0_xattn_v_img_b': _L0_xattn_in['v_img_b'], 'L0_xattn_o_w': _L0_xattn_in['o_w'], 'L0_xattn_o_b': _L0_xattn_in['o_b'], 'L0_xattn_norm_q_w': _L0_xattn_in['norm_q_w'], 'L0_xattn_norm_k_w': _L0_xattn_in['norm_k_w'], 'L0_xattn_norm_k_img_w': _L0_xattn_in['norm_k_img_w'], 'L0_ffn_Wr': _L0_ffn_in['Wr'], 'L0_ffn_Wg': _L0_ffn_in['Wg'], 'L0_ffn_Wu': _L0_ffn_in['Wu'], 'L0_ffn_Wd': _L0_ffn_in['Wd']}

def reference(x, ctx_2048, L0_attn_Wq, L0_attn_Wk, L0_attn_Wv, L0_attn_Wo, L0_xattn_q_w, L0_xattn_q_b, L0_xattn_k_w, L0_xattn_k_b, L0_xattn_v_w, L0_xattn_v_b, L0_xattn_k_img_w, L0_xattn_k_img_b, L0_xattn_v_img_w, L0_xattn_v_img_b, L0_xattn_o_w, L0_xattn_o_b, L0_xattn_norm_q_w, L0_xattn_norm_k_w, L0_xattn_norm_k_img_w, L0_ffn_Wr, L0_ffn_Wg, L0_ffn_Wu, L0_ffn_Wd):
    import jax
    import jax.numpy as jnp

    def _L0_attn_ref(hidden_states, Wq, Wk, Wv, Wo):
        import jax, jax.numpy as jnp
        import numpy as np
        HQ, HKV, HD, WIN = (16, 4, 128, 64)

        def _sliding_window_attention(q, k, v, win):
            B, H, S, hd = q.shape
            W = win
            nb = S // W
            qb = q.reshape(B, H, nb, W, hd)
            kpad = jnp.pad(k, ((0, 0), (0, 0), (W, 0), (0, 0)))
            vpad = jnp.pad(v, ((0, 0), (0, 0), (W, 0), (0, 0)))
            kb = jnp.concatenate([kpad[:, :, :S].reshape(B, H, nb, W, hd), k.reshape(B, H, nb, W, hd)], axis=3)
            vb = jnp.concatenate([vpad[:, :, :S].reshape(B, H, nb, W, hd), v.reshape(B, H, nb, W, hd)], axis=3)
            scores = jnp.einsum('bhnqd,bhnkd->bhnqk', qb, kb) / jnp.asarray(hd, qb.dtype)
            qi = jnp.arange(W)[:, None]
            ki = jnp.arange(2 * W)[None, :]
            band = (ki >= qi + 1) & (ki <= qi + W)
            blk = jnp.arange(nb)[:, None, None]
            valid = band[None] & ((blk > 0) | (ki[None] >= W))
            neg = jnp.finfo(scores.dtype).min
            scores = jnp.where(valid[None, None], scores, neg)
            probs = jax.nn.softmax(scores, axis=-1)
            out = jnp.einsum('bhnqk,bhnkd->bhnqd', probs, vb)
            return out.reshape(B, H, S, hd)
        B, S, D = hidden_states.shape
        q = (hidden_states @ Wq).reshape(B, S, HQ, HD).transpose(0, 2, 1, 3)
        k = (hidden_states @ Wk).reshape(B, S, HKV, HD).transpose(0, 2, 1, 3)
        v = (hidden_states @ Wv).reshape(B, S, HKV, HD).transpose(0, 2, 1, 3)
        rep = HQ // HKV
        k = jnp.repeat(k, rep, axis=1)
        v = jnp.repeat(v, rep, axis=1)
        attn = _sliding_window_attention(q, k, v, WIN)
        attn = attn.transpose(0, 2, 1, 3).reshape(B, S, HQ * HD)
        return attn @ Wo

    def _L0_xattn_ref(x, context, q_w, q_b, k_w, k_b, v_w, v_b, k_img_w, k_img_b, v_img_w, v_img_b, o_w, o_b, norm_q_w, norm_k_w, norm_k_img_w):
        import jax, jax.numpy as jnp
        import numpy as np
        DIM = 256
        NH = 16
        HD = DIM // NH
        EPS = 1e-06
        IMG_LEN = 257

        def rms_norm(x, w, eps=EPS):
            xf = x.astype(jnp.float32)
            y = xf * jax.lax.rsqrt(jnp.mean(xf * xf, axis=-1, keepdims=True) + eps)
            return y.astype(x.dtype) * w

        def linear(x, w, b):
            return jnp.einsum('blc,oc->blo', x, w) + b

        def attention(q, k, v):
            scale = 1.0 / jnp.sqrt(jnp.asarray(HD, q.dtype))
            scores = jnp.einsum('bqhd,bkhd->bhqk', q, k) * scale
            probs = jax.nn.softmax(scores, axis=-1)
            return jnp.einsum('bhqk,bkhd->bqhd', probs, v)
        B, L, _ = x.shape
        ctx_img = context[:, :IMG_LEN]
        ctx_txt = context[:, IMG_LEN:]
        q = rms_norm(linear(x, q_w, q_b), norm_q_w).reshape(B, L, NH, HD)
        k = rms_norm(linear(ctx_txt, k_w, k_b), norm_k_w).reshape(B, -1, NH, HD)
        v = linear(ctx_txt, v_w, v_b).reshape(B, -1, NH, HD)
        k_img = rms_norm(linear(ctx_img, k_img_w, k_img_b), norm_k_img_w).reshape(B, -1, NH, HD)
        v_img = linear(ctx_img, v_img_w, v_img_b).reshape(B, -1, NH, HD)
        img_x = attention(q, k_img, v_img)
        txt_x = attention(q, k, v)
        out = (txt_x + img_x).reshape(B, L, DIM)
        return linear(out, o_w, o_b)

    def _L0_ffn_ref(x, Wr, Wg, Wu, Wd):
        import jax, jax.numpy as jnp
        import numpy as np
        B, T, D = (4, 256, 256)
        E = 8
        K = 2
        F = 1024 // (E // 2)
        probs = jax.nn.softmax(x @ Wr, axis=-1)
        topk_w, topk_idx = jax.lax.top_k(probs, K)
        topk_w = topk_w / jnp.sum(topk_w, axis=-1, keepdims=True)
        output = jnp.zeros_like(x)
        for i in range(E):
            sel = topk_idx == i
            w_i = jnp.sum(topk_w * sel.astype(x.dtype), axis=-1, keepdims=True)
            h = jax.nn.silu(x @ Wg[i]) * (x @ Wu[i])
            e_out = h @ Wd[i]
            output = output + w_i * e_out
        return output
    x = x + _L0_attn_ref(_layernorm(x, axis=-1), L0_attn_Wq, L0_attn_Wk, L0_attn_Wv, L0_attn_Wo)
    x = x + _L0_xattn_ref(_layernorm(x, axis=-1), ctx_2048, L0_xattn_q_w, L0_xattn_q_b, L0_xattn_k_w, L0_xattn_k_b, L0_xattn_v_w, L0_xattn_v_b, L0_xattn_k_img_w, L0_xattn_k_img_b, L0_xattn_v_img_w, L0_xattn_v_img_b, L0_xattn_o_w, L0_xattn_o_b, L0_xattn_norm_q_w, L0_xattn_norm_k_w, L0_xattn_norm_k_img_w)
    x = x + _L0_ffn_ref(_layernorm(x, axis=-1), L0_ffn_Wr, L0_ffn_Wg, L0_ffn_Wu, L0_ffn_Wd)
    return x

_drawn_inputs = setup_inputs


def setup_inputs(seed=0):
    import zlib

    import numpy as np

    out = dict(_drawn_inputs(seed))
    spreads = {'L0_xattn_q_b': (0.0, 0.277),
     'L0_xattn_k_b': (0.0, 0.8),
     'L0_xattn_v_b': (0.0, 0.1),
     'L0_xattn_k_img_b': (0.0, 0.795),
     'L0_xattn_v_img_b': (0.0, 0.1),
     'L0_xattn_o_b': (0.0, 0.1),
     'L0_xattn_norm_q_w': (1.0, 0.6),
     'L0_xattn_norm_k_w': (1.0, 0.6),
     'L0_xattn_norm_k_img_w': (1.0, 0.6)}
    factors = {'L0_attn_Wq': 8.0, 'L0_attn_Wk': 8.0}
    for name, (base, spread) in spreads.items():
        noise = np.random.default_rng([zlib.crc32(name.encode()), seed]).standard_normal(out[name].shape)
        drawn = base * np.exp(spread * noise) if base else spread * noise
        out[name] = jnp.asarray(drawn.astype(out[name].dtype))
    for name, factor in factors.items():
        out[name] = (out[name] * factor).astype(out[name].dtype)
    return out
```

```python
import concourse.bass as bass
from concourse import mybir
from contextlib import ExitStack

F32 = mybir.dt.float32
BF16 = mybir.dt.bfloat16
I32 = mybir.dt.int32
ALU = mybir.AluOpType
ACT = mybir.ActivationFunctionType
X_AXIS = mybir.AxisListType.X

P = 128
B, S, D = 8, 256, 256
NT = B * S // P
FT = D // P
LN_EPS, RMS_EPS = 1e-5, 1e-6

HQ, HKV, HD, WIN = 16, 4, 128, 64
NBLK = S // WIN
NSTEP = NBLK * 2
P_RING = 4

NH, XD = 16, 16
N_TXT, N_IMG = 1344, 257
NKEY = N_TXT + N_IMG
KT_TILES = -(-NKEY // P)
LAST = NKEY - (KT_TILES - 1) * P
MIX = N_TXT // P
HALF = N_TXT - MIX * P
NG = 4
XSTEP = NG * KT_TILES
PARTS = [(0, 0), (0, 1), (1, 0), (1, 1), (0, 2), (2, 0)]
KROWS = 16 * len(PARTS)
MAXN = N_TXT // 3
MAX_CHUNKS = [(0, MAXN), (MAXN, MAXN), (2 * MAXN, MAXN), (N_TXT, N_IMG)]
UNITS = 4 * 2 * len(MAX_CHUNKS)
XP_RING = 4
CHUNKS = [(0, 2), (2, 4), (4, 6), (6, 8), (8, 10), (10, 11), (11, 13)]
NCH = len(CHUNKS)
VW = XD + 1

E, F = 8, 256
TG = 4


def kinds_of(t):
    return [(0, 0, P)] if t < MIX else [(0, 0, HALF), (1, HALF, P)] if t == MIX else [(1, 0, key_count(t))]


def v_slots(t):
    return (t,) if t < MIX else (MIX, MIX + 1) if t == MIX else (t + 1,)


def key_count(t):
    return LAST if t == KT_TILES - 1 else P


def attention_events(tail, prep, at_start=False):
    ev = []
    misc1 = {s: [] for s in range(XSTEP)}
    misc2 = {s: [] for s in range(XSTEP)}
    if tail:
        misc1[2] += [("otr", -1, 3)]
        misc1[4] += [("atr", -1)]
        misc1[6] += [("oproj", -1)]
    for hg in range(NG - 1):
        misc1[KT_TILES * (hg + 1) + 2] += [("otr", 0, hg)]
    for hg in range(NG - 1 + prep):
        misc1[KT_TILES * hg + 11] += [("mpost", hg + 1)]
    if prep:
        misc2[0] += [("ln",), ("xT",)]
        misc2[1] += [("q",)]
        for t in range(KT_TILES):
            misc2[1 + t] += [("ct", t)]
            misc2[2 + t] += [("kv", t)]
        misc2[2 + KT_TILES] += [("rms",), ("sc", 0), ("sc", 1)]
        misc2[4 + KT_TILES] += [("qt",)]
        for j in range(NCH):
            misc2[5 + KT_TILES + j] += [("kt", j)]
            if j + 2 <= NCH:
                misc2[4 + KT_TILES + j] += [("sc", j + 2)]
            misc2[6 + KT_TILES + j] += [("k2", j)]
        misc2[6 + KT_TILES + NCH] += [("k2", NCH), ("ctx",), ("kq", 0), ("kq", 1)]
        misc2[3 * KT_TILES + 1] += [("kq", 2)]
    for s in range(XSTEP):
        hg, t = divmod(s, KT_TILES)
        ev.append(("st", s))
        ev += misc1[s]
        if hg < NG - 1 or prep:
            ev += [("mx", hg + 1, u) for u in range(3 * t, min(3 * t + 3, UNITS))]
            if t == UNITS // 3:
                ev.append(("mred", hg + 1))
        if s:
            ev.append(("pv", 0, s - 1))
        elif tail:
            ev.append(("pv", -1, XSTEP - 1))
        if s == 0:
            ev += [("vc", 0, KT_TILES - 2), ("vc", 0, KT_TILES - 1)]
        if t == 0 and (hg or tail):
            ev.append(("oev", 0, hg - 1) if hg else ("oev", -1, NG - 1))
        if prep and s - 3 * KT_TILES - 2 >= 0:
            ev.append(("vc", 1, s - 3 * KT_TILES - 2))
        ev += misc2[s]
    if prep:
        ev.append(("kq", 3))
    return ev


def first_events():
    ev = [("ctx0",), ("ln",), ("xT",), ("q",)]
    for t in range(KT_TILES + 1):
        if t < KT_TILES:
            ev.append(("ct", t))
        if t:
            ev.append(("kv", t - 1))
    ev += [("vc", 1, t) for t in range(KT_TILES - 2)]
    ev += [("rms",)] + [("sc", j) for j in range(NCH + 1)] + [("qt",)]
    for j in range(NCH):
        ev += [("kt", j), ("k2", j)]
    ev += [("k2", NCH), ("ctx",)] + [("kq", g) for g in range(NG)]
    for u in range(UNITS):
        ev.append(("mx", NG, u))
    return ev + [("mred", NG), ("mpost", NG)]


def last_events():
    return [("pv", -1, XSTEP - 1), ("oev", -1, NG - 1), ("otr", -1, NG - 1), ("atr", -1), ("oproj", -1)]


MISC = ("xT", "q", "ct", "kv", "qt", "kt", "mpost", "otr", "atr", "oproj")

TURNS = {
    "first": first_events(),
    "head": attention_events(tail=False, prep=True),
    "body": attention_events(tail=True, prep=True),
    "foot": attention_events(tail=True, prep=False),
    "last": last_events(),
}
MISC_COUNT = {k: sum(e[0] in MISC for e in v) for k, v in TURNS.items()}


def numbered(turn, b):
    base = {
        "first": 0,
        "head": MISC_COUNT["first"],
        "body": MISC_COUNT["first"] + MISC_COUNT["head"] + (b - 1) * MISC_COUNT["body"],
        "foot": MISC_COUNT["first"] + MISC_COUNT["head"] + (B - 2) * MISC_COUNT["body"],
        "last": MISC_COUNT["first"] + MISC_COUNT["head"] + (B - 2) * MISC_COUNT["body"] + MISC_COUNT["foot"],
    }[turn]
    n = 0
    out, place = [], {}
    for e in TURNS[turn]:
        out.append((e, base + n))
        if e[0] in MISC:
            place[e] = base + n
            n += 1
    return out, place


def decoder_layer(nc, a, out):
    ctx = ExitStack()
    with ctx:
        def sb(name, shape, dt=F32, stack=ctx):
            return stack.enter_context(nc.sbuf_tensor(name, shape, dt))

        def sem(name):
            return ctx.enter_context(nc.semaphore(name))

        X = sb("X", [P, NT, D])
        ident = sb("ident", [P, P])
        identb = sb("identb", [P, P], BF16)
        stats = sb("stats", [P, NT, 6])
        meanvar = sb("meanvar", [P, NT, 2])
        rstd = sb("rstd", [P, NT])
        newton_v = sb("newton_v", [P, NT])
        newton_t = sb("newton_t", [P, NT])
        newton_i = sb("newton_i", [P, NT], I32)
        newton_y = sb("newton_y", [P, NT], I32)

        pair = [ctx.enter_context(nc.psum_tensor(f"pair{i}", [P, 2, 512], F32)) for i in range(2)]
        bank = [ctx.enter_context(nc.psum_tensor(f"bank{i}", [P, 512], F32)) for i in range(4)]

        with ExitStack() as sa:
            XT = sb("XT", [P, FT, B * S], stack=sa)
            XN = sb("XN", [P, NT, D], stack=sa)
            wq = sb("wq", [P, FT, HQ * HD], stack=sa)
            wk = sb("wk", [P, FT, HKV * HD], stack=sa)
            wv = sb("wv", [P, FT, HKV * HD], stack=sa)
            wo = sb("wo", [P, HQ, D], stack=sa)
            QT = sb("QT", [P, NBLK, HQ, WIN], stack=sa)
            KT = sb("KT", [P, HKV, S], stack=sa)
            VT = sb("VT", [P, HKV, S], stack=sa)
            V = sb("V", [P, 3, HKV * HD], stack=sa)
            PA = sb("PA", [P, P_RING, 512], stack=sa)
            PT = sb("PT", [P, 2, 512], stack=sa)
            OT = sb("OT", [P, HQ, S], stack=sa)
            maskf = sb("maskf", [P, 3, P], stack=sa)
            mask = sb("mask", [P, 3, 4, P], BF16, stack=sa)
            rowmax = sb("rowmax", [P, P_RING, 4], stack=sa)
            negmax = sb("negmax", [P, P_RING, 4], stack=sa)
            rowsum = sb("rowsum", [P, P_RING, 4], stack=sa)
            rowinv = sb("rowinv", [P, P_RING, 4], stack=sa)

        with ExitStack() as sbk:
            xq_w = sb("xq_w", [P, FT, D], stack=sbk)
            xkv_w = [sb(f"xkv_w{i}", [P, FT, 2 * D], stack=sbk) for i in range(2)]
            xo_w = sb("xo_w", [P, FT, D], stack=sbk)
            xq_b = sb("xq_b", [P, D], stack=sbk)
            xkv_b = [sb(f"xkv_b{i}", [P, 2 * D], stack=sbk) for i in range(2)]
            xo_b = sb("xo_b", [P, D], stack=sbk)
            norm_w = sb("norm_w", [P, 3, FT], stack=sbk)
            ctxk = sb("ctxk", [P, KT_TILES, D], stack=sbk)
            xn = sb("xn", [P, FT, D], stack=sbk)
            xT = sb("xT", [P, FT, S], stack=sbk)
            qraw = xn
            ctxT = sb("ctxT", [P, 2, FT, P], stack=sbk)
            Vn = sb("Vn", [P, KT_TILES, D], stack=sbk)
            Vc = sb("Vc", [P, KT_TILES + 1, NH, VW], stack=sbk)
            kw = sb("kw", [P, 2, FT, 2 * P], stack=sbk)
            kp = sb("kp", [P, 3, FT, NKEY], BF16, stack=sbk)
            qw = sb("qw", [P, FT, S], stack=sbk)
            qp = sb("qp", [P, 3, FT, S], BF16, stack=sbk)
            KS = sb("KS", [KROWS + 2, NG, 4, NKEY], BF16, stack=sbk)
            QS = sb("QS", [KROWS + 2, NG, 4, S], BF16, stack=sbk)
            PX = sb("PX", [P, XP_RING, 2, 512], stack=sbk)
            kindf = PX[0:2, :, :, :].rearrange("p a b n -> p (a b n)")[:, 0:NKEY]
            kind = kp[0:2, 0, 0, :]
            Osb = sb("Osb", [P, 2, S], stack=sbk)
            attn = sb("attn", [P, 2, D], stack=sbk)
            attnT = sb("attnT", [P, FT, S], stack=sbk)
            junk = sb("junk", [P, D], stack=sbk)
            oproj = sb("oproj", [P, 2, D], stack=sbk)
            sumsq = sb("sumsq", [P, KT_TILES + 2], stack=sbk)
            kq_rstd = sb("kq_rstd", [P, KT_TILES + 2], stack=sbk)
            xmax = sb("xmax", [P, 2, 4, 4], stack=sbk)
            m8 = sb("m8", [P, 2, 2, 4], stack=sbk)
            mneg = sb("mneg", [P, 2, 8], stack=sbk)
            mT = sb("mT", [8, S], BF16, stack=sbk)
            oinv = sb("oinv", [P, 2, 2, 4], stack=sbk)
            otmp = sb("otmp", [P, 2, 2, 64], stack=sbk)

        with ExitStack() as sc:
            XT3 = sb("XT3", [P, FT, B * S], stack=sc)
            XN3 = sb("XN3", [P, NT, D], stack=sc)
            wr = sb("wr", [P, FT, E], stack=sc)
            tri = sb("tri", [P, E, E], stack=sc)
            wg = sb("wg", [P, 2, FT, F], stack=sc)
            wu = sb("wu", [P, 2, FT, F], stack=sc)
            wd = sb("wd", [P, 2, FT, D], stack=sc)
            logit = sb("logit", [P, NT, E], stack=sc)
            prob = sb("prob", [P, NT, E], stack=sc)
            beats = sb("beats", [P, NT, E, E], stack=sc)
            ties = sb("ties", [P, NT, E, E], stack=sc)
            rank = sb("rank", [P, NT, E], stack=sc)
            gate = sb("gate", [P, NT, E], stack=sc)
            top = sb("top", [P, NT], stack=sc)
            topsum = sb("topsum", [P, NT], stack=sc)
            silu = sb("silu", [P, 2, 512], stack=sc)
            hT = sb("hT", [P, 2, FT, 512], stack=sc)

        chain = sem("chain")
        load_x = [sem(f"load_x{i}") for i in range(4)]
        load_const = sem("load_const")
        load_qkv = sem("load_qkv")
        load_o = sem("load_o")
        const_ready = sem("const_ready")
        xn_ready = sem("xn_ready")
        xt_made = sem("xt_made")
        xt_ready = sem("xt_ready")
        a_kv = sem("a_kv")
        a_kv_evac = sem("a_kv_evac")
        a_q = sem("a_q")
        a_q_evac = sem("a_q_evac")
        a_score = sem("a_score")
        a_negmax = sem("a_negmax")
        a_exp = sem("a_exp")
        a_norm = sem("a_norm")
        a_turned = sem("a_turned")
        a_pt = sem("a_pt")
        a_pv = sem("a_pv")
        a_o_evac = sem("a_o_evac")

        load_b = sem("load_b")
        kind_ready = sem("kind_ready")
        kind_rows = sem("kind_rows")
        b_init = sem("b_init")
        ctx_loaded = sem("ctx_loaded")
        gone_ahead = sem("gone_ahead")
        misc_full = sem("misc_full")
        misc_free = sem("misc_free")
        b_xn = sem("b_xn")
        v_ready = sem("v_ready")
        v_copied = sem("v_copied")
        sq_done = sem("sq_done")
        scaled = sem("scaled")
        r1_done = sem("r1_done")
        k2_done = sem("k2_done")
        split_done = sem("split_done")
        kq_loaded = [sem(f"kq_loaded{g}") for g in range(NG)]
        smax_made = sem("smax_made")
        smax_done = sem("smax_done")
        mneg_ready = sem("mneg_ready")
        mT_ready = sem("mT_ready")
        m_rows = sem("m_rows")
        st_made = sem("st_made")
        exp_done = sem("exp_done")
        pv_done = sem("pv_done")
        o_evac = sem("o_evac")
        attn_part = sem("attn_part")
        x_added = sem("x_added")

        load_r = sem("load_r")
        load_w = [sem(f"load_w{i}") for i in range(2)]
        c_logit = sem("c_logit")
        c_shift = sem("c_shift")
        c_exp = sem("c_exp")
        c_gate = sem("c_gate")
        c_gu = sem("c_gu")
        c_silu = sem("c_silu")
        c_h = sem("c_h")
        c_down = sem("c_down")
        c_down_evac = sem("c_down_evac")
        stored = sem("stored")

        A_KV_EVAC = 9
        A_KV = 7
        CTX_DMAS = 4
        KQ = 16 * 2 * len(PARTS)

        x_flat = a["x"].rearrange("b s d -> (b s) d")
        out_flat = out.rearrange("b s d -> (b s) d")
        block = ctx.enter_context(nc.Block())

        def dve_link(eng):
            count = [0]

            def link(ins):
                count[0] += 1
                ins.then_inc(chain, 1)
                eng.wait_ge(chain, count[0])
            return link

        def inverse_root(eng, link, n, result):
            v, t, y = newton_v[:, 0:n], newton_t[:, 0:n], newton_y[:, 0:n].bitcast(F32)
            link(eng.tensor_single_scalar(newton_i[:, 0:n], v.bitcast(I32), 1, ALU.logical_shift_right))
            link(eng.tensor_scalar(newton_y[:, 0:n], newton_i[:, 0:n], -1.0, float(0x5F3759DF), ALU.mult, ALU.add))
            for k in range(3):
                link(eng.scalar_tensor_tensor(out=t, in0=y, scalar=-0.5, in1=y, op0=ALU.mult, op1=ALU.mult))
                link(eng.tensor_tensor(t, t, v, ALU.mult))
                link(eng.scalar_tensor_tensor(out=y if k < 2 else result, in0=t, scalar=1.5, in1=y,
                                              op0=ALU.add, op1=ALU.mult))

        def norm_stats(eng, loads=False):
            link = dve_link(eng)
            for t in range(NT):
                if loads and t % 4 == 0:
                    eng.wait_ge(load_x[t // 4], 16)
                ins = eng.bn_stats(stats[:, t, :], X[:, t, :])
            link(ins)
            for t in range(NT):
                ins = eng.bn_aggr(meanvar[:, t, :], stats[:, t, :])
            link(ins)
            link(eng.tensor_scalar(newton_v[:, :], meanvar[:, :, 1], 1.0, LN_EPS, ALU.mult, ALU.add))
            inverse_root(eng, link, NT, rstd[:, :])
            eng.sem_clear(chain)

        def norm_rows(eng, dst):
            for t in range(NT):
                ins = eng.tensor_scalar(dst[:, t, :], X[:, t, :], meanvar[:, t, 0:1], rstd[:, t:t + 1],
                                        ALU.subtract, ALU.mult)
                if t % 2:
                    ins.then_inc(xn_ready, 1)

        @block.sync
        def _(sp):
            for i in range(4):
                sp.dma_start(X[:, 4 * i:4 * i + 4, :],
                             x_flat[512 * i:512 * i + 512, :].rearrange("(t p) d -> p t d", p=P)).then_inc(load_x[i], 16)
            sp.dma_start(ident[:, :], a["c_ident"]).then_inc(load_const, 16)
            sp.dma_start(maskf[:, :, :], a["c_mask"]).then_inc(load_const, 16)
            for w, n in ((wk, "L0_attn_Wk"), (wq, "L0_attn_Wq"), (wv, "L0_attn_Wv")):
                sp.dma_start(w[:, :, :], a[n].rearrange("(f p) n -> p f n", p=P)).then_inc(load_qkv, 16)
            sp.dma_start(wo[:, :, :], a["L0_attn_Wo"].rearrange("(h p) n -> p h n", p=P)).then_inc(load_o, 16)

            sp.wait_ge(a_kv_evac, 1 + A_KV_EVAC * B)
            def wt(name):
                return a[name].rearrange("(f p) n -> p f n", p=P)
            sp.dma_start(xq_w[:, :, :], wt("wT_q")).then_inc(load_b, 16)
            for i, s in enumerate(("", "_img")):
                sp.dma_start(xkv_w[i][:, :, 0:D], wt(f"wT_k{s}")).then_inc(load_b, 16)
                sp.dma_start(xkv_w[i][:, :, D:2 * D], wt(f"wT_v{s}")).then_inc(load_b, 16)
                sp.dma_start(xkv_b[i][:, 0:D], a[f"L0_xattn_k{s}_b"].partition_broadcast(P)).then_inc(load_b, 16)
                sp.dma_start(xkv_b[i][:, D:2 * D], a[f"L0_xattn_v{s}_b"].partition_broadcast(P)).then_inc(load_b, 16)
            sp.dma_start(xo_w[:, :, :], wt("wT_o")).then_inc(load_b, 16)
            sp.dma_start(xq_b[:, :], a["L0_xattn_q_b"].partition_broadcast(P)).then_inc(load_b, 16)
            sp.dma_start(xo_b[:, :], a["L0_xattn_o_b"].partition_broadcast(P)).then_inc(load_b, 16)
            for i, n in enumerate(("q", "k", "k_img")):
                for f in range(FT):
                    sp.dma_start(norm_w[:, i, f:f + 1],
                                 a[f"L0_xattn_norm_{n}_w"][f * P:(f + 1) * P].unsqueeze(1)).then_inc(load_b, 16)
            sp.dma_start(kindf, a["c_kind"]).then_inc(load_b, 16)

            c_ = a["ctx_2048"]

            def load_ctx(c):
                cc = c_[bass.ds(c, 1)].rearrange("o k d -> (o k) d")
                sp.dma_start(ctxk[:, 0:MIX, :],
                             cc[N_IMG:N_IMG + MIX * P, :].rearrange("(t p) d -> p t d", p=P)).then_inc(ctx_loaded, 16)
                sp.dma_start(ctxk[0:HALF, MIX, :], cc[N_IMG + MIX * P:NKEY, :]).then_inc(ctx_loaded, 16)
                sp.dma_start(ctxk[HALF:P, MIX, :], cc[0:P - HALF, :]).then_inc(ctx_loaded, 16)
                sp.dma_start(ctxk[:, MIX + 1, :], cc[P - HALF:2 * P - HALF, :]).then_inc(ctx_loaded, 16)
                sp.dma_start(ctxk[0:LAST, MIX + 2, :], cc[2 * P - HALF:N_IMG, :]).then_inc(ctx_loaded, 16)

            def turn(name, b, more=True):
                c = b + 1
                events, place = numbered(name, b)
                for e, n in events:
                    if e[0] == "ctx0":
                        load_ctx(0)
                    elif e[0] == "ctx":
                        sp.wait_ge(misc_full, place[("kt", NCH - 1)] + 1)
                        sp.sem_inc(gone_ahead, 1)
                        if more:
                            load_ctx(c + 1)
                    elif e[0] == "kq":
                        g = e[1]
                        sp.wait_ge(split_done, (NCH + 1) * (c + 1))
                        sp.sem_inc(gone_ahead, 1)
                        if name != "first":
                            sp.wait_ge(st_made, XSTEP * b + KT_TILES * (g + 1))
                            sp.sem_inc(gone_ahead, 1)
                        else:
                            sp.wait_ge(kind_ready, 1)
                        half, r = divmod(g, 2)
                        for i, (pk, pq) in enumerate(PARTS):
                            sp.dma_start(KS[16 * i:16 * i + 16, g, :, :],
                                         kp[64 * r:64 * r + 64, pk, half, :]).then_inc(kq_loaded[g], 16)
                            sp.dma_start(QS[16 * i:16 * i + 16, g, :, :],
                                         qp[64 * r:64 * r + 64, pq, half, :]).then_inc(kq_loaded[g], 16)
                    elif e[0] == "mpost":
                        g = e[1]
                        sp.wait_ge(mT_ready, NG * b + g + 1)
                        sp.sem_inc(gone_ahead, 1)
                        sp.dma_start(QS[KROWS:KROWS + 2, g % NG, :, :], mT[:, :]).then_inc(m_rows, 16)

            sp.wait_ge(kind_ready, 1)
            for g in range(NG):
                for h in range(4):
                    sp.dma_start(KS[KROWS:KROWS + 2, g, h, :], kind).then_inc(kind_rows, 16)
            turn("first", -1)
            turn("head", 0)
            with sp.Fori(1, B - 2) as b:
                turn("body", b)
            turn("body", B - 2, more=False)
            turn("foot", B - 1)

            sp.wait_ge(x_added, B)
            sp.dma_start(wr[:, :, :], a["L0_ffn_Wr"].rearrange("(f p) n -> p f n", p=P)).then_inc(load_r, 16)
            sp.dma_start(tri[:, :, :], a["c_tri"]).then_inc(load_r, 16)

            def load_expert(e, i):
                for w, n in ((wg, "L0_ffn_Wg"), (wu, "L0_ffn_Wu"), (wd, "L0_ffn_Wd")):
                    sp.dma_start(w[:, i, :, :],
                                 a[n][bass.ds(e, 1)].rearrange("o (f p) n -> p (o f) n", p=P)).then_inc(load_w[i], 16)

            load_expert(0, 0)
            load_expert(1, 1)
            with sp.Fori(1, E // 2) as k:
                for i in range(2):
                    sp.wait_ge(c_down, (2 * k + i - 1) * TG * 2)
                    sp.sem_inc(gone_ahead, 1)
                    load_expert(2 * k + i, i)
            for g in range(TG):
                sp.wait_ge(c_down_evac, 2 + 2 * (TG * (E - 1) + g + 1))
                sp.dma_start(out_flat[512 * g:512 * g + 512, :].rearrange("(t p) d -> p t d", p=P),
                             X[:, 4 * g:4 * g + 4, :]).then_inc(stored, 16)
            sp.wait_ge(stored, 16 * TG)

        @block.tensor
        def _(pe):
            def turn_all(src, count0):
                for i in range(NT // 2):
                    pe.wait_ge(xn_ready, count0 + i + 1)
                    if count0 + i >= 2:
                        pe.wait_ge(xt_ready, count0 + i - 1)
                    for f in range(FT):
                        for u in range(2):
                            mm = pe.transpose(bank[i % 2][:, f * 256 + u * P:f * 256 + (u + 1) * P],
                                              src[:, 2 * i + u, f * P:(f + 1) * P], ident[:, :])
                    mm.then_inc(xt_made, 1)

            pe.wait_ge(load_const, 32)
            turn_all(XN, 0)
            pe.wait_ge(xt_ready, NT // 2)
            pe.wait_ge(load_qkv, 48)
            pe.wait_ge(const_ready, 1)
            with pe.Fori(0, B) as b:
                def project(dst, w, head, ft_src):
                    for f in range(FT):
                        mm = pe.matmul(dst, w[:, f, head * HD:(head + 1) * HD], XT[:, f, bass.ds(ft_src, S)],
                                       start=(f == 0), stop=(f == FT - 1))
                    return mm

                def kv_heads(k):
                    w = wk if k < 2 else wv
                    pe.wait_ge(a_kv_evac, 1 + A_KV_EVAC * b + k)
                    for u in range(2):
                        mm = project(bank[3][:, u * S:(u + 1) * S], w, 2 * (k % 2) + u, b * S)
                    mm.then_inc(a_kv, 1)

                def q_heads(k):
                    pe.wait_ge(a_q_evac, 1 + 8 * b + k)
                    for u in range(2):
                        mm = project(bank[2][:, u * S:(u + 1) * S], wq, 2 * k + u, b * S)
                    mm.then_inc(a_q, 1)

                def v_turn(t):
                    pe.wait_ge(a_kv_evac, 1 + A_KV_EVAC * b + 4 + 2 * t)
                    for g in range(HKV):
                        mm = pe.transpose(bank[3][:, g * P:(g + 1) * P], VT[:, g, t * P:(t + 1) * P], ident[:, :])
                    mm.then_inc(a_kv, 1)

                for k in range(4):
                    kv_heads(k)
                    q_heads(k)
                v_turn(0)
                q_heads(4)
                v_turn(1)
                for k in range(5, 8):
                    q_heads(k)

                def scores(i):
                    blk, j = divmod(i, 2)
                    if i < 2:
                        pe.wait_ge(a_kv_evac, 1 + A_KV_EVAC * b + 4)
                        pe.wait_ge(a_q_evac, 1 + 8 * b + 4 * (j + 1))
                    pe.wait_ge(a_exp, NSTEP * b + i + 1)
                    sbank = pair[0][:, i % 2, :]
                    pe.matmul(sbank, identb[:, :], mask[:, (0, 1, 2, 1)[blk], :, :], start=True, stop=False,
                              skip_group_check=True)
                    if blk == 2:
                        spans = [(0, 128, 64), (64, 64, 64)]
                    else:
                        spans = [(0, 128 if blk == 3 else 0, 128)]
                    for gg in range(2):
                        g = 2 * j + gg
                        for p2 in range(2):
                            h = 4 * g + 2 * p2
                            for c, k0, n in spans:
                                o = (2 * gg + p2) * P + c
                                mm = pe.matmul(sbank[:, o:o + n], QT[:, blk, h:h + 2, :].rearrange("p h q -> p (h q)"),
                                               KT[:, g, k0:k0 + n], start=False, stop=True, skip_group_check=True)
                    mm.then_inc(a_score, 1)

                def turn_probs(i):
                    pe.wait_ge(a_norm, NSTEP * b + i + 1)
                    pe.wait_ge(a_pt, NSTEP * b + i + 1)
                    for q in range(4):
                        mm = pe.transpose(pair[1][:, i % 2, q * P:(q + 1) * P], PA[:, i % P_RING, q * P:(q + 1) * P],
                                          ident[:, :])
                    mm.then_inc(a_turned, 1)

                def values(i):
                    blk, j = divmod(i, 2)
                    if i == 0:
                        pe.wait_ge(a_kv_evac, 1 + A_KV_EVAC * b + 8)
                    pe.wait_ge(a_pt, 2 + NSTEP * b + i + 1)
                    pe.wait_ge(a_o_evac, NSTEP * b + i + 1)
                    for gg in range(2):
                        g = 2 * j + gg
                        mm = pe.matmul(bank[i % 2][:, gg * 256:(gg + 1) * 256], V[:, (0, 0, 2, 1)[blk], g * HD:(g + 1) * HD],
                                       PT[:, i % 2, gg * 256:(gg + 1) * 256], start=True, stop=True)
                    mm.then_inc(a_pv, 1)

                for i in range(NSTEP + 3):
                    if i < NSTEP:
                        scores(i)
                    if 2 <= i < NSTEP + 2:
                        turn_probs(i - 2)
                    if i >= 3:
                        values(i - 3)

                pe.wait_ge(load_o, 16)
                pe.wait_ge(a_kv_evac, 1 + A_KV_EVAC * b + 8)
                pe.wait_ge(a_o_evac, 2 + NSTEP * (b + 1))
                for t in range(2):
                    for h in range(HQ):
                        mm = pe.matmul(bank[3][:, t * D:(t + 1) * D], OT[:, h, t * P:(t + 1) * P], wo[:, h, :],
                                       start=(h == 0), stop=(h == HQ - 1))
                mm.then_inc(a_kv, 1)

            ST, SM, OB, MB = pair, (bank[0], bank[1]), bank[2], bank[3]
            OBv = OB[:, :].rearrange("p (k q) -> p k q", k=2)
            pe.wait_ge(load_b, 16 * 19)
            pe.wait_ge(b_init, 3)
            pe.wait_ge(kind_rows, 16 * NH)

            def turn(name, b):
                c = b + 1
                events, place = numbered(name, b)
                for e, n in events:
                    kind_, arg = e[0], e[1:]
                    if kind_ in MISC and not (name == "first" and kind_ == "xT"):
                        pe.wait_ge(misc_free, n)
                    if kind_ == "st":
                        s = arg[0]
                        g, t = divmod(s, KT_TILES)
                        kn = key_count(t)
                        if t == 0:
                            pe.wait_ge(m_rows, 16 * (NG * b + g + 1))
                        pe.wait_ge(exp_done, XSTEP * b + s + 1)
                        for h in range(4):
                            mm = pe.matmul(ST[s % 2][0:kn, h // 2, (h % 2) * S:(h % 2 + 1) * S],
                                           KS[:, g, h, t * P:t * P + kn], QS[:, g, h, :], start=True, stop=True)
                        mm.then_inc(st_made, 1)
                    elif kind_ == "mx":
                        g, u = arg
                        h, r = divmod(u, 8)
                        qt, ch = divmod(r, 4)
                        k0, kn = MAX_CHUNKS[ch]
                        if u == 0:
                            pe.wait_ge(kq_loaded[g % NG], KQ * (b + 1 + g // NG))
                        pe.wait_ge(smax_done, UNITS * (NG * b + g) + u + 1)
                        pe.matmul(SM[u % 2][:, 0:kn], QS[0:KROWS, g % NG, h, qt * P:(qt + 1) * P],
                                  KS[0:KROWS, g % NG, h, k0:k0 + kn], start=True, stop=True).then_inc(smax_made, 1)
                    elif kind_ == "pv":
                        db, s = arg
                        bb = b + db
                        g, t = divmod(s, KT_TILES)
                        kn = key_count(t)
                        pe.wait_ge(exp_done, 2 + XSTEP * bb + s + 1)
                        if g == 0:
                            pe.wait_ge(v_copied, (KT_TILES + 1) * bb + v_slots(t)[-1] + 1)
                        if t == 0:
                            pe.wait_ge(o_evac, 1 + NG * bb + g)
                        for v in v_slots(t):
                            for h in range(4):
                                mm = pe.matmul(OBv[32 * h:32 * h + VW, v // (MIX + 1), :], Vc[0:kn, v, 4 * g + h, :],
                                               PX[0:kn, s % XP_RING, h // 2, (h % 2) * S:(h % 2 + 1) * S],
                                               start=v in (0, MIX + 1), stop=v in (MIX, KT_TILES),
                                               tile_position=(0, 32 * h))
                        mm.then_inc(pv_done, 1)
                    elif kind_ == "otr":
                        bb, g = b + arg[0], arg[1]
                        pe.wait_ge(o_evac, 1 + NG * bb + g + 1)
                        for kd in range(2):
                            for qt in range(2):
                                o = (2 * kd + qt) * P
                                mm = pe.transpose(MB[:, o:o + P], Osb[:, kd, qt * P:(qt + 1) * P], ident[:, :])
                        mm.then_inc(misc_full, 1)
                    elif kind_ == "atr":
                        pe.wait_ge(attn_part, NG * b)
                        for f in range(FT):
                            for qt in range(2):
                                o = f * S + qt * P
                                mm = pe.transpose(MB[:, o:o + P], attn[:, qt, f * P:(f + 1) * P], ident[:, :])
                        mm.then_inc(misc_full, 1)
                    elif kind_ == "oproj":
                        for qt in range(2):
                            for f in range(FT):
                                mm = pe.matmul(MB[:, qt * D:(qt + 1) * D], attnT[:, f, qt * P:(qt + 1) * P], xo_w[:, f, :],
                                               start=(f == 0), stop=(f == FT - 1))
                        mm.then_inc(misc_full, 1)
                    elif kind_ == "mpost":
                        pe.wait_ge(mneg_ready, NG * b + arg[0] + 1)
                        for qt in range(2):
                            mm = pe.transpose(MB[0:8, qt * P:(qt + 1) * P], mneg[:, qt, :], ident[:, :])
                        mm.then_inc(misc_full, 1)
                    elif kind_ == "xT":
                        pe.wait_ge(b_xn, c + 1)
                        for f in range(FT):
                            for u in range(2):
                                o = f * S + u * P
                                mm = pe.transpose(MB[:, o:o + P], xn[:, u, f * P:(f + 1) * P], ident[:, :])
                        mm.then_inc(misc_full, 1)
                    elif kind_ == "q":
                        for u in range(2):
                            for f in range(FT):
                                mm = pe.matmul(MB[:, u * D:(u + 1) * D], xT[:, f, u * P:(u + 1) * P], xq_w[:, f, :],
                                               start=(f == 0), stop=(f == FT - 1))
                        mm.then_inc(misc_full, 1)
                    elif kind_ == "ct":
                        t = arg[0]
                        kn = key_count(t)
                        if t == 0:
                            pe.wait_ge(ctx_loaded, 80 * (c + 1))
                        for f in range(FT):
                            mm = pe.transpose(MB[:, f * P:f * P + kn], ctxk[0:kn, t, f * P:(f + 1) * P],
                                              ident[0:kn, 0:kn])
                        mm.then_inc(misc_full, 1)
                    elif kind_ == "kv":
                        t = arg[0]
                        kn = key_count(t)
                        pe.wait_ge(misc_free, place[("ct", t)] + 1)
                        for i, r0, r1 in kinds_of(t):
                            for f in range(FT):
                                mm = pe.matmul(MB[r0:r1, :], ctxT[:, t % 2, f, r0:r1], xkv_w[i][:, f, :],
                                               start=(f == 0), stop=(f == FT - 1))
                        mm.then_inc(misc_full, 1)
                    elif kind_ == "qt":
                        pe.wait_ge(scaled, (NCH + 1) * c + 1)
                        for f in range(FT):
                            for u in range(2):
                                o = f * S + u * P
                                mm = pe.transpose(MB[:, o:o + P], qraw[:, u, f * P:(f + 1) * P], ident[:, :])
                        mm.then_inc(misc_full, 1)
                    elif kind_ == "kt":
                        j = arg[0]
                        pe.wait_ge(scaled, (NCH + 1) * c + j + 2)
                        t0, t1 = CHUNKS[j]
                        for f in range(FT):
                            for t in range(t0, t1):
                                kn = key_count(t)
                                o = f * 256 + (t - t0) * P
                                mm = pe.transpose(MB[:, o:o + kn], ctxk[0:kn, t, f * P:(f + 1) * P], ident[0:kn, 0:kn])
                        mm.then_inc(misc_full, 1)

            turn("first", -1)
            turn("head", 0)
            with pe.Fori(1, B - 1) as b:
                turn("body", b)
            turn("foot", B - 1)
            turn("last", B)

            turn_all(XN3, NT // 2)
            pe.wait_ge(xt_ready, NT)
            pe.wait_ge(load_r, 32)
            for t in range(NT):
                for f in range(FT):
                    mm = pe.matmul(bank[2][:, t * E:(t + 1) * E], XT3[:, f, t * P:(t + 1) * P], wr[:, f, :],
                                   start=(f == 0), stop=(f == FT - 1))
            mm.then_inc(c_logit, 1)

            def gate_up(i, e, g):
                n = TG * e + g
                for m in range(FT):
                    pe.wait_ge(c_h, 2 * n + m + 1)
                    for j, w in enumerate((wg, wu)):
                        for f in range(FT):
                            mm = pe.matmul(pair[m][:, j, :], w[:, i, f, m * P:(m + 1) * P],
                                           XT3[:, f, 512 * g:512 * (g + 1)], start=(f == 0), stop=(f == FT - 1))
                    mm.then_inc(c_gu, 1)

            def down(i, e, g):
                n = TG * e + g
                pe.wait_ge(c_h, 2 + 2 * n + 2)
                for u in range(2):
                    pe.wait_ge(c_down_evac, 2 * n + u + 1)
                    for t in range(2):
                        for m in range(FT):
                            o = (2 * u + t) * P
                            mm = pe.matmul(bank[u][:, t * D:(t + 1) * D], hT[:, g % 2, m, o:o + P], wd[:, i, m, :],
                                           start=(m == 0), stop=(m == FT - 1))
                    mm.then_inc(c_down, 1)

            with pe.Fori(0, E, 2) as e2:
                for i in range(2):
                    e = e2 + i
                    pe.wait_ge(load_w[i], 24 * e2 + 48)
                    gate_up(i, e, 0)
                    for g in range(TG):
                        if g + 1 < TG:
                            gate_up(i, e, g + 1)
                        down(i, e, g)

        @block.scalar
        def _(act):
            act.sem_inc(a_q_evac, 1)
            act.sem_inc(a_exp, 2)
            act.sem_inc(a_pt, 2)

            def move_all(dst, count0):
                for i in range(NT // 2):
                    act.wait_ge(xt_made, count0 + i + 1)
                    act.activation(dst[:, :, 256 * i:256 * (i + 1)], bank[i % 2][:, :].rearrange("p (f n) -> p f n", f=FT),
                                   ACT.Copy).then_inc(xt_ready, 1)

            move_all(XT, 0)
            with act.Fori(0, B) as b:
                for k in range(8):
                    act.wait_ge(a_q, 8 * b + k + 1)
                    act.activation(QT[:, :, 2 * k:2 * k + 2, :].rearrange("p b h q -> p h b q"),
                                   bank[2][:, :].rearrange("p (h b q) -> p h b q", h=2, b=NBLK),
                                   ACT.Copy).then_inc(a_q_evac, 1)

                for i in range(NSTEP + 2):
                    if i < NSTEP:
                        act.wait_ge(a_negmax, NSTEP * b + i + 1)
                        act.wait_ge(a_turned, NSTEP * b + i + 1)
                        for q in range(4):
                            ins = act.activation(PA[:, i % P_RING, q * P:(q + 1) * P], pair[0][:, i % 2, q * P:(q + 1) * P],
                                                 ACT.Exp, bias=negmax[:, i % P_RING, q:q + 1], scale=1.0 / HD,
                                                 accum_out=rowsum[:, i % P_RING, q:q + 1])
                        ins.then_inc(a_exp, 1)
                    if i >= 2:
                        k = i - 2
                        act.wait_ge(a_turned, P_RING + NSTEP * b + k + 1)
                        act.wait_ge(a_pv, NSTEP * b + k + 1)
                        act.activation(PT[:, k % 2, :], pair[1][:, k % 2, :], ACT.Copy).then_inc(a_pt, 1)

            ST, OB, MB = pair, bank[2], bank[3]
            MB3 = MB[:, :].rearrange("p (f n) -> p f n", f=FT)
            act.sem_inc(exp_done, 2)
            act.sem_inc(o_evac, 1)
            act.wait_ge(a_kv_evac, 1 + A_KV_EVAC * B)
            act.wait_ge(b_init, 3)
            act.wait_ge(load_b, 16 * 19)
            act.activation(kind, kindf, ACT.Copy).then_inc(kind_ready, 1)

            def turn(name, b):
                c = b + 1
                events, place = numbered(name, b)
                for e, n in events:
                    kind_, arg = e[0], e[1:]
                    if kind_ == "st":
                        s = arg[0]
                        kn = key_count(s % KT_TILES)
                        act.wait_ge(st_made, XSTEP * b + s + 1)
                        act.wait_ge(pv_done, XSTEP * b + s + 1)
                        act.activation(PX[0:kn, s % XP_RING, :, :], ST[s % 2][0:kn, :, :], ACT.Exp,
                                       scale=float(XD) ** -0.5).then_inc(exp_done, 1)
                    elif kind_ == "oev":
                        bb, g = b + arg[0], arg[1]
                        act.wait_ge(pv_done, XP_RING + XSTEP * bb + KT_TILES * (g + 1))
                        act.wait_ge(attn_part, NG * bb + g)
                        act.activation(Osb[:, :, :], OB[:, :].rearrange("p (k q) -> p k q", k=2), ACT.Copy)\
                           .then_inc(o_evac, 1)
                    elif kind_ in ("xT", "atr"):
                        act.wait_ge(misc_full, n + 1)
                        act.activation((xT if kind_ == "xT" else attnT)[:, :, :], MB3, ACT.Copy).then_inc(misc_free, 1)
                    elif kind_ == "ct":
                        t = arg[0]
                        kn = key_count(t)
                        act.wait_ge(misc_full, n + 1)
                        act.activation(ctxT[:, t % 2, :, 0:kn], MB[:, 0:2 * P].rearrange("p (f n) -> p f n", f=FT)[:, :, 0:kn],
                                       ACT.Copy).then_inc(misc_free, 1)
                    elif kind_ in ("qt", "kt"):
                        act.wait_ge(misc_full, n + 1)
                        if kind_ == "qt":
                            if name != "first":
                                act.wait_ge(split_done, (NCH + 1) * c)
                            segs = [(0, 0, S)]
                            k0, dst, part = 0, qw, qp
                            for g in range(NG):
                                act.wait_ge(kq_loaded[g], KQ * c)
                        else:
                            j = arg[0]
                            k0 = CHUNKS[j][0] * P
                            k1 = min(CHUNKS[j][1] * P, NKEY)
                            segs = [(1, k0, min(k1, N_TXT))] if k0 < N_TXT else []
                            segs += [(2, max(k0, N_TXT), k1)] if k1 > N_TXT else []
                            act.wait_ge(split_done, (NCH + 1) * c + (j if j >= 2 else 0))
                            dst, part = kw[:, j % 2, :, :], kp
                        todo = [(w, s0, s1, f, o) for w, s0, s1 in segs for f in range(FT) for o in range(2)]
                        for w, s0, s1, f, o in todo:
                            to = dst[:, f, s0 - k0:s1 - k0] if o == 0 else part[:, 0, f, s0:s1]
                            ins = act.activation(to, MB3[:, f, s0 - k0:s1 - k0], ACT.Copy, scale=norm_w[:, w, f:f + 1])
                        ins.then_inc(misc_free, 1)
                    elif kind_ == "k2":
                        j = arg[0]
                        act.wait_ge(r1_done, (NCH + 1) * c + j + 1)
                        if j == 0:
                            act.activation(qp[:, 1, :, :], qw[:, :, :], ACT.Copy).then_inc(k2_done, 1)
                        else:
                            k0 = CHUNKS[j - 1][0] * P
                            k1 = min(CHUNKS[j - 1][1] * P, NKEY)
                            act.activation(kp[:, 1, :, k0:k1], kw[:, (j - 1) % 2, :, 0:k1 - k0], ACT.Copy).then_inc(k2_done, 1)
                    if kind_ == "kv":
                        t = arg[0]
                        kn = key_count(t)
                        act.wait_ge(misc_full, n + 1)
                        if name != "first":
                            act.wait_ge(v_copied, (KT_TILES + 1) * (c - 1) + v_slots(t)[-1] + 1)
                        act.activation(Vn[0:kn, t, :], MB[0:kn, D:2 * D], ACT.Copy).then_inc(v_ready, 1)
                    if kind_ in ("q", "kv"):
                        act.wait_ge(misc_free, n + 1)
                        for t in ((13, 14) if kind_ == "q" else (arg[0],)):
                            kn = P if t >= KT_TILES else key_count(t)
                            src = qraw[:, t - KT_TILES, :] if t >= KT_TILES else ctxk[0:kn, t, :]
                            act.wait_ge(sq_done, (KT_TILES + 2) * c + (t - KT_TILES if t >= KT_TILES else t + 2))
                            act.activation(junk[0:kn, :], src, ACT.Square, accum_out=sumsq[0:kn, t:t + 1])\
                               .then_inc(sq_done, 1)

            turn("first", -1)
            turn("head", 0)
            with act.Fori(1, B - 1) as b:
                turn("body", b)
            turn("foot", B - 1)
            turn("last", B)

            act.wait_ge(x_added, B)
            move_all(XT3, NT // 2)
            act.wait_ge(c_shift, 1)
            act.activation(prob[:, :, :], logit[:, :, :], ACT.Exp).then_inc(c_exp, 1)
            with act.Fori(0, E * TG) as n:
                for m in range(FT):
                    act.wait_ge(c_gu, 2 * n + m + 1)
                    act.wait_ge(c_h, 2 * n + m + 1)
                    act.activation(silu[:, m, :], pair[m][:, 0, :], ACT.Silu).then_inc(c_silu, 1)

        @block.vector
        def _(dve):
            dve.sem_inc(a_kv_evac, 1)
            dve.sem_inc(a_o_evac, 2)
            norm_stats(dve, loads=True)
            norm_rows(dve, XN)
            dve.wait_ge(load_const, 32)
            dve.tensor_copy(identb[:, :], ident[:, :])
            for m in range(4):
                ins = dve.tensor_copy(mask[:, :, m, :], maskf[:, :, :])
            ins.then_inc(const_ready, 1)

            with dve.Fori(0, B) as b:
                D2 = bank[3][:, :].rearrange("p (h n) -> p h n", h=2)
                for k in range(4):
                    dve.wait_ge(a_kv, A_KV * b + k + 1)
                    dve.tensor_copy((KT if k < 2 else VT)[:, 2 * (k % 2):2 * (k % 2) + 2, :], D2).then_inc(a_kv_evac, 1)
                for t in range(2):
                    dve.wait_ge(a_kv, A_KV * b + 5 + t)
                    dve.tensor_copy(V[:, t, :], bank[3][:, :]).then_inc(a_kv_evac, 1)
                    lo, hi = (64, 128) if t == 0 else (0, 64)
                    dve.tensor_copy(V[lo:hi, 2, :], bank[3][lo:hi, :]).then_inc(a_kv_evac, 1)

                link = dve_link(dve)
                for i in range(NSTEP + 3):
                    if i < NSTEP:
                        r = i % P_RING
                        dve.wait_ge(a_score, NSTEP * b + i + 1)
                        link(dve.tensor_reduce(rowmax[:, r, :], pair[0][:, i % 2, :].rearrange("p (q k) -> p q k", q=4),
                                               X_AXIS, ALU.max))
                        dve.tensor_scalar(negmax[:, r, :], rowmax[:, r, :], -1.0 / HD, None, ALU.mult).then_inc(a_negmax, 1)
                    if 1 <= i < NSTEP + 1:
                        r = (i - 1) % P_RING
                        dve.wait_ge(a_exp, 2 + NSTEP * b + i)
                        link(dve.reciprocal(rowinv[:, r, :], rowsum[:, r, :]))
                        pv = PA[:, r, :].rearrange("p (q k) -> p q k", q=4)
                        dve.tensor_tensor(pv, pv, rowinv[:, r, :].unsqueeze(2).to_broadcast([P, 4, P]), ALU.mult)\
                           .then_inc(a_norm, 1)
                    if i >= 3:
                        k = i - 3
                        blk, j = divmod(k, 2)
                        dve.wait_ge(a_pv, 2 + NSTEP * b + k + 1)
                        dve.tensor_copy(OT[:, 8 * j:8 * j + 8, blk * WIN:(blk + 1) * WIN],
                                        bank[k % 2][:, :].rearrange("p (h n) -> p h n", h=8)).then_inc(a_o_evac, 1)
                dve.wait_ge(a_kv, A_KV * (b + 1))
                xv = X[:, bass.ds(2 * b, 2), :]
                dve.tensor_tensor(xv, xv, D2, ALU.add).then_inc(a_kv_evac, 1)
                dve.sem_clear(chain)

            SM, OB, MB = (bank[0], bank[1]), bank[2], bank[3]
            MB2 = MB[:, :].rearrange("p (u n) -> p u n", u=2)
            dve.sem_inc(smax_done, 2)
            dve.wait_ge(a_kv_evac, 1 + A_KV_EVAC * B)
            norm_stats(dve)
            dve.memset(Vc[:, :, :, :], 1.0).then_inc(b_init, 1)
            dve.wait_ge(b_init, 1)
            dve.memset(Vc[HALF:P, MIX, :, :], 0.0)
            dve.memset(Vc[0:HALF, MIX + 1, :, :], 0.0)
            dve.memset(sumsq[:, :], 1.0).then_inc(b_init, 1)
            dve.memset(OB[:, :], 0.0).then_inc(b_init, 1)
            dve.wait_ge(b_init, 3)
            dve.wait_ge(load_b, 16 * 19)

            def turn(name, b):
                c = b + 1
                events, place = numbered(name, b)
                link = dve_link(dve)
                for e, n in events:
                    kind_, arg = e[0], e[1:]
                    if kind_ == "mx":
                        g, u = arg
                        h, r = divmod(u, 8)
                        qt, ch = divmod(r, 4)
                        dve.wait_ge(smax_made, UNITS * (NG * b + g) + u + 1)
                        dve.tensor_reduce(xmax[:, qt, h, ch:ch + 1], SM[u % 2][:, 0:MAX_CHUNKS[ch][1]], X_AXIS, ALU.max)\
                           .then_inc(smax_done, 1)
                    elif kind_ == "mred":
                        g = arg[0]
                        dve.wait_ge(smax_done, 2 + UNITS * (NG * b + g + 1))
                        dve.tensor_reduce(m8[:, :, 0, :], xmax[:, :, :, 0:3], X_AXIS, ALU.max)
                        link(dve.tensor_copy(m8[:, :, 1, :], xmax[:, :, :, 3]))
                        dve.tensor_scalar(mneg[:, :, :], m8[:, :, :, :].rearrange("p a k h -> p a (k h)"), -1.0, None,
                                          ALU.mult).then_inc(mneg_ready, 1)
                    elif kind_ == "mpost":
                        dve.wait_ge(misc_full, n + 1)
                        dve.wait_ge(m_rows, 16 * (NG * b + arg[0]))
                        dve.tensor_copy(mT[:, :], MB[0:8, 0:S]).then_inc(misc_free, 1)
                        dve.wait_ge(misc_free, n + 1)
                        dve.sem_inc(mT_ready, 1)
                    elif kind_ == "otr":
                        bb, g = b + arg[0], arg[1]
                        dve.wait_ge(misc_full, n + 1)
                        ov = MB[:, :].rearrange("p (k q h d) -> p k q h d", k=2, q=2, h=4)
                        link(dve.reciprocal(oinv[:, :, :, :], ov[:, :, :, :, XD]))
                        for kd in range(2):
                            ins = dve.tensor_tensor(otmp[:, kd, :, :].rearrange("p q (h d) -> p q h d", h=4),
                                                    ov[:, kd, :, :, 0:XD],
                                                    oinv[:, kd, :, :].unsqueeze(3).to_broadcast([P, 2, 4, XD]), ALU.mult)
                        ins.then_inc(misc_free, 1)
                        dve.wait_ge(misc_free, n + 1)
                        dve.tensor_tensor(attn[:, :, 64 * g:64 * g + 64], otmp[:, 0, :, :], otmp[:, 1, :, :], ALU.add)\
                           .then_inc(attn_part, 1)
                    elif kind_ == "oproj":
                        dve.wait_ge(misc_full, n + 1)
                        dve.tensor_tensor(oproj[:, :, :], MB2, xo_b[:, :].unsqueeze(1).to_broadcast([P, 2, D]), ALU.add)\
                           .then_inc(misc_free, 1)
                        dve.wait_ge(misc_free, n + 1)
                        xv = X[:, bass.ds(2 * (b - 1), 2), :]
                        dve.tensor_tensor(xv, xv, oproj[:, :, :], ALU.add).then_inc(x_added, 1)
                    elif kind_ == "ln":
                        for u in range(2):
                            ins = dve.tensor_scalar(xn[:, u, :], X[:, bass.ds(2 * c + u, 1), :].rearrange("p o d -> p (o d)"),
                                                    meanvar[:, bass.ds(2 * c + u, 1), 0:1].rearrange("p o d -> p (o d)"),
                                                    rstd[:, bass.ds(2 * c + u, 1)], ALU.subtract, ALU.mult)
                        ins.then_inc(b_xn, 1)
                    elif kind_ == "q":
                        dve.wait_ge(misc_full, n + 1)
                        dve.tensor_tensor(qraw[:, :, :], MB2, xq_b[:, :].unsqueeze(1).to_broadcast([P, 2, D]), ALU.add)\
                           .then_inc(misc_free, 1)
                    elif kind_ == "kv":
                        t = arg[0]
                        dve.wait_ge(misc_full, n + 1)
                        dve.wait_ge(v_ready, KT_TILES * c + t + 1)
                        for i, r0, r1 in kinds_of(t):
                            ins = dve.tensor_tensor(ctxk[r0:r1, t, :], MB[r0:r1, 0:D], xkv_b[i][r0:r1, 0:D], ALU.add)
                        ins.then_inc(misc_free, 1)
                    elif kind_ == "rms":
                        dve.wait_ge(sq_done, (KT_TILES + 2) * (c + 1))
                        link(dve.tensor_scalar(newton_v[:, 0:KT_TILES + 2], sumsq[:, :], 1.0 / D, RMS_EPS, ALU.mult, ALU.add))
                        inverse_root(dve, link, KT_TILES + 2, kq_rstd[:, :])
                    elif kind_ == "sc":
                        j = arg[0]
                        if j == 0:
                            for u in range(2):
                                ins = dve.tensor_scalar(qraw[:, u, :], qraw[:, u, :], kq_rstd[:, KT_TILES + u:KT_TILES + u + 1],
                                                        None, ALU.mult)
                        else:
                            for t in range(*CHUNKS[j - 1]):
                                kn = key_count(t)
                                ins = dve.tensor_scalar(ctxk[0:kn, t, :], ctxk[0:kn, t, :], kq_rstd[0:kn, t:t + 1], None,
                                                        ALU.mult)
                        ins.then_inc(scaled, 1)
                dve.sem_clear(chain)

            turn("first", -1)
            turn("head", 0)
            with dve.Fori(1, B - 1) as b:
                turn("body", b)
            turn("foot", B - 1)
            turn("last", B)

            dve.sem_inc(c_h, 2)
            dve.sem_inc(c_down_evac, 2)
            dve.wait_ge(x_added, B)
            norm_stats(dve)
            norm_rows(dve, XN3)
            link = dve_link(dve)
            dve.wait_ge(c_logit, 1)
            lv = bank[2][:, 0:NT * E].rearrange("p (t e) -> p t e", e=E)
            link(dve.tensor_reduce(top[:, :], lv, X_AXIS, ALU.max))
            dve.tensor_tensor(logit[:, :, :], lv, top[:, :].unsqueeze(2).to_broadcast([P, NT, E]), ALU.subtract)\
               .then_inc(c_shift, 1)
            dve.wait_ge(c_exp, 1)
            dve.wait_ge(load_r, 32)
            pj = prob[:, :, :].unsqueeze(2).to_broadcast([P, NT, E, E])
            pi = prob[:, :, :].unsqueeze(3).to_broadcast([P, NT, E, E])
            dve.tensor_tensor(beats[:, :, :, :], pj, pi, ALU.is_gt)
            link(dve.tensor_tensor(ties[:, :, :, :], pj, pi, ALU.is_equal))
            link(dve.tensor_tensor(ties[:, :, :, :], ties[:, :, :, :],
                                   tri[:, :, :].unsqueeze(1).to_broadcast([P, NT, E, E]), ALU.mult))
            link(dve.tensor_tensor(beats[:, :, :, :], beats[:, :, :, :], ties[:, :, :, :], ALU.add))
            link(dve.tensor_reduce(rank[:, :, :], beats[:, :, :, :], X_AXIS, ALU.add))
            link(dve.scalar_tensor_tensor(out=gate[:, :, :], in0=rank[:, :, :], scalar=1.5, in1=prob[:, :, :],
                                          op0=ALU.is_lt, op1=ALU.mult))
            link(dve.tensor_reduce(topsum[:, :], gate[:, :, :], X_AXIS, ALU.add))
            link(dve.reciprocal(top[:, :], topsum[:, :]))
            link(dve.tensor_tensor(gate[:, :, :], gate[:, :, :], top[:, :].unsqueeze(2).to_broadcast([P, NT, E]), ALU.mult))
            dve.sem_clear(chain)

            def hidden(e, g):
                n = TG * e + g
                for m in range(FT):
                    dve.wait_ge(c_silu, 2 * n + m + 1)
                    if g >= 2:
                        dve.wait_ge(c_down, 2 * (n - 1))
                    dve.tensor_tensor(hT[:, g % 2, m, :], silu[:, m, :], pair[m][:, 1, :], ALU.mult).then_inc(c_h, 1)

            def add(e, g):
                n = TG * e + g
                for u in range(2):
                    dve.wait_ge(c_down, 2 * n + u + 1)
                    for t in range(2):
                        tile = 4 * g + 2 * u + t
                        ins = dve.scalar_tensor_tensor(out=X[:, tile, :], in0=bank[u][:, t * D:(t + 1) * D],
                                                       scalar=gate[:, tile, bass.ds(e, 1)], in1=X[:, tile, :],
                                                       op0=ALU.mult, op1=ALU.add)
                    ins.then_inc(c_down_evac, 1)

            with dve.Fori(0, E) as e:
                hidden(e, 0)
                for g in range(TG):
                    if g + 1 < TG:
                        hidden(e, g + 1)
                    add(e, g)

        @block.gpsimd
        def _(pool):
            pool.sem_inc(a_turned, P_RING)
            pool.sem_inc(a_pv, 2)
            pool.sem_inc(pv_done, XP_RING)

            def turn(name, b):
                c = b + 1
                events, place = numbered(name, b)
                for e, n in events:
                    kind_, arg = e[0], e[1:]
                    if kind_ in ("qt", "kt"):
                        pool.wait_ge(misc_free, n + 1)
                        if kind_ == "qt":
                            pool.tensor_tensor(qw[:, :, :], qw[:, :, :], qp[:, 0, :, :], ALU.subtract).then_inc(r1_done, 1)
                        else:
                            j = arg[0]
                            k0 = CHUNKS[j][0] * P
                            k1 = min(CHUNKS[j][1] * P, NKEY)
                            kv = kw[:, j % 2, :, 0:k1 - k0]
                            pool.tensor_tensor(kv, kv, kp[:, 0, :, k0:k1], ALU.subtract).then_inc(r1_done, 1)
                    elif kind_ == "k2":
                        j = arg[0]
                        pool.wait_ge(k2_done, (NCH + 1) * c + j + 1)
                        if j == 0:
                            pool.tensor_tensor(qp[:, 2, :, :], qw[:, :, :], qp[:, 1, :, :], ALU.subtract).then_inc(split_done, 1)
                        else:
                            k0 = CHUNKS[j - 1][0] * P
                            k1 = min(CHUNKS[j - 1][1] * P, NKEY)
                            pool.tensor_tensor(kp[:, 2, :, k0:k1], kw[:, (j - 1) % 2, :, 0:k1 - k0], kp[:, 1, :, k0:k1],
                                               ALU.subtract).then_inc(split_done, 1)
                    elif kind_ == "vc":
                        cb, t = b + arg[0], arg[1]
                        kn = key_count(t)
                        pool.wait_ge(v_ready, KT_TILES * cb + t + 1)
                        if not (name in ("first", "head") and cb in (0,)):
                            pool.wait_ge(pv_done, XP_RING + XSTEP * (cb - 1) + (NG - 1) * KT_TILES + t + 1)
                        for v, (i, r0, r1) in zip(v_slots(t), kinds_of(t)):
                            pool.tensor_tensor(Vc[r0:r1, v, :, 0:XD],
                                               Vn[r0:r1, t, :].rearrange("p (h d) -> p h d", d=XD),
                                               xkv_b[i][r0:r1, D:2 * D].rearrange("p (h d) -> p h d", d=XD), ALU.add)\
                                .then_inc(v_copied, 1)
                            if t == MIX:
                                pool.wait_ge(v_copied, (KT_TILES + 1) * cb + v + 1)

            pool.wait_ge(b_init, 3)
            turn("first", -1)
            turn("head", 0)
            with pool.Fori(1, B - 1) as b:
                turn("body", b)
            turn("foot", B - 1)


def kernel(**inputs):
    import numpy as _np
    import concourse.bacc as _bacc
    from concourse.bass_utils import run_bass_kernel_spmd as _run

    def constants():
        r = _np.arange(P)[:, None] % WIN
        k = _np.arange(P)[None, :]
        own = (k < WIN) & (k <= r)
        std = (k >= r + 1) & (k <= r + WIN)
        swap = ((k < WIN) & (k <= r)) | ((k >= WIN) & (k - WIN >= r + 1))
        mask = _np.stack([_np.where(m, 0.0, -1e30) for m in (own, std, swap)], 1).astype(_np.float32)
        tri = _np.broadcast_to(_np.tril(_np.ones((E, E), _np.float32), -1), (P, E, E))
        kinds = _np.zeros((2, NKEY), _np.float32)
        kinds[0, :N_TXT] = 1.0
        kinds[1, N_TXT:] = 1.0
        return {"c_ident": _np.eye(P, dtype=_np.float32), "c_mask": mask, "c_tri": _np.ascontiguousarray(tri), "c_kind": kinds}

    data = {n: _np.asarray(v) for n, v in inputs.items()}
    for n in ("q_w", "q_b", "k_w", "k_b", "k_img_w", "k_img_b", "norm_q_w", "norm_k_w", "norm_k_img_w"):
        v = data[f"L0_xattn_{n}"]
        data[f"L0_xattn_{n}"] = v.reshape(NG, 4, XD, -1).transpose(0, 2, 1, 3).reshape(v.shape)
    for n in ("q", "k", "v", "k_img", "v_img", "o"):
        data[f"wT_{n}"] = _np.ascontiguousarray(data.pop(f"L0_xattn_{n}_w").T)
    data.update(constants())
    nc = _bacc.Bacc("TRN2", target_bir_lowering=False, num_devices=1)
    arrays, aps = {}, {}
    for name, v in data.items():
        v = _np.ascontiguousarray(v)
        arrays[f"in_{name}"] = v
        aps[name] = nc.dram_tensor(f"in_{name}", v.shape, mybir.dt.from_np(v.dtype), kind="ExternalInput").ap()
    out = nc.dram_tensor("out_x", (B, S, D), F32, kind="ExternalOutput").ap()
    decoder_layer(nc, aps, out)
    r = _run(nc, [arrays], core_ids=[0])
    return r.results[0]["out_x"]
```

```python
import concourse.bass as bass
from concourse import mybir
from contextlib import ExitStack

F32 = mybir.dt.float32
BF16 = mybir.dt.bfloat16
I32 = mybir.dt.int32
ALU = mybir.AluOpType
ACT = mybir.ActivationFunctionType
X_AXIS = mybir.AxisListType.X

P = 128
B, S, D = 8, 256, 256
NT = B * S // P
FT = D // P
LN_EPS, RMS_EPS = 1e-5, 1e-6

HQ, HKV, HD, WIN = 16, 4, 128, 64
NBLK = S // WIN
NSTEP = NBLK * 2
P_RING = 4

NH, XD = 16, 16
N_TXT, N_IMG = 1344, 257
NKEY = N_TXT + N_IMG
KT_TILES = -(-NKEY // P)
LAST = NKEY - (KT_TILES - 1) * P
MIX = N_TXT // P
HALF = N_TXT - MIX * P
NG = 4
XSTEP = NG * KT_TILES
PARTS = [(0, 0), (0, 1), (1, 0), (1, 1), (0, 2), (2, 0), (1, 2)]
KROWS = 16 * len(PARTS)
MAXN = N_TXT // 3
MAX_CHUNKS = [(0, MAXN), (MAXN, MAXN), (2 * MAXN, MAXN), (N_TXT, N_IMG)]
UNITS = 4 * 2 * len(MAX_CHUNKS)
XP_RING = 4
CHUNKS = [(0, 2), (2, 4), (4, 6), (6, 8), (8, 10), (10, 11), (11, 13)]
NCH = len(CHUNKS)
MAX_WINDOWS = [(0, 11), (11, 23), (23, 35), (37, 49)]
K_STEPS = (20, 22, 24, 25, 27, 29, 30)
RMS_OPS = 12
VW = XD + 1

E, F = 8, 256
TG = 4


def kinds_of(t):
    return [(0, 0, P)] if t < MIX else [(0, 0, HALF), (1, HALF, P)] if t == MIX else [(1, 0, key_count(t))]


def chunk_of(t):
    return next((j, t - t0) for j, (t0, t1) in enumerate(CHUNKS) if t0 <= t < t1)


def v_slots(t):
    return (t,) if t < MIX else (MIX, MIX + 1) if t == MIX else (t + 1,)


def key_count(t):
    return LAST if t == KT_TILES - 1 else P


CONTEXT_EVENTS = [e for j, (t0, t1) in enumerate(CHUNKS) for e in [("ct", j)] + [("kv", t) for t in range(t0, t1)]]
EARLY = 9


def early_events():
    return [("xT", 2), ("q", 2)] + [(k, 2, i) for k, i in CONTEXT_EVENTS[:EARLY]]


def squares(e):
    return [("sq", e[1], t) for t in ((KT_TILES, KT_TILES + 1) if e[0] == "q" else (e[2],))]


def with_squares(events):
    return [x for e in events for x in [e] + (squares(e) if e[0] in ("q", "kv") else [])]


def attention_events(tail, prep, early):
    mid = {s: [] for s in range(XSTEP)}
    end = {s: [] for s in range(XSTEP)}
    late = {s: [] for s in range(XSTEP)}
    used = set()

    def use(s, e):
        mid[s] += [e]
        used.add(s)

    def context_event(s, e):
        end[s] += [e]
        if e[0] in ("q", "kv"):
            (mid[s + 1] if s + 1 < XSTEP else end[s]).extend(squares(e))

    def free_step(s):
        while s in used:
            s += 1
        used.add(s)
        return s

    if tail:
        use(2, ("otr", -1, 3))
        use(4, ("atr", -1))
        use(6, ("oproj", -1))
    for hg in range(NG - 1):
        use(KT_TILES * (hg + 1) + 2, ("otr", 0, hg))
    for hg, (s0, s1) in enumerate(MAX_WINDOWS[:NG - 1 + prep]):
        for u in range(UNITS):
            s, part = divmod(u * (s1 - s0) * 3 // UNITS, 3)
            (mid, end, late)[part][s0 + s] += [("mx", hg + 1, u)]
        late[s1 - 1] += [("mred", hg + 1)]
        end[s1] += [("mpost", hg + 1)]
        used.add(s1)
    if prep:
        at = 0
        for k, i in CONTEXT_EVENTS[EARLY:]:
            at = free_step(at)
            context_event(at, (k, 1, i))
        for k in range(RMS_OPS):
            (mid, end, late)[k % 6 // 2][at + 1 + k // 6] += [("rms", k)]
        at += 1 + RMS_OPS // 6
        late[at - 1] += [("sc", 0), ("sc", 1)]
        use(at + 1, ("qt",))
        mid[at + 2] += [("k2", 0)]
        end[at + 3] += [("qp", 0)]
        assert at + 1 < K_STEPS[0]
        for j, at in enumerate(K_STEPS):
            end[at - 3] += [("sc", j + 1)] if j else []
            assert at not in used
            use(at, ("kt", j))
            mid[at + 1] += [("k2", j + 1)]
        end[at + 1] += [("kq", 0)]
        end[at + 3] += [("ctx",)]
        end[MAX_WINDOWS[2][1]] += [("kq", 1)]
        end[3 * KT_TILES + 1] += [("kq", 2)]
    if early:
        at = MAX_WINDOWS[2][1] + 1
        end[at - 2] += [("ln", 2)]
        for e in early_events():
            at = free_step(max(at, 3 * KT_TILES + 3) if e[0] == "ct" else at)
            context_event(at, e)
    ev = []
    for s in range(XSTEP):
        hg, t = divmod(s, KT_TILES)
        ev.append(("st", s))
        ev += mid[s]
        if s:
            ev.append(("pv", 0, s - 1))
        elif tail:
            ev.append(("pv", -1, XSTEP - 1))
        if t == 0 and (hg or tail):
            ev.append(("oev", 0, hg - 1) if hg else ("oev", -1, NG - 1))
        if s == 0:
            ev += [("vc", 0, KT_TILES - 2), ("vc", 0, KT_TILES - 1)]
        if prep and s - 3 * KT_TILES - 2 >= 0:
            ev.append(("vc", 1, s - 3 * KT_TILES - 2))
        ev += end[s] + late[s]
    if prep:
        ev.append(("kq", 3))
    return ev


def first_events():
    ev = [("ctx0",), ("ln", 1)] + with_squares([("xT", 1), ("q", 1)] + [(k, 1, i) for k, i in CONTEXT_EVENTS])
    ev += [("vc", 1, t) for t in range(KT_TILES - 2)]
    ev += [("rms", k) for k in range(RMS_OPS)] + [("sc", j) for j in range(NCH + 1)] + [("qt",)]
    for j in range(NCH):
        ev += [("kt", j), ("k2", j)]
    ev += [("k2", NCH), ("qp", 0), ("kq", 0), ("ctx",)] + [("kq", g) for g in range(1, NG)] + [("ln", 2)]
    early = with_squares(early_events())
    for u in range(UNITS):
        ev.append(("mx", NG, u))
        if u % 2 and early:
            ev.append(early.pop(0))
    return ev + early + [("mred", NG), ("mpost", NG)]


def last_events():
    return [("pv", -1, XSTEP - 1), ("oev", -1, NG - 1), ("otr", -1, NG - 1), ("atr", -1), ("oproj", -1)]


MISC = ("xT", "q", "ct", "kv", "qt", "kt", "mpost", "otr", "atr", "oproj")

TURNS = {
    "first": first_events(),
    "head": attention_events(tail=False, prep=True, early=True),
    "body": attention_events(tail=True, prep=True, early=True),
    "near": attention_events(tail=True, prep=True, early=False),
    "foot": attention_events(tail=True, prep=False, early=False),
    "last": last_events(),
}
MISC_COUNT = {k: sum(e[0] in MISC for e in v) for k, v in TURNS.items()}


def numbered(turn, b):
    base = 0
    for name, count in (("first", 1), ("head", 1), ("body", B - 3), ("near", 1), ("foot", 1), ("last", 1)):
        if name == turn:
            break
        base += MISC_COUNT[name] * count
    if turn == "body":
        base += (b - 1) * MISC_COUNT["body"]
    n = 0
    out, place = [], {}
    for e in TURNS[turn]:
        out.append((e, base + n))
        if e[0] in MISC:
            place[e] = base + n
            n += 1
    return out, place


def decoder_layer(nc, a, out):
    ctx = ExitStack()
    with ctx:
        def sb(name, shape, dt=F32, stack=ctx):
            return stack.enter_context(nc.sbuf_tensor(name, shape, dt))

        def sem(name):
            return ctx.enter_context(nc.semaphore(name))

        X = sb("X", [P, NT, D])
        ident = sb("ident", [P, P])
        identb = sb("identb", [P, P], BF16)
        stats = sb("stats", [P, NT, 6])
        meanvar = sb("meanvar", [P, NT, 2])
        rstd = sb("rstd", [P, NT])
        newton_v = sb("newton_v", [P, NT])
        newton_t = sb("newton_t", [P, NT])
        newton_i = sb("newton_i", [P, NT], I32)
        newton_y = sb("newton_y", [P, NT], I32)

        pair = [ctx.enter_context(nc.psum_tensor(f"pair{i}", [P, 2, 512], F32)) for i in range(2)]
        bank = [ctx.enter_context(nc.psum_tensor(f"bank{i}", [P, 512], F32)) for i in range(4)]

        with ExitStack() as sa:
            XT = sb("XT", [P, FT, B * S], stack=sa)
            XN = sb("XN", [P, NT, D], stack=sa)
            wq = sb("wq", [P, FT, HQ * HD], stack=sa)
            wk = sb("wk", [P, FT, HKV * HD], stack=sa)
            wv = sb("wv", [P, FT, HKV * HD], stack=sa)
            wo = sb("wo", [P, HQ, D], stack=sa)
            QT = sb("QT", [P, NBLK, HQ, WIN], stack=sa)
            KT = sb("KT", [P, HKV, S], stack=sa)
            VT = sb("VT", [P, HKV, S], stack=sa)
            V = sb("V", [P, 3, HKV * HD], stack=sa)
            PA = sb("PA", [P, P_RING, 512], stack=sa)
            PT = sb("PT", [P, 2, 512], stack=sa)
            OT = sb("OT", [P, HQ, S], stack=sa)
            maskf = sb("maskf", [P, 3, P], stack=sa)
            mask = sb("mask", [P, 3, 4, P], BF16, stack=sa)
            rowmax = sb("rowmax", [P, P_RING, 4], stack=sa)
            negmax = sb("negmax", [P, P_RING, 4], stack=sa)
            rowsum = sb("rowsum", [P, P_RING, 4], stack=sa)
            rowinv = sb("rowinv", [P, P_RING, 4], stack=sa)

        with ExitStack() as sbk:
            xq_w = sb("xq_w", [P, FT, D], stack=sbk)
            xkv_w = [sb(f"xkv_w{i}", [P, FT, 2 * D], stack=sbk) for i in range(2)]
            xo_w = sb("xo_w", [P, FT, D], stack=sbk)
            xq_b = sb("xq_b", [P, D], stack=sbk)
            xkv_b = [sb(f"xkv_b{i}", [P, 2 * D], stack=sbk) for i in range(2)]
            xo_b = sb("xo_b", [P, D], stack=sbk)
            norm_w = sb("norm_w", [P, 3, FT], stack=sbk)
            kv = sb("kv", [P, KT_TILES, 2 * D], stack=sbk)
            ctxk = kv[:, :, 0:D]
            Vn = kv[:, :, D:2 * D]
            xn = sb("xn", [P, FT, D], stack=sbk)
            xT = sb("xT", [P, FT, S], stack=sbk)
            qraw = xn
            ctxT = sb("ctxT", [P, 2, FT, 2 * P], stack=sbk)
            Vc = sb("Vc", [P, KT_TILES + 1, NH, VW], stack=sbk)
            kw = sb("kw", [P, 2, FT, 2 * P], stack=sbk)
            kp = sb("kp", [P, 3, FT, NKEY], BF16, stack=sbk)
            qw = sb("qw", [P, FT, S], stack=sbk)
            qp = sb("qp", [P, 3, FT, S], BF16, stack=sbk)
            KS = sb("KS", [P, NG, 4, NKEY], BF16, stack=sbk)
            QS = sb("QS", [P, NG, 4, S], BF16, stack=sbk)
            PX = sb("PX", [P, XP_RING, 2, 512], stack=sbk)
            kindf = PX[0:2, :, :, :].rearrange("p a b n -> p (a b n)")[:, 0:NKEY]
            kind = kp[0:2, 0, 0, :]
            Osb = sb("Osb", [P, 2, S], stack=sbk)
            attn = sb("attn", [P, 2, D], stack=sbk)
            attnT = sb("attnT", [P, FT, S], stack=sbk)
            junk = sb("junk", [P, D], stack=sbk)
            oproj = sb("oproj", [P, 2, D], stack=sbk)
            sumsq = sb("sumsq", [P, KT_TILES + 2], stack=sbk)
            kq_rstd = sb("kq_rstd", [P, KT_TILES + 2], stack=sbk)
            xmax = sb("xmax", [P, 2, 4, 4], stack=sbk)
            m8 = sb("m8", [P, 2, 2, 4], stack=sbk)
            mneg = sb("mneg", [P, 2, 8], stack=sbk)
            mT = sb("mT", [8, S], BF16, stack=sbk)
            oinv = sb("oinv", [P, 2, 2, 4], stack=sbk)
            otmp = sb("otmp", [P, 2, 2, 64], stack=sbk)

        with ExitStack() as sc:
            XT3 = sb("XT3", [P, FT, B * S], stack=sc)
            XN3 = sb("XN3", [P, NT, D], stack=sc)
            wr = sb("wr", [P, FT, E], stack=sc)
            tri = sb("tri", [P, E, E], stack=sc)
            wg = sb("wg", [P, 2, FT, F], stack=sc)
            wu = sb("wu", [P, 2, FT, F], stack=sc)
            wd = sb("wd", [P, 2, FT, D], stack=sc)
            logit = sb("logit", [P, NT, E], stack=sc)
            prob = sb("prob", [P, NT, E], stack=sc)
            beats = sb("beats", [P, NT, E, E], stack=sc)
            ties = sb("ties", [P, NT, E, E], stack=sc)
            rank = sb("rank", [P, NT, E], stack=sc)
            gate = sb("gate", [P, NT, E], stack=sc)
            top = sb("top", [P, NT], stack=sc)
            topsum = sb("topsum", [P, NT], stack=sc)
            silu = sb("silu", [P, 2, 512], stack=sc)
            hT = sb("hT", [P, 2, FT, 512], stack=sc)

        chain = sem("chain")
        load_x = [sem(f"load_x{i}") for i in range(4)]
        load_const = sem("load_const")
        load_qkv = sem("load_qkv")
        load_o = sem("load_o")
        const_ready = sem("const_ready")
        xn_ready = sem("xn_ready")
        xt_made = sem("xt_made")
        xt_ready = sem("xt_ready")
        a_kv = sem("a_kv")
        a_kv_evac = sem("a_kv_evac")
        a_q = sem("a_q")
        a_q_evac = sem("a_q_evac")
        a_score = sem("a_score")
        a_negmax = sem("a_negmax")
        a_exp = sem("a_exp")
        a_norm = sem("a_norm")
        a_turned = sem("a_turned")
        a_pt = sem("a_pt")
        a_pv = sem("a_pv")
        a_o_evac = sem("a_o_evac")

        load_b = sem("load_b")
        zero_rows = sem("zero_rows")
        kind_ready = sem("kind_ready")
        kind_rows = sem("kind_rows")
        b_init = sem("b_init")
        ctx_loaded = sem("ctx_loaded")
        gone_ahead = sem("gone_ahead")
        misc_full = sem("misc_full")
        misc_free = sem("misc_free")
        b_xn = sem("b_xn")
        v_copied = sem("v_copied")
        sq_done = sem("sq_done")
        rms_step = sem("rms_step")
        scaled = sem("scaled")
        r1_done = sem("r1_done")
        k2_done = sem("k2_done")
        split_done = sem("split_done")
        kq_loaded = [sem(f"kq_loaded{g}") for g in range(NG)]
        smax_made = sem("smax_made")
        smax_done = sem("smax_done")
        mneg_ready = sem("mneg_ready")
        mT_ready = sem("mT_ready")
        m_rows = sem("m_rows")
        st_made = sem("st_made")
        exp_done = sem("exp_done")
        pv_done = sem("pv_done")
        o_evac = sem("o_evac")
        attn_part = sem("attn_part")
        x_added = sem("x_added")

        load_r = sem("load_r")
        load_w = [sem(f"load_w{i}") for i in range(2)]
        c_logit = sem("c_logit")
        c_shift = sem("c_shift")
        c_exp = sem("c_exp")
        c_gate = sem("c_gate")
        c_gu = sem("c_gu")
        c_silu = sem("c_silu")
        c_h = sem("c_h")
        c_down = sem("c_down")
        c_down_evac = sem("c_down_evac")
        stored = sem("stored")

        A_KV_EVAC = 9
        A_KV = 7
        CTX_DMAS = 4
        KQ = 16 * 2 * len(PARTS)

        x_flat = a["x"].rearrange("b s d -> (b s) d")
        out_flat = out.rearrange("b s d -> (b s) d")
        block = ctx.enter_context(nc.Block())

        def dve_link(eng):
            count = [0]

            def link(ins):
                count[0] += 1
                ins.then_inc(chain, 1)
                eng.wait_ge(chain, count[0])
            return link

        def inverse_root(eng, k, src, scale, eps, n, result):
            v, t, y = newton_v[:, 0:n], newton_t[:, 0:n], newton_y[:, 0:n].bitcast(F32)
            if k == 0:
                return eng.tensor_scalar(v, src, scale, eps, ALU.mult, ALU.add)
            if k == 1:
                return eng.tensor_single_scalar(newton_i[:, 0:n], v.bitcast(I32), 1, ALU.logical_shift_right)
            if k == 2:
                return eng.tensor_scalar(newton_y[:, 0:n], newton_i[:, 0:n], -1.0, float(0x5F3759DF), ALU.mult, ALU.add)
            if k % 3 == 0:
                return eng.scalar_tensor_tensor(out=t, in0=y, scalar=-0.5, in1=y, op0=ALU.mult, op1=ALU.mult)
            if k % 3 == 1:
                return eng.tensor_tensor(t, t, v, ALU.mult)
            return eng.scalar_tensor_tensor(out=result if k == RMS_OPS - 1 else y, in0=t, scalar=1.5, in1=y,
                                            op0=ALU.add, op1=ALU.mult)

        def norm_stats(eng, loads=False):
            link = dve_link(eng)
            for t in range(NT):
                if loads and t % 4 == 0:
                    eng.wait_ge(load_x[t // 4], 16)
                ins = eng.bn_stats(stats[:, t, :], X[:, t, :])
            link(ins)
            for t in range(NT):
                ins = eng.bn_aggr(meanvar[:, t, :], stats[:, t, :])
            link(ins)
            for k in range(RMS_OPS):
                link(inverse_root(eng, k, meanvar[:, :, 1], 1.0, LN_EPS, NT, rstd[:, :]))
            eng.sem_clear(chain)

        def norm_rows(eng, dst):
            for t in range(NT):
                ins = eng.tensor_scalar(dst[:, t, :], X[:, t, :], meanvar[:, t, 0:1], rstd[:, t:t + 1],
                                        ALU.subtract, ALU.mult)
                if t % 2:
                    ins.then_inc(xn_ready, 1)

        @block.sync
        def _(sp):
            for i in range(4):
                sp.dma_start(X[:, 4 * i:4 * i + 4, :],
                             x_flat[512 * i:512 * i + 512, :].rearrange("(t p) d -> p t d", p=P)).then_inc(load_x[i], 16)
            sp.dma_start(ident[:, :], a["c_ident"]).then_inc(load_const, 16)
            sp.dma_start(maskf[:, :, :], a["c_mask"]).then_inc(load_const, 16)
            for w, n in ((wk, "L0_attn_Wk"), (wq, "L0_attn_Wq"), (wv, "L0_attn_Wv")):
                sp.dma_start(w[:, :, :], a[n].rearrange("(f p) n -> p f n", p=P)).then_inc(load_qkv, 16)
            sp.dma_start(wo[:, :, :], a["L0_attn_Wo"].rearrange("(h p) n -> p h n", p=P)).then_inc(load_o, 16)

            sp.wait_ge(a_kv_evac, 1 + A_KV_EVAC * B)
            def wt(name):
                return a[name].rearrange("(f p) n -> p f n", p=P)
            sp.dma_start(xq_w[:, :, :], wt("wT_q")).then_inc(load_b, 16)
            for i, s in enumerate(("", "_img")):
                sp.dma_start(xkv_w[i][:, :, 0:D], wt(f"wT_k{s}")).then_inc(load_b, 16)
                sp.dma_start(xkv_w[i][:, :, D:2 * D], wt(f"wT_v{s}")).then_inc(load_b, 16)
                sp.dma_start(xkv_b[i][:, 0:D], a[f"L0_xattn_k{s}_b"].partition_broadcast(P)).then_inc(load_b, 16)
                sp.dma_start(xkv_b[i][:, D:2 * D], a[f"L0_xattn_v{s}_b"].partition_broadcast(P)).then_inc(load_b, 16)
            sp.dma_start(xo_w[:, :, :], wt("wT_o")).then_inc(load_b, 16)
            sp.dma_start(xq_b[:, :], a["L0_xattn_q_b"].partition_broadcast(P)).then_inc(load_b, 16)
            sp.dma_start(xo_b[:, :], a["L0_xattn_o_b"].partition_broadcast(P)).then_inc(load_b, 16)
            for i, n in enumerate(("q", "k", "k_img")):
                for f in range(FT):
                    sp.dma_start(norm_w[:, i, f:f + 1],
                                 a[f"L0_xattn_norm_{n}_w"][f * P:(f + 1) * P].unsqueeze(1)).then_inc(load_b, 16)
            sp.dma_start(kindf, a["c_kind"]).then_inc(load_b, 16)

            c_ = a["ctx_2048"]

            def load_ctx(c):
                cc = c_[bass.ds(c, 1)].rearrange("o k d -> (o k) d")
                sp.dma_start(ctxk[:, 0:MIX, :],
                             cc[N_IMG:N_IMG + MIX * P, :].rearrange("(t p) d -> p t d", p=P)).then_inc(ctx_loaded, 16)
                sp.dma_start(ctxk[0:HALF, MIX, :], cc[N_IMG + MIX * P:NKEY, :]).then_inc(ctx_loaded, 16)
                sp.dma_start(ctxk[HALF:P, MIX, :], cc[0:P - HALF, :]).then_inc(ctx_loaded, 16)
                sp.dma_start(ctxk[:, MIX + 1, :], cc[P - HALF:2 * P - HALF, :]).then_inc(ctx_loaded, 16)
                sp.dma_start(ctxk[0:LAST, MIX + 2, :], cc[2 * P - HALF:N_IMG, :]).then_inc(ctx_loaded, 16)

            def turn(name, b):
                c = b + 1
                events, place = numbered(name, b)
                for e, n in events:
                    if e[0] == "ctx0":
                        load_ctx(0)
                    elif e[0] == "ctx":
                        sp.wait_ge(misc_full, place[("kt", NCH - 1)] + 1)
                        sp.sem_inc(gone_ahead, 1)
                        if name != "near":
                            load_ctx(c + 1)
                    elif e[0] in ("qp", "kq"):
                        g = e[1]
                        sp.wait_ge(split_done, (NCH + 1) * c + 1 if e[0] == "qp" else (NCH + 1) * (c + 1))
                        sp.sem_inc(gone_ahead, 1)
                        if name != "first":
                            sp.wait_ge(st_made, XSTEP * b + KT_TILES * (g + 1))
                            sp.sem_inc(gone_ahead, 1)
                        else:
                            sp.wait_ge(kind_ready, 1)
                        half, r = divmod(g, 2)
                        for i, (pk, pq) in enumerate(PARTS):
                            if e[0] == "kq":
                                sp.dma_start(KS[16 * i:16 * i + 16, g, :, :],
                                             kp[64 * r:64 * r + 64, pk, half, :]).then_inc(kq_loaded[g], 16)
                            if g or e[0] == "qp":
                                sp.dma_start(QS[16 * i:16 * i + 16, g, :, :],
                                             qp[64 * r:64 * r + 64, pq, half, :]).then_inc(kq_loaded[g], 16)
                    elif e[0] == "mpost":
                        g = e[1]
                        sp.wait_ge(mT_ready, NG * b + g + 1)
                        sp.sem_inc(gone_ahead, 1)
                        sp.dma_start(QS[KROWS:KROWS + 2, g % NG, :, :], mT[:, :]).then_inc(m_rows, 16)

            sp.wait_ge(kind_ready, 1)
            sp.wait_ge(zero_rows, 1)
            for g in range(NG):
                for h in range(4):
                    sp.dma_start(KS[KROWS:KROWS + 2, g, h, :], kind).then_inc(kind_rows, 16)
            turn("first", -1)
            turn("head", 0)
            with sp.Fori(1, B - 2) as b:
                turn("body", b)
            turn("near", B - 2)
            turn("foot", B - 1)

            sp.wait_ge(x_added, B)
            sp.dma_start(wr[:, :, :], a["L0_ffn_Wr"].rearrange("(f p) n -> p f n", p=P)).then_inc(load_r, 16)
            sp.dma_start(tri[:, :, :], a["c_tri"]).then_inc(load_r, 16)

            def load_expert(e, i):
                for w, n in ((wg, "L0_ffn_Wg"), (wu, "L0_ffn_Wu"), (wd, "L0_ffn_Wd")):
                    sp.dma_start(w[:, i, :, :],
                                 a[n][bass.ds(e, 1)].rearrange("o (f p) n -> p (o f) n", p=P)).then_inc(load_w[i], 16)

            load_expert(0, 0)
            load_expert(1, 1)
            with sp.Fori(1, E // 2) as k:
                for i in range(2):
                    sp.wait_ge(c_down, (2 * k + i - 1) * TG * 2)
                    sp.sem_inc(gone_ahead, 1)
                    load_expert(2 * k + i, i)
            for g in range(TG):
                sp.wait_ge(c_down_evac, 2 + 2 * (TG * (E - 1) + g + 1))
                sp.dma_start(out_flat[512 * g:512 * g + 512, :].rearrange("(t p) d -> p t d", p=P),
                             X[:, 4 * g:4 * g + 4, :]).then_inc(stored, 16)
            sp.wait_ge(stored, 16 * TG)

        @block.tensor
        def _(pe):
            def turn_all(src, count0):
                for i in range(NT // 2):
                    pe.wait_ge(xn_ready, count0 + i + 1)
                    if count0 + i >= 2:
                        pe.wait_ge(xt_ready, count0 + i - 1)
                    for f in range(FT):
                        for u in range(2):
                            mm = pe.transpose(bank[i % 2][:, f * 256 + u * P:f * 256 + (u + 1) * P],
                                              src[:, 2 * i + u, f * P:(f + 1) * P], ident[:, :])
                    mm.then_inc(xt_made, 1)

            pe.wait_ge(load_const, 32)
            turn_all(XN, 0)
            pe.wait_ge(xt_ready, NT // 2)
            pe.wait_ge(load_qkv, 48)
            pe.wait_ge(const_ready, 1)
            with pe.Fori(0, B) as b:
                def project(dst, w, head, ft_src):
                    for f in range(FT):
                        mm = pe.matmul(dst, w[:, f, head * HD:(head + 1) * HD], XT[:, f, bass.ds(ft_src, S)],
                                       start=(f == 0), stop=(f == FT - 1))
                    return mm

                def kv_heads(k):
                    w = wk if k < 2 else wv
                    pe.wait_ge(a_kv_evac, 1 + A_KV_EVAC * b + k)
                    for u in range(2):
                        mm = project(bank[3][:, u * S:(u + 1) * S], w, 2 * (k % 2) + u, b * S)
                    mm.then_inc(a_kv, 1)

                def q_heads(k):
                    pe.wait_ge(a_q_evac, 1 + 8 * b + k)
                    for u in range(2):
                        mm = project(bank[2][:, u * S:(u + 1) * S], wq, 2 * k + u, b * S)
                    mm.then_inc(a_q, 1)

                def v_turn(t):
                    pe.wait_ge(a_kv_evac, 1 + A_KV_EVAC * b + 4 + 2 * t)
                    for g in range(HKV):
                        mm = pe.transpose(bank[3][:, g * P:(g + 1) * P], VT[:, g, t * P:(t + 1) * P], ident[:, :])
                    mm.then_inc(a_kv, 1)

                for k in range(4):
                    kv_heads(k)
                    q_heads(k)
                v_turn(0)
                q_heads(4)
                v_turn(1)
                for k in range(5, 8):
                    q_heads(k)

                def scores(i):
                    blk, j = divmod(i, 2)
                    if i < 2:
                        pe.wait_ge(a_kv_evac, 1 + A_KV_EVAC * b + 4)
                        pe.wait_ge(a_q_evac, 1 + 8 * b + 4 * (j + 1))
                    pe.wait_ge(a_exp, NSTEP * b + i + 1)
                    sbank = pair[0][:, i % 2, :]
                    pe.matmul(sbank, identb[:, :], mask[:, (0, 1, 2, 1)[blk], :, :], start=True, stop=False,
                              skip_group_check=True)
                    if blk == 2:
                        spans = [(0, 128, 64), (64, 64, 64)]
                    else:
                        spans = [(0, 128 if blk == 3 else 0, 128)]
                    for gg in range(2):
                        g = 2 * j + gg
                        for p2 in range(2):
                            h = 4 * g + 2 * p2
                            for c, k0, n in spans:
                                o = (2 * gg + p2) * P + c
                                mm = pe.matmul(sbank[:, o:o + n], QT[:, blk, h:h + 2, :].rearrange("p h q -> p (h q)"),
                                               KT[:, g, k0:k0 + n], start=False, stop=True, skip_group_check=True)
                    mm.then_inc(a_score, 1)

                def turn_probs(i):
                    pe.wait_ge(a_norm, NSTEP * b + i + 1)
                    pe.wait_ge(a_pt, NSTEP * b + i + 1)
                    for q in range(4):
                        mm = pe.transpose(pair[1][:, i % 2, q * P:(q + 1) * P], PA[:, i % P_RING, q * P:(q + 1) * P],
                                          ident[:, :])
                    mm.then_inc(a_turned, 1)

                def values(i):
                    blk, j = divmod(i, 2)
                    if i == 0:
                        pe.wait_ge(a_kv_evac, 1 + A_KV_EVAC * b + 8)
                    pe.wait_ge(a_pt, 2 + NSTEP * b + i + 1)
                    pe.wait_ge(a_o_evac, NSTEP * b + i + 1)
                    for gg in range(2):
                        g = 2 * j + gg
                        mm = pe.matmul(bank[i % 2][:, gg * 256:(gg + 1) * 256], V[:, (0, 0, 2, 1)[blk], g * HD:(g + 1) * HD],
                                       PT[:, i % 2, gg * 256:(gg + 1) * 256], start=True, stop=True)
                    mm.then_inc(a_pv, 1)

                for i in range(NSTEP + 3):
                    if i < NSTEP:
                        scores(i)
                    if 2 <= i < NSTEP + 2:
                        turn_probs(i - 2)
                    if i >= 3:
                        values(i - 3)

                pe.wait_ge(load_o, 16)
                pe.wait_ge(a_kv_evac, 1 + A_KV_EVAC * b + 8)
                pe.wait_ge(a_o_evac, 2 + NSTEP * (b + 1))
                for t in range(2):
                    for h in range(HQ):
                        mm = pe.matmul(bank[3][:, t * D:(t + 1) * D], OT[:, h, t * P:(t + 1) * P], wo[:, h, :],
                                       start=(h == 0), stop=(h == HQ - 1))
                mm.then_inc(a_kv, 1)

            ST, SM, OB, MB = pair, (bank[0], bank[1]), bank[2], bank[3]
            OBv = OB[:, :].rearrange("p (k q) -> p k q", k=2)
            pe.wait_ge(load_b, 16 * 19)
            pe.wait_ge(b_init, 3)
            pe.wait_ge(kind_rows, 16 * NH)

            def turn(name, b):
                c = b + 1
                events, place = numbered(name, b)
                for e, n in events:
                    kind_, arg = e[0], e[1:]
                    if kind_ in MISC and not (name == "first" and n == 0):
                        pe.wait_ge(misc_free, n)
                    if kind_ == "st":
                        s = arg[0]
                        g, t = divmod(s, KT_TILES)
                        kn = key_count(t)
                        if t == 0:
                            pe.wait_ge(m_rows, 16 * (NG * b + g + 1))
                        pe.wait_ge(exp_done, XSTEP * b + s + 1)
                        for h in range(4):
                            mm = pe.matmul(ST[s % 2][0:kn, h // 2, (h % 2) * S:(h % 2 + 1) * S],
                                           KS[:, g, h, t * P:t * P + kn], QS[:, g, h, :], start=True, stop=True)
                        mm.then_inc(st_made, 1)
                    elif kind_ == "mx":
                        g, u = arg
                        h, r = divmod(u, 8)
                        qt, ch = divmod(r, 4)
                        k0, kn = MAX_CHUNKS[ch]
                        if u == 0:
                            pe.wait_ge(kq_loaded[g % NG], KQ * (b + 1 + g // NG))
                        pe.wait_ge(smax_done, UNITS * (NG * b + g) + u + 1)
                        pe.matmul(SM[u % 2][:, 0:kn], QS[0:KROWS, g % NG, h, qt * P:(qt + 1) * P],
                                  KS[0:KROWS, g % NG, h, k0:k0 + kn], start=True, stop=True).then_inc(smax_made, 1)
                    elif kind_ == "pv":
                        db, s = arg
                        bb = b + db
                        g, t = divmod(s, KT_TILES)
                        kn = key_count(t)
                        pe.wait_ge(exp_done, 2 + XSTEP * bb + s + 1)
                        if g == 0:
                            pe.wait_ge(v_copied, (KT_TILES + 1) * bb + v_slots(t)[-1] + 1)
                        if t == 0:
                            pe.wait_ge(o_evac, 1 + NG * bb + g)
                        for v in v_slots(t):
                            for h in range(4):
                                mm = pe.matmul(OBv[32 * h:32 * h + VW, v // (MIX + 1), :], Vc[0:kn, v, 4 * g + h, :],
                                               PX[0:kn, s % XP_RING, h // 2, (h % 2) * S:(h % 2 + 1) * S],
                                               start=v in (0, MIX + 1), stop=v in (MIX, KT_TILES),
                                               tile_position=(0, 32 * h))
                        mm.then_inc(pv_done, 1)
                    elif kind_ == "otr":
                        bb, g = b + arg[0], arg[1]
                        pe.wait_ge(o_evac, 1 + NG * bb + g + 1)
                        for kd in range(2):
                            for qt in range(2):
                                o = (2 * kd + qt) * P
                                mm = pe.transpose(MB[:, o:o + P], Osb[:, kd, qt * P:(qt + 1) * P], ident[:, :])
                        mm.then_inc(misc_full, 1)
                    elif kind_ == "atr":
                        pe.wait_ge(attn_part, NG * b)
                        for f in range(FT):
                            for qt in range(2):
                                o = f * S + qt * P
                                mm = pe.transpose(MB[:, o:o + P], attn[:, qt, f * P:(f + 1) * P], ident[:, :])
                        mm.then_inc(misc_full, 1)
                    elif kind_ == "oproj":
                        for qt in range(2):
                            for f in range(FT):
                                mm = pe.matmul(MB[:, qt * D:(qt + 1) * D], attnT[:, f, qt * P:(qt + 1) * P], xo_w[:, f, :],
                                               start=(f == 0), stop=(f == FT - 1))
                        mm.then_inc(misc_full, 1)
                    elif kind_ == "mpost":
                        pe.wait_ge(mneg_ready, NG * b + arg[0] + 1)
                        for qt in range(2):
                            mm = pe.transpose(MB[0:8, qt * P:(qt + 1) * P], mneg[:, qt, :], ident[:, :])
                        mm.then_inc(misc_full, 1)
                    elif kind_ == "xT":
                        pe.wait_ge(b_xn, b + arg[0] + 1)
                        for f in range(FT):
                            for u in range(2):
                                o = f * S + u * P
                                mm = pe.transpose(MB[:, o:o + P], xn[:, u, f * P:(f + 1) * P], ident[:, :])
                        mm.then_inc(misc_full, 1)
                    elif kind_ == "q":
                        for u in range(2):
                            for f in range(FT):
                                mm = pe.matmul(MB[:, u * D:(u + 1) * D], xT[:, f, u * P:(u + 1) * P], xq_w[:, f, :],
                                               start=(f == 0), stop=(f == FT - 1))
                        mm.then_inc(misc_full, 1)
                    elif kind_ == "ct":
                        j = arg[1]
                        if j == 0:
                            pe.wait_ge(ctx_loaded, 80 * (b + arg[0] + 1))
                        for f in range(FT):
                            for i, t in enumerate(range(*CHUNKS[j])):
                                kn = key_count(t)
                                o = f * 2 * P + i * P
                                mm = pe.transpose(MB[:, o:o + kn], ctxk[0:kn, t, f * P:(f + 1) * P],
                                                  ident[0:kn, 0:kn])
                        mm.then_inc(misc_full, 1)
                    elif kind_ == "kv":
                        t = arg[1]
                        j, i0 = chunk_of(t)
                        for i, r0, r1 in kinds_of(t):
                            for f in range(FT):
                                mm = pe.matmul(MB[r0:r1, :], ctxT[:, j % 2, f, i0 * P + r0:i0 * P + r1], xkv_w[i][:, f, :],
                                               start=(f == 0), stop=(f == FT - 1))
                        mm.then_inc(misc_full, 1)
                    elif kind_ == "qt":
                        pe.wait_ge(scaled, (NCH + 1) * c + 1)
                        for f in range(FT):
                            for u in range(2):
                                o = f * S + u * P
                                mm = pe.transpose(MB[:, o:o + P], qraw[:, u, f * P:(f + 1) * P], ident[:, :])
                        mm.then_inc(misc_full, 1)
                    elif kind_ == "kt":
                        j = arg[0]
                        pe.wait_ge(scaled, (NCH + 1) * c + j + 2)
                        t0, t1 = CHUNKS[j]
                        for f in range(FT):
                            for t in range(t0, t1):
                                kn = key_count(t)
                                o = f * 256 + (t - t0) * P
                                mm = pe.transpose(MB[:, o:o + kn], ctxk[0:kn, t, f * P:(f + 1) * P], ident[0:kn, 0:kn])
                        mm.then_inc(misc_full, 1)

            turn("first", -1)
            turn("head", 0)
            with pe.Fori(1, B - 2) as b:
                turn("body", b)
            turn("near", B - 2)
            turn("foot", B - 1)
            turn("last", B)

            turn_all(XN3, NT // 2)
            pe.wait_ge(xt_ready, NT)
            pe.wait_ge(load_r, 32)
            for t in range(NT):
                for f in range(FT):
                    mm = pe.matmul(bank[2][:, t * E:(t + 1) * E], XT3[:, f, t * P:(t + 1) * P], wr[:, f, :],
                                   start=(f == 0), stop=(f == FT - 1))
            mm.then_inc(c_logit, 1)

            def gate_up(i, e, g):
                n = TG * e + g
                for m in range(FT):
                    pe.wait_ge(c_h, 2 * n + m + 1)
                    for j, w in enumerate((wg, wu)):
                        for f in range(FT):
                            mm = pe.matmul(pair[m][:, j, :], w[:, i, f, m * P:(m + 1) * P],
                                           XT3[:, f, 512 * g:512 * (g + 1)], start=(f == 0), stop=(f == FT - 1))
                    mm.then_inc(c_gu, 1)

            def down(i, e, g):
                n = TG * e + g
                pe.wait_ge(c_h, 2 + 2 * n + 2)
                for u in range(2):
                    pe.wait_ge(c_down_evac, 2 * n + u + 1)
                    for t in range(2):
                        for m in range(FT):
                            o = (2 * u + t) * P
                            mm = pe.matmul(bank[u][:, t * D:(t + 1) * D], hT[:, g % 2, m, o:o + P], wd[:, i, m, :],
                                           start=(m == 0), stop=(m == FT - 1))
                    mm.then_inc(c_down, 1)

            with pe.Fori(0, E, 2) as e2:
                for i in range(2):
                    e = e2 + i
                    pe.wait_ge(load_w[i], 24 * e2 + 48)
                    gate_up(i, e, 0)
                    for g in range(TG):
                        if g + 1 < TG:
                            gate_up(i, e, g + 1)
                        down(i, e, g)

        @block.scalar
        def _(act):
            act.sem_inc(a_q_evac, 1)
            act.sem_inc(a_exp, 2)
            act.sem_inc(a_pt, 2)

            def move_all(dst, count0):
                for i in range(NT // 2):
                    act.wait_ge(xt_made, count0 + i + 1)
                    act.activation(dst[:, :, 256 * i:256 * (i + 1)], bank[i % 2][:, :].rearrange("p (f n) -> p f n", f=FT),
                                   ACT.Copy).then_inc(xt_ready, 1)

            move_all(XT, 0)
            with act.Fori(0, B) as b:
                for k in range(8):
                    act.wait_ge(a_q, 8 * b + k + 1)
                    act.activation(QT[:, :, 2 * k:2 * k + 2, :].rearrange("p b h q -> p h b q"),
                                   bank[2][:, :].rearrange("p (h b q) -> p h b q", h=2, b=NBLK),
                                   ACT.Copy).then_inc(a_q_evac, 1)

                for i in range(NSTEP + 2):
                    if i < NSTEP:
                        act.wait_ge(a_negmax, NSTEP * b + i + 1)
                        act.wait_ge(a_turned, NSTEP * b + i + 1)
                        for q in range(4):
                            ins = act.activation(PA[:, i % P_RING, q * P:(q + 1) * P], pair[0][:, i % 2, q * P:(q + 1) * P],
                                                 ACT.Exp, bias=negmax[:, i % P_RING, q:q + 1], scale=1.0 / HD,
                                                 accum_out=rowsum[:, i % P_RING, q:q + 1])
                        ins.then_inc(a_exp, 1)
                    if i >= 2:
                        k = i - 2
                        act.wait_ge(a_turned, P_RING + NSTEP * b + k + 1)
                        act.wait_ge(a_pv, NSTEP * b + k + 1)
                        act.activation(PT[:, k % 2, :], pair[1][:, k % 2, :], ACT.Copy).then_inc(a_pt, 1)

            ST, OB, MB = pair, bank[2], bank[3]
            MB3 = MB[:, :].rearrange("p (f n) -> p f n", f=FT)
            act.sem_inc(exp_done, 2)
            act.sem_inc(o_evac, 1)
            act.wait_ge(a_kv_evac, 1 + A_KV_EVAC * B)
            act.wait_ge(b_init, 3)
            act.wait_ge(load_b, 16 * 19)
            act.activation(kind, kindf, ACT.Copy).then_inc(kind_ready, 1)

            def turn(name, b):
                c = b + 1
                events, place = numbered(name, b)
                rows_made = {("sq",) + q[1:]: place[e] for e in place if e[0] in ("q", "kv") for q in squares(e)}
                for e, n in events:
                    kind_, arg = e[0], e[1:]
                    if kind_ == "st":
                        s = arg[0]
                        kn = key_count(s % KT_TILES)
                        act.wait_ge(st_made, XSTEP * b + s + 1)
                        act.wait_ge(pv_done, XSTEP * b + s + 1)
                        act.activation(PX[0:kn, s % XP_RING, :, :], ST[s % 2][0:kn, :, :], ACT.Exp,
                                       scale=float(XD) ** -0.5).then_inc(exp_done, 1)
                    elif kind_ == "oev":
                        bb, g = b + arg[0], arg[1]
                        act.wait_ge(pv_done, XP_RING + XSTEP * bb + KT_TILES * (g + 1))
                        act.wait_ge(attn_part, NG * bb + g)
                        act.activation(Osb[:, :, :], OB[:, :].rearrange("p (k q) -> p k q", k=2), ACT.Copy)\
                           .then_inc(o_evac, 1)
                    elif kind_ in ("xT", "atr"):
                        act.wait_ge(misc_full, n + 1)
                        act.activation((xT if kind_ == "xT" else attnT)[:, :, :], MB3, ACT.Copy).then_inc(misc_free, 1)
                    elif kind_ == "ct":
                        j = arg[1]
                        kn = min(CHUNKS[j][1] * P, NKEY) - CHUNKS[j][0] * P
                        act.wait_ge(misc_full, n + 1)
                        act.activation(ctxT[:, j % 2, :, 0:kn], MB3[:, :, 0:kn], ACT.Copy).then_inc(misc_free, 1)
                    elif kind_ in ("qt", "kt"):
                        act.wait_ge(misc_full, n + 1)
                        if kind_ == "qt":
                            if name != "first":
                                act.wait_ge(split_done, (NCH + 1) * c)
                            segs = [(0, 0, S)]
                            k0, dst, part = 0, qw, qp
                            for g in range(NG):
                                act.wait_ge(kq_loaded[g], KQ * c)
                        else:
                            j = arg[0]
                            k0 = CHUNKS[j][0] * P
                            k1 = min(CHUNKS[j][1] * P, NKEY)
                            segs = [(1, k0, min(k1, N_TXT))] if k0 < N_TXT else []
                            segs += [(2, max(k0, N_TXT), k1)] if k1 > N_TXT else []
                            act.wait_ge(split_done, (NCH + 1) * c + (j if j >= 2 else 0))
                            dst, part = kw[:, j % 2, :, :], kp
                        todo = [(w, s0, s1, f, o) for w, s0, s1 in segs for f in range(FT) for o in range(2)]
                        for w, s0, s1, f, o in todo:
                            to = dst[:, f, s0 - k0:s1 - k0] if o == 0 else part[:, 0, f, s0:s1]
                            ins = act.activation(to, MB3[:, f, s0 - k0:s1 - k0], ACT.Copy, scale=norm_w[:, w, f:f + 1])
                        ins.then_inc(misc_free, 1)
                    elif kind_ == "k2":
                        j = arg[0]
                        act.wait_ge(r1_done, (NCH + 1) * c + j + 1)
                        if j == 0:
                            act.activation(qp[:, 1, :, :], qw[:, :, :], ACT.Copy).then_inc(k2_done, 1)
                        else:
                            k0 = CHUNKS[j - 1][0] * P
                            k1 = min(CHUNKS[j - 1][1] * P, NKEY)
                            act.activation(kp[:, 1, :, k0:k1], kw[:, (j - 1) % 2, :, 0:k1 - k0], ACT.Copy).then_inc(k2_done, 1)
                    if kind_ == "sq":
                        t = arg[1]
                        kn = P if t >= KT_TILES else key_count(t)
                        src = qraw[:, t - KT_TILES, :] if t >= KT_TILES else ctxk[0:kn, t, :]
                        act.wait_ge(misc_free, rows_made[e] + 1)
                        act.wait_ge(sq_done, (KT_TILES + 2) * (b + arg[0]) + (t - KT_TILES if t >= KT_TILES else t + 2))
                        act.activation(junk[0:kn, :], src, ACT.Square, accum_out=sumsq[0:kn, t:t + 1])\
                           .then_inc(sq_done, 1)
                    elif kind_ == "vc":
                        cb, t = b + arg[0], arg[1]
                        if not (name in ("first", "head") and cb in (0,)):
                            act.wait_ge(pv_done, XP_RING + XSTEP * (cb - 1) + (NG - 1) * KT_TILES + t + 1)
                        for v, (i, r0, r1) in zip(v_slots(t), kinds_of(t)):
                            act.activation(Vc[r0:r1, v, :, 0:XD], Vn[r0:r1, t, :].rearrange("p (h d) -> p h d", d=XD),
                                           ACT.Copy).then_inc(v_copied, 1)

            turn("first", -1)
            turn("head", 0)
            with act.Fori(1, B - 2) as b:
                turn("body", b)
            turn("near", B - 2)
            turn("foot", B - 1)
            turn("last", B)

            act.wait_ge(x_added, B)
            move_all(XT3, NT // 2)
            act.wait_ge(c_shift, 1)
            act.activation(prob[:, :, :], logit[:, :, :], ACT.Exp).then_inc(c_exp, 1)
            with act.Fori(0, E * TG) as n:
                for m in range(FT):
                    act.wait_ge(c_gu, 2 * n + m + 1)
                    act.wait_ge(c_h, 2 * n + m + 1)
                    act.activation(silu[:, m, :], pair[m][:, 0, :], ACT.Silu).then_inc(c_silu, 1)

        @block.vector
        def _(dve):
            dve.sem_inc(a_kv_evac, 1)
            dve.sem_inc(a_o_evac, 2)
            norm_stats(dve, loads=True)
            norm_rows(dve, XN)
            dve.wait_ge(load_const, 32)
            dve.tensor_copy(identb[:, :], ident[:, :])
            for m in range(4):
                ins = dve.tensor_copy(mask[:, :, m, :], maskf[:, :, :])
            ins.then_inc(const_ready, 1)

            with dve.Fori(0, B) as b:
                D2 = bank[3][:, :].rearrange("p (h n) -> p h n", h=2)
                for k in range(4):
                    dve.wait_ge(a_kv, A_KV * b + k + 1)
                    dve.tensor_copy((KT if k < 2 else VT)[:, 2 * (k % 2):2 * (k % 2) + 2, :], D2).then_inc(a_kv_evac, 1)
                for t in range(2):
                    dve.wait_ge(a_kv, A_KV * b + 5 + t)
                    dve.tensor_copy(V[:, t, :], bank[3][:, :]).then_inc(a_kv_evac, 1)
                    lo, hi = (64, 128) if t == 0 else (0, 64)
                    dve.tensor_copy(V[lo:hi, 2, :], bank[3][lo:hi, :]).then_inc(a_kv_evac, 1)

                link = dve_link(dve)
                for i in range(NSTEP + 3):
                    if i < NSTEP:
                        r = i % P_RING
                        dve.wait_ge(a_score, NSTEP * b + i + 1)
                        link(dve.tensor_reduce(rowmax[:, r, :], pair[0][:, i % 2, :].rearrange("p (q k) -> p q k", q=4),
                                               X_AXIS, ALU.max))
                        dve.tensor_scalar(negmax[:, r, :], rowmax[:, r, :], -1.0 / HD, None, ALU.mult).then_inc(a_negmax, 1)
                    if 1 <= i < NSTEP + 1:
                        r = (i - 1) % P_RING
                        dve.wait_ge(a_exp, 2 + NSTEP * b + i)
                        link(dve.reciprocal(rowinv[:, r, :], rowsum[:, r, :]))
                        pv = PA[:, r, :].rearrange("p (q k) -> p q k", q=4)
                        dve.tensor_tensor(pv, pv, rowinv[:, r, :].unsqueeze(2).to_broadcast([P, 4, P]), ALU.mult)\
                           .then_inc(a_norm, 1)
                    if i >= 3:
                        k = i - 3
                        blk, j = divmod(k, 2)
                        dve.wait_ge(a_pv, 2 + NSTEP * b + k + 1)
                        dve.tensor_copy(OT[:, 8 * j:8 * j + 8, blk * WIN:(blk + 1) * WIN],
                                        bank[k % 2][:, :].rearrange("p (h n) -> p h n", h=8)).then_inc(a_o_evac, 1)
                dve.wait_ge(a_kv, A_KV * (b + 1))
                xv = X[:, bass.ds(2 * b, 2), :]
                dve.tensor_tensor(xv, xv, D2, ALU.add).then_inc(a_kv_evac, 1)
                dve.sem_clear(chain)

            SM, OB, MB = (bank[0], bank[1]), bank[2], bank[3]
            MB2 = MB[:, :].rearrange("p (u n) -> p u n", u=2)
            dve.sem_inc(smax_done, 2)
            dve.wait_ge(a_kv_evac, 1 + A_KV_EVAC * B)
            norm_stats(dve)
            dve.memset(Vc[:, :, :, :], 1.0).then_inc(b_init, 1)
            dve.wait_ge(b_init, 1)
            dve.memset(Vc[HALF:P, MIX, :, :], 0.0)
            dve.memset(Vc[0:HALF, MIX + 1, :, :], 0.0)
            dve.memset(sumsq[:, :], 1.0).then_inc(b_init, 1)
            dve.memset(OB[:, :], 0.0).then_inc(b_init, 1)
            dve.wait_ge(b_init, 3)
            dve.wait_ge(load_b, 16 * 19)

            def turn(name, b):
                c = b + 1
                events, place = numbered(name, b)
                link = dve_link(dve)
                for e, n in events:
                    kind_, arg = e[0], e[1:]
                    if kind_ == "mx":
                        g, u = arg
                        h, r = divmod(u, 8)
                        qt, ch = divmod(r, 4)
                        dve.wait_ge(smax_made, UNITS * (NG * b + g) + u + 1)
                        dve.tensor_reduce(xmax[:, qt, h, ch:ch + 1], SM[u % 2][:, 0:MAX_CHUNKS[ch][1]], X_AXIS, ALU.max)\
                           .then_inc(smax_done, 1)
                    elif kind_ == "mred":
                        g = arg[0]
                        dve.wait_ge(smax_done, 2 + UNITS * (NG * b + g + 1))
                        dve.tensor_reduce(m8[:, :, 0, :], xmax[:, :, :, 0:3], X_AXIS, ALU.max)
                        link(dve.tensor_copy(m8[:, :, 1, :], xmax[:, :, :, 3]))
                        dve.tensor_scalar(mneg[:, :, :], m8[:, :, :, :].rearrange("p a k h -> p a (k h)"), -1.0, None,
                                          ALU.mult).then_inc(mneg_ready, 1)
                    elif kind_ == "mpost":
                        dve.wait_ge(misc_full, n + 1)
                        dve.wait_ge(m_rows, 16 * (NG * b + arg[0]))
                        dve.tensor_copy(mT[:, :], MB[0:8, 0:S]).then_inc(misc_free, 1)
                        dve.wait_ge(misc_free, n + 1)
                        dve.sem_inc(mT_ready, 1)
                    elif kind_ == "otr":
                        bb, g = b + arg[0], arg[1]
                        dve.wait_ge(misc_full, n + 1)
                        ov = MB[:, :].rearrange("p (k q h d) -> p k q h d", k=2, q=2, h=4)
                        link(dve.reciprocal(oinv[:, :, :, :], ov[:, :, :, :, XD]))
                        for kd in range(2):
                            ins = dve.tensor_tensor(otmp[:, kd, :, :].rearrange("p q (h d) -> p q h d", h=4),
                                                    ov[:, kd, :, :, 0:XD],
                                                    oinv[:, kd, :, :].unsqueeze(3).to_broadcast([P, 2, 4, XD]), ALU.mult)
                        ins.then_inc(misc_free, 1)
                        dve.wait_ge(misc_free, n + 1)
                        dve.tensor_tensor(attn[:, :, 64 * g:64 * g + 64], otmp[:, 0, :, :], otmp[:, 1, :, :], ALU.add)\
                           .then_inc(attn_part, 1)
                    elif kind_ == "oproj":
                        dve.wait_ge(misc_full, n + 1)
                        dve.tensor_tensor(oproj[:, :, :], MB2, xo_b[:, :].unsqueeze(1).to_broadcast([P, 2, D]), ALU.add)\
                           .then_inc(misc_free, 1)
                        dve.wait_ge(misc_free, n + 1)
                        xv = X[:, bass.ds(2 * (b - 1), 2), :]
                        dve.tensor_tensor(xv, xv, oproj[:, :, :], ALU.add).then_inc(x_added, 1)
                    elif kind_ == "ln":
                        c2 = b + arg[0]
                        if arg[0] == 2:
                            dve.wait_ge(misc_full, place[("qt",)] + 1)
                        for u in range(2):
                            ins = dve.tensor_scalar(xn[:, u, :], X[:, bass.ds(2 * c2 + u, 1), :].rearrange("p o d -> p (o d)"),
                                                    meanvar[:, bass.ds(2 * c2 + u, 1), 0:1].rearrange("p o d -> p (o d)"),
                                                    rstd[:, bass.ds(2 * c2 + u, 1)], ALU.subtract, ALU.mult)
                        ins.then_inc(b_xn, 1)
                    elif kind_ == "q":
                        dve.wait_ge(misc_full, n + 1)
                        dve.tensor_tensor(qraw[:, :, :], MB2, xq_b[:, :].unsqueeze(1).to_broadcast([P, 2, D]), ALU.add)\
                           .then_inc(misc_free, 1)
                    elif kind_ == "kv":
                        t = arg[1]
                        dve.wait_ge(misc_full, n + 1)
                        if not (name == "first" and arg[0] == 1):
                            dve.wait_ge(v_copied, (KT_TILES + 1) * (b + arg[0] - 1) + v_slots(t)[-1] + 1)
                        for i, r0, r1 in kinds_of(t):
                            ins = dve.tensor_tensor(kv[r0:r1, t, :], MB[r0:r1, :], xkv_b[i][r0:r1, :], ALU.add)
                        ins.then_inc(misc_free, 1)
                    elif kind_ == "rms":
                        if arg[0] == 0:
                            dve.wait_ge(sq_done, (KT_TILES + 2) * (c + 1))
                        else:
                            dve.wait_ge(rms_step, RMS_OPS * c + arg[0])
                        inverse_root(dve, arg[0], sumsq[:, :], 1.0 / D, RMS_EPS, KT_TILES + 2, kq_rstd[:, :])\
                            .then_inc(rms_step, 1)
                    elif kind_ == "sc":
                        j = arg[0]
                        dve.wait_ge(rms_step, RMS_OPS * (c + 1))
                        if j == 0:
                            for u in range(2):
                                ins = dve.tensor_scalar(qraw[:, u, :], qraw[:, u, :], kq_rstd[:, KT_TILES + u:KT_TILES + u + 1],
                                                        None, ALU.mult)
                        else:
                            for t in range(*CHUNKS[j - 1]):
                                kn = key_count(t)
                                ins = dve.tensor_scalar(ctxk[0:kn, t, :], ctxk[0:kn, t, :], kq_rstd[0:kn, t:t + 1], None,
                                                        ALU.mult)
                        ins.then_inc(scaled, 1)
                dve.sem_clear(chain)

            turn("first", -1)
            turn("head", 0)
            with dve.Fori(1, B - 2) as b:
                turn("body", b)
            turn("near", B - 2)
            turn("foot", B - 1)
            turn("last", B)

            dve.sem_inc(c_h, 2)
            dve.sem_inc(c_down_evac, 2)
            dve.wait_ge(x_added, B)
            norm_stats(dve)
            norm_rows(dve, XN3)
            link = dve_link(dve)
            dve.wait_ge(c_logit, 1)
            lv = bank[2][:, 0:NT * E].rearrange("p (t e) -> p t e", e=E)
            link(dve.tensor_reduce(top[:, :], lv, X_AXIS, ALU.max))
            dve.tensor_tensor(logit[:, :, :], lv, top[:, :].unsqueeze(2).to_broadcast([P, NT, E]), ALU.subtract)\
               .then_inc(c_shift, 1)
            dve.wait_ge(c_exp, 1)
            dve.wait_ge(load_r, 32)
            pj = prob[:, :, :].unsqueeze(2).to_broadcast([P, NT, E, E])
            pi = prob[:, :, :].unsqueeze(3).to_broadcast([P, NT, E, E])
            dve.tensor_tensor(beats[:, :, :, :], pj, pi, ALU.is_gt)
            link(dve.tensor_tensor(ties[:, :, :, :], pj, pi, ALU.is_equal))
            link(dve.tensor_tensor(ties[:, :, :, :], ties[:, :, :, :],
                                   tri[:, :, :].unsqueeze(1).to_broadcast([P, NT, E, E]), ALU.mult))
            link(dve.tensor_tensor(beats[:, :, :, :], beats[:, :, :, :], ties[:, :, :, :], ALU.add))
            link(dve.tensor_reduce(rank[:, :, :], beats[:, :, :, :], X_AXIS, ALU.add))
            link(dve.scalar_tensor_tensor(out=gate[:, :, :], in0=rank[:, :, :], scalar=1.5, in1=prob[:, :, :],
                                          op0=ALU.is_lt, op1=ALU.mult))
            link(dve.tensor_reduce(topsum[:, :], gate[:, :, :], X_AXIS, ALU.add))
            link(dve.reciprocal(top[:, :], topsum[:, :]))
            link(dve.tensor_tensor(gate[:, :, :], gate[:, :, :], top[:, :].unsqueeze(2).to_broadcast([P, NT, E]), ALU.mult))
            dve.sem_clear(chain)

            def hidden(e, g):
                n = TG * e + g
                for m in range(FT):
                    dve.wait_ge(c_silu, 2 * n + m + 1)
                    if g >= 2:
                        dve.wait_ge(c_down, 2 * (n - 1))
                    dve.tensor_tensor(hT[:, g % 2, m, :], silu[:, m, :], pair[m][:, 1, :], ALU.mult).then_inc(c_h, 1)

            def add(e, g):
                n = TG * e + g
                for u in range(2):
                    dve.wait_ge(c_down, 2 * n + u + 1)
                    for t in range(2):
                        tile = 4 * g + 2 * u + t
                        ins = dve.scalar_tensor_tensor(out=X[:, tile, :], in0=bank[u][:, t * D:(t + 1) * D],
                                                       scalar=gate[:, tile, bass.ds(e, 1)], in1=X[:, tile, :],
                                                       op0=ALU.mult, op1=ALU.add)
                    ins.then_inc(c_down_evac, 1)

            with dve.Fori(0, E) as e:
                hidden(e, 0)
                for g in range(TG):
                    if g + 1 < TG:
                        hidden(e, g + 1)
                    add(e, g)

        @block.gpsimd
        def _(pool):
            pool.sem_inc(a_turned, P_RING)
            pool.sem_inc(a_pv, 2)
            pool.sem_inc(pv_done, XP_RING)

            def turn(name, b):
                c = b + 1
                events, place = numbered(name, b)
                for e, n in events:
                    kind_, arg = e[0], e[1:]
                    if kind_ in ("qt", "kt"):
                        pool.wait_ge(misc_free, n + 1)
                        if kind_ == "qt":
                            pool.tensor_tensor(qw[:, :, :], qw[:, :, :], qp[:, 0, :, :], ALU.subtract).then_inc(r1_done, 1)
                        else:
                            j = arg[0]
                            k0 = CHUNKS[j][0] * P
                            k1 = min(CHUNKS[j][1] * P, NKEY)
                            kv = kw[:, j % 2, :, 0:k1 - k0]
                            pool.tensor_tensor(kv, kv, kp[:, 0, :, k0:k1], ALU.subtract).then_inc(r1_done, 1)
                    elif kind_ == "k2":
                        j = arg[0]
                        pool.wait_ge(k2_done, (NCH + 1) * c + j + 1)
                        if j == 0:
                            pool.tensor_tensor(qp[:, 2, :, :], qw[:, :, :], qp[:, 1, :, :], ALU.subtract).then_inc(split_done, 1)
                        else:
                            k0 = CHUNKS[j - 1][0] * P
                            k1 = min(CHUNKS[j - 1][1] * P, NKEY)
                            pool.tensor_tensor(kp[:, 2, :, k0:k1], kw[:, (j - 1) % 2, :, 0:k1 - k0], kp[:, 1, :, k0:k1],
                                               ALU.subtract).then_inc(split_done, 1)

            pool.wait_ge(a_kv_evac, 1 + A_KV_EVAC * B)
            pool.memset(KS[96:P, :, :, :], 0.0)
            pool.memset(QS[96:P, :, :, :], 0.0).then_inc(zero_rows, 1)
            pool.wait_ge(b_init, 3)
            turn("first", -1)
            turn("head", 0)
            with pool.Fori(1, B - 2) as b:
                turn("body", b)
            turn("near", B - 2)
            turn("foot", B - 1)


def kernel(**inputs):
    import numpy as _np
    import concourse.bacc as _bacc
    from concourse.bass_utils import run_bass_kernel_spmd as _run

    def constants():
        r = _np.arange(P)[:, None] % WIN
        k = _np.arange(P)[None, :]
        own = (k < WIN) & (k <= r)
        std = (k >= r + 1) & (k <= r + WIN)
        swap = ((k < WIN) & (k <= r)) | ((k >= WIN) & (k - WIN >= r + 1))
        mask = _np.stack([_np.where(m, 0.0, -1e30) for m in (own, std, swap)], 1).astype(_np.float32)
        tri = _np.broadcast_to(_np.tril(_np.ones((E, E), _np.float32), -1), (P, E, E))
        kinds = _np.zeros((2, NKEY), _np.float32)
        kinds[0, :N_TXT] = 1.0
        kinds[1, N_TXT:] = 1.0
        return {"c_ident": _np.eye(P, dtype=_np.float32), "c_mask": mask, "c_tri": _np.ascontiguousarray(tri), "c_kind": kinds}

    data = {n: _np.asarray(v) for n, v in inputs.items()}
    for n in ("q_w", "q_b", "k_w", "k_b", "k_img_w", "k_img_b", "norm_q_w", "norm_k_w", "norm_k_img_w"):
        v = data[f"L0_xattn_{n}"]
        data[f"L0_xattn_{n}"] = v.reshape(NG, 4, XD, -1).transpose(0, 2, 1, 3).reshape(v.shape)
    for n in ("q", "k", "v", "k_img", "v_img", "o"):
        data[f"wT_{n}"] = _np.ascontiguousarray(data.pop(f"L0_xattn_{n}_w").T)
    data.update(constants())
    nc = _bacc.Bacc("TRN2", target_bir_lowering=False, num_devices=1)
    arrays, aps = {}, {}
    for name, v in data.items():
        v = _np.ascontiguousarray(v)
        arrays[f"in_{name}"] = v
        aps[name] = nc.dram_tensor(f"in_{name}", v.shape, mybir.dt.from_np(v.dtype), kind="ExternalInput").ap()
    out = nc.dram_tensor("out_x", (B, S, D), F32, kind="ExternalOutput").ap()
    decoder_layer(nc, aps, out)
    r = _run(nc, [arrays], core_ids=[0])
    return r.results[0]["out_x"]
```

```python
import concourse.bass as bass
from concourse import mybir
from contextlib import ExitStack

F32 = mybir.dt.float32
BF16 = mybir.dt.bfloat16
F32R = mybir.dt.float32r
I32 = mybir.dt.int32
ALU = mybir.AluOpType
ACT = mybir.ActivationFunctionType
X_AXIS = mybir.AxisListType.X

P = 128
B, S, D = 8, 256, 256
NT = B * S // P
FT = D // P
X_LOADS = [(0, 2), (2, 6), (6, 11), (11, 16)]
LN_EPS, RMS_EPS = 1e-5, 1e-6

HQ, HKV, HD, WIN = 16, 4, 128, 64
NBLK = S // WIN
NSTEP = NBLK * 2
P_RING = 4

NH, XD = 16, 16
N_TXT, N_IMG = 1344, 257
NKEY = N_TXT + N_IMG
KT_TILES = -(-NKEY // P)
LAST = NKEY - (KT_TILES - 1) * P
MIX = N_TXT // P
HALF = N_TXT - MIX * P
NG = 4
XSTEP = NG * KT_TILES
PARTS = [(0, 0), (0, 1), (1, 0), (1, 1), (0, 2), (2, 0), (1, 2)]
KROWS = 16 * len(PARTS)
MAXN = N_TXT // 3
MAX_CHUNKS = [(0, MAXN), (MAXN, MAXN), (2 * MAXN, MAXN), (N_TXT, N_IMG)]
UNITS = 4 * 2 * len(MAX_CHUNKS)
XP_RING = 4
KW_RING = 3
CHUNKS = [(0, 2), (2, 4), (4, 6), (6, 8), (8, 10), (10, 11), (11, 13)]
NCH = len(CHUNKS)
MAX_WINDOWS = [(0, 11), (11, 23), (23, 35), (37, 49)]
K_STEPS = (20, 22, 24, 25, 27, 29, 30)
RMS_OPS = 12
VW = XD + 1

E, F = 8, 256
TG = 4


def kinds_of(t):
    return [(0, 0, P)] if t < MIX else [(0, 0, HALF), (1, HALF, P)] if t == MIX else [(1, 0, key_count(t))]


def chunk_of(t):
    return next((j, t - t0) for j, (t0, t1) in enumerate(CHUNKS) if t0 <= t < t1)


def v_slots(t):
    return (t,) if t < MIX else (MIX, MIX + 1) if t == MIX else (t + 1,)


def key_count(t):
    return LAST if t == KT_TILES - 1 else P


CONTEXT_EVENTS = [e for j, (t0, t1) in enumerate(CHUNKS) for e in [("ct", j)] + [("kv", t) for t in range(t0, t1)]]
EARLY = 9


def early_events():
    return [("xT", 2), ("q", 2)] + [(k, 2, i) for k, i in CONTEXT_EVENTS[:EARLY]]


def squares(e):
    return [("sq", e[1], t) for t in ((KT_TILES, KT_TILES + 1) if e[0] == "q" else (e[2],))]


def with_squares(events):
    return [x for e in events for x in [e] + (squares(e) if e[0] in ("q", "kv") else [])]


def attention_events(tail, prep, early):
    mid = {s: [] for s in range(XSTEP)}
    end = {s: [] for s in range(XSTEP)}
    late = {s: [] for s in range(XSTEP)}
    used = set()

    def use(s, e):
        mid[s] += [e]
        used.add(s)

    def context_event(s, e):
        end[s] += [e]
        if e[0] in ("q", "kv"):
            (mid[s + 1] if s + 1 < XSTEP else end[s]).extend(squares(e))

    def free_step(s):
        while s in used:
            s += 1
        used.add(s)
        return s

    if tail:
        use(2, ("otr", -1, 3))
        use(4, ("atr", -1))
        use(6, ("oproj", -1))
    for hg in range(NG - 1):
        use(KT_TILES * (hg + 1) + 2, ("otr", 0, hg))
    for hg, (s0, s1) in enumerate(MAX_WINDOWS[:NG - 1 + prep]):
        for u in range(UNITS):
            s, part = divmod(u * (s1 - s0) * 3 // UNITS, 3)
            (mid, end, late)[part][s0 + s] += [("mx", hg + 1, u)]
        late[s1 - 1] += [("mred", hg + 1)]
        end[s1] += [("mpost", hg + 1)]
        used.add(s1)
    if prep:
        at = 0
        for k, i in CONTEXT_EVENTS[EARLY:]:
            at = free_step(at)
            context_event(at, (k, 1, i))
        for k in range(RMS_OPS):
            (mid, end, late)[k % 6 // 2][at + 1 + k // 6] += [("rms", k)]
        at += 1 + RMS_OPS // 6
        late[at - 1] += [("sc", 0), ("sc", 1)]
        use(at + 1, ("qt",))
        mid[at + 2] += [("k2", 0)]
        end[at + 3] += [("qp", 0)]
        assert at + 1 < K_STEPS[0]
        for j, at in enumerate(K_STEPS):
            end[at - 3] += [("sc", j + 1)] if j else []
            assert at not in used
            use(at, ("kt", j))
            mid[at + 1] += [("k2", j + 1)]
        end[at + 1] += [("kq", 0)]
        end[at + 3] += [("ctx",)]
        end[MAX_WINDOWS[2][1]] += [("kq", 1)]
        end[3 * KT_TILES + 1] += [("kq", 2)]
    if early:
        at = MAX_WINDOWS[2][1] + 1
        end[at - 2] += [("ln", 2)]
        for e in early_events():
            at = free_step(max(at, 3 * KT_TILES + 3) if e[0] == "ct" else at)
            context_event(at, e)
    if not prep:
        first = MAX_WINDOWS[NG - 2][1] - 3
        for p in range(B - 1):
            end[first + p // 2] += [("cs", p)]
        end[first + 3] += [("ca", 0, NT - 2)]
        for k in range(RMS_OPS):
            end[first + 4 + k // 6] += [("cr", 0, NT - 2, k)]
        at = first + 5
        for p in range(B - 1):
            at = free_step(at + 1)
            end[at - 1] += [("cw", p)]
            end[at] += [("cT", p)]
    ev = []
    for s in range(XSTEP):
        hg, t = divmod(s, KT_TILES)
        ev.append(("st", s))
        ev += mid[s]
        if s:
            ev.append(("pv", 0, s - 1))
        elif tail:
            ev.append(("pv", -1, XSTEP - 1))
        if t == 0 and (hg or tail):
            ev.append(("oev", 0, hg - 1) if hg else ("oev", -1, NG - 1))
        if s == 0:
            ev += [("vc", 0, KT_TILES - 2), ("vc", 0, KT_TILES - 1)]
        if prep and s - 3 * KT_TILES - 2 >= 0:
            ev.append(("vc", 1, s - 3 * KT_TILES - 2))
        ev += end[s] + late[s]
    if prep:
        ev.append(("kq", 3))
    return ev


def first_events():
    ev = [("ct", 1, 0), ("ct", 1, 1), ("kinds",), ("ln", 1)] + with_squares([("xT", 1), ("q", 1)])
    for j, (t0, t1) in enumerate(CHUNKS):
        ev += with_squares([("kv", 1, t) for t in range(t0, t1)])
        ev += [("ct", 1, j + 2)] if j + 2 < NCH else []
    ev += [("rms", k) for k in range(RMS_OPS)] + [("sc", j) for j in range(NCH + 1)] + [("qt",)]
    for j in range(NCH):
        ev += [("kt", j), ("k2", j)] + ([("qp", 0)] if j == 1 else [])
    ev += [("k2", NCH), ("kq", 0), ("ctx",)] + [("kq", g) for g in range(1, NG)]
    ev += [("vc", 1, t) for t in range(KT_TILES - 2)] + [("ln", 2)]
    early = with_squares(early_events())
    ev += early[:4]
    early = early[4:]
    for u in range(UNITS):
        ev.append(("mx", NG, u))
        if early and u > 7:
            ev.append(early.pop(0))
    return ev + early + [("mred", NG), ("mpost", NG)]


def last_events():
    return [("pv", -1, XSTEP - 1), ("oev", -1, NG - 1), ("otr", -1, NG - 1), ("atr", -1), ("oproj", -1),
            ("cs", B - 1), ("ca", NT - 2, NT)] + [("cr", NT - 2, NT, k) for k in range(RMS_OPS)] + \
           [("cw", B - 1), ("cT", B - 1)]


MISC = ("cT", "xT", "q", "ct", "kv", "qt", "kt", "mpost", "otr", "atr", "oproj")

TURNS = {
    "first": first_events(),
    "head": attention_events(tail=False, prep=True, early=True),
    "body": attention_events(tail=True, prep=True, early=True),
    "near": attention_events(tail=True, prep=True, early=False),
    "foot": attention_events(tail=True, prep=False, early=False),
    "last": last_events(),
}
MISC_BANKS = 5
FIRST_MX = next(i for i, e in enumerate(TURNS["first"]) if e[0] == "mx")


def misc_slots(turn):
    k = 0
    for i, e in enumerate(TURNS[turn]):
        if e[0] in MISC:
            yield k % MISC_BANKS if turn == "first" and i < FIRST_MX else 0
            k += 1
        else:
            yield None


MISC_COUNT = {name: sum(m == 0 for m in misc_slots(name)) for name in TURNS}
FIRST_COUNT = [sum(m == i for m in misc_slots("first")) for i in range(MISC_BANKS)]


def numbered(turn, b):
    base = 0
    for name, count in (("first", 1), ("head", 1), ("body", B - 3), ("near", 1), ("foot", 1), ("last", 1)):
        if name == turn:
            break
        base += MISC_COUNT[name] * count
    if turn == "body":
        base += (b - 1) * MISC_COUNT["body"]
    used = [0] * MISC_BANKS
    out, place = [], {}
    for e, m in zip(TURNS[turn], misc_slots(turn)):
        if m is None:
            out.append((e, 0, 0))
        else:
            n = used[m] + (base if m == 0 else 0)
            out.append((e, m, n))
            place[e] = (m, n)
            used[m] += 1
    return out, place


def decoder_layer(nc, a, out):
    ctx = ExitStack()
    with ctx:
        def sb(name, shape, dt=F32, stack=ctx):
            return stack.enter_context(nc.sbuf_tensor(name, shape, dt))

        def sem(name):
            return ctx.enter_context(nc.semaphore(name))

        X = sb("X", [P, NT, D])
        ident = sb("ident", [P, P])
        identb = sb("identb", [P, P], BF16)
        stats = sb("stats", [P, NT, 6])
        meanvar = sb("meanvar", [P, NT, 2])
        rstd = sb("rstd", [P, NT])
        newton_v = sb("newton_v", [P, NT])
        newton_t = sb("newton_t", [P, NT])
        newton_i = sb("newton_i", [P, NT], I32)
        newton_y = sb("newton_y", [P, NT], I32)

        pair = [ctx.enter_context(nc.psum_tensor(f"pair{i}", [P, 2, 512], F32)) for i in range(2)]
        bank = [ctx.enter_context(nc.psum_tensor(f"bank{i}", [P, 512], F32)) for i in range(4)]

        xo_w = sb("xo_w", [P, FT, D])
        xo_b = sb("xo_b", [P, D])
        norm_w = sb("norm_w", [P, 3, FT])

        ahead = ExitStack()
        xq_b = sb("xq_b", [P, D], stack=ahead)
        xq_w = sb("xq_w", [P, FT, D], stack=ahead)
        xkv_b = [sb(f"xkv_b{i}", [P, 2 * D], stack=ahead) for i in range(2)]
        xkv_w = [sb(f"xkv_w{i}", [P, FT, 2 * D], stack=ahead) for i in range(2)]
        kv = sb("kv", [P, KT_TILES, 2 * D], stack=ahead)
        ctxk = kv[:, :, 0:D]
        Vn = kv[:, :, D:2 * D]

        with ExitStack() as sa:
            XT = sb("XT", [P, FT, S], stack=sa)
            XN = sb("XN", [P, 2, D], stack=sa)
            XS = sb("XS", [P, 2, 6], stack=sa)
            XMV = sb("XMV", [P, 2, 2], stack=sa)
            XR = sb("XR", [P, 2], stack=sa)
            wq = sb("wq", [P, FT, HQ * HD], stack=sa)
            wk = sb("wk", [P, FT, HKV * HD], stack=sa)
            wv = sb("wv", [P, FT, HKV * HD], stack=sa)
            wo = sb("wo", [P, 2, HQ, D], F32R, stack=sa)
            wo_raw = kv[:, 0:HQ // 2, :].rearrange("p t (u n) -> p (t u) n", u=2)
            QT = sb("QT", [P, NBLK, HQ, WIN], stack=sa)
            KT = sb("KT", [P, HKV, S], stack=sa)
            VT = sb("VT", [P, HKV, S], stack=sa)
            V = sb("V", [P, 3, HKV * HD], stack=sa)
            PA = sb("PA", [P, P_RING, 512], stack=sa)
            PT = sb("PT", [P, 2, 512], stack=sa)
            OT = sb("OT", [P, 2, HQ, S], F32R, stack=sa)
            maskf = sb("maskf", [P, 3, P], stack=sa)
            mask = sb("mask", [P, 3, 4, P], BF16, stack=sa)
            rowmax = sb("rowmax", [P, P_RING, 4], stack=sa)
            negmax = sb("negmax", [P, P_RING, 4], stack=sa)
            rowsum = sb("rowsum", [P, P_RING, 4], stack=sa)
            rowinv = sb("rowinv", [P, P_RING, 4], stack=sa)

        with ExitStack() as sbk:
            kp = sb("kp", [P, 3, FT, NKEY], BF16, stack=sbk)
            kw = sb("kw", [P, KW_RING, FT, 2 * P], stack=sbk)
            qw = sb("qw", [P, FT, S], stack=sbk)
            qp = sb("qp", [P, 3, FT, S], BF16, stack=sbk)
            xn = sb("xn", [P, FT, D], stack=sbk)
            xT = sb("xT", [P, FT, S], stack=sbk)
            qraw = xn
            ctxT = sb("ctxT", [P, 2, FT, 2 * P], stack=sbk)
            Vc = sb("Vc", [P, KT_TILES + 1, NH, VW], stack=sbk)
            KS = sb("KS", [P, NG, 4, NKEY], BF16, stack=sbk)
            QS = sb("QS", [P, NG, 4, S], BF16, stack=sbk)
            PX = sb("PX", [P, XP_RING, 2, 512], stack=sbk)
            kindf = PX[0:2, :, :, :].rearrange("p a b n -> p (a b n)")[:, 0:NKEY]
            kind = PX[0:2, :, :, :].rearrange("p a b n -> p (a b n)")[:, 2048:2048 + (NKEY + 1) // 2].bitcast(BF16)[:, 0:NKEY]
            Osb = sb("Osb", [P, 2, S], stack=sbk)
            attn = sb("attn", [P, 2, D], stack=sbk)
            attnT = sb("attnT", [P, FT, S], stack=sbk)
            junk = sb("junk", [P, D], stack=sbk)
            oproj = sb("oproj", [P, 2, D], stack=sbk)
            sumsq = sb("sumsq", [P, KT_TILES + 2], stack=sbk)
            kq_rstd = sb("kq_rstd", [P, KT_TILES + 2], stack=sbk)
            xmax = sb("xmax", [P, 2, 4, 4], stack=sbk)
            m8 = sb("m8", [P, 2, 2, 4], stack=sbk)
            mneg = sb("mneg", [P, 2, 8], stack=sbk)
            mT = sb("mT", [8, S], BF16, stack=sbk)
            oinv = sb("oinv", [P, 2, 2, 4], stack=sbk)
            otmp = sb("otmp", [P, 2, 2, 64], stack=sbk)
        ahead.close()

        with ExitStack() as sc:
            XN3 = sb("XN3", [P, NT, D], stack=sc)
            XT3 = sb("XT3", [P, 2, FT, B * S], F32R, stack=sc)
            wr = sb("wr", [P, FT, E], stack=sc)
            tri = sb("tri", [P, E, E], stack=sc)
            w3 = sb("w3", [P, 2, 3, FT, F], stack=sc)
            wrp = sb("wrp", [P, 2, FT, P], F32R, stack=sc)
            logitT = sb("logitT", [E, B * S], stack=sc)
            w3p = sb("w3p", [P, 2, 2, 3, FT, F], F32R, stack=sc)
            logit = sb("logit", [P, NT, E], stack=sc)
            prob = sb("prob", [P, NT, E], stack=sc)
            beats = sb("beats", [P, NT, E, E], stack=sc)
            ties = sb("ties", [P, NT, E, E], stack=sc)
            rank = sb("rank", [P, NT, E], stack=sc)
            gate = sb("gate", [P, NT, E], stack=sc)
            top = sb("top", [P, NT], stack=sc)
            topsum = sb("topsum", [P, NT], stack=sc)
            silu = sb("silu", [P, 2, 512], stack=sc)
            hf = sb("hf", [P, 2, 512], stack=sc)
            hT = sb("hT", [P, 2, 2, FT, 512], F32R, stack=sc)

        chain = sem("chain")
        load_x = [sem(f"load_x{i}") for i in range(len(X_LOADS))]
        load_ident = sem("load_ident")
        load_mask = sem("load_mask")
        load_k = sem("load_k")
        load_q = [sem(f"load_q{q}") for q in range(4)]
        load_v = sem("load_v")
        load_o = sem("load_o")
        o_split = sem("o_split")
        const_ready = sem("const_ready")
        xn_ready = sem("xn_ready")
        xt_made = sem("xt_made")
        xt_ready = sem("xt_ready")
        a_kv = sem("a_kv")
        a_kv_evac = sem("a_kv_evac")
        a_q = sem("a_q")
        a_q_evac = sem("a_q_evac")
        a_score = sem("a_score")
        a_negmax = sem("a_negmax")
        a_exp = sem("a_exp")
        a_norm = sem("a_norm")
        a_turned = sem("a_turned")
        a_pt = sem("a_pt")
        a_pv = sem("a_pv")
        a_o_evac = sem("a_o_evac")

        load_b = sem("load_b")
        load_kind = sem("load_kind")
        v_init = sem("v_init")
        zero_rows = sem("zero_rows")
        kind_ready = sem("kind_ready")
        kind_rows = sem("kind_rows")
        b_init = sem("b_init")
        ctx_loaded = sem("ctx_loaded")
        gone_ahead = sem("gone_ahead")
        misc_full = [sem(f"misc_full{i}") for i in range(MISC_BANKS)]
        misc_free = [sem(f"misc_free{i}") for i in range(MISC_BANKS)]
        b_xn = sem("b_xn")
        v_copied = sem("v_copied")
        sq_done = sem("sq_done")
        rms_step = sem("rms_step")
        scaled = sem("scaled")
        r1_done = sem("r1_done")
        k2_done = sem("k2_done")
        split_done = sem("split_done")
        kq_loaded = [sem(f"kq_loaded{g}") for g in range(NG)]
        smax_made = sem("smax_made")
        smax_done = sem("smax_done")
        mneg_ready = sem("mneg_ready")
        mT_ready = sem("mT_ready")
        m_rows = sem("m_rows")
        st_made = sem("st_made")
        exp_done = sem("exp_done")
        pv_done = sem("pv_done")
        o_evac = sem("o_evac")
        attn_part = sem("attn_part")
        x_added = sem("x_added")

        load_r = sem("load_r")
        load_w = [sem(f"load_w{i}") for i in range(2)]
        c_logit = sem("c_logit")
        c_shift = sem("c_shift")
        c_exp = sem("c_exp")
        c_gu = sem("c_gu")
        c_silu = sem("c_silu")
        c_xhi = sem("c_xhi")
        wr_split = sem("wr_split")
        wr_zeros = sem("wr_zeros")
        c_router = sem("c_router")
        c_router_evac = sem("c_router_evac")
        w_hi = sem("w_hi")
        w_lo = sem("w_lo")
        c_h = sem("c_h")
        c_hhi = sem("c_hhi")
        c_hlo = sem("c_hlo")
        c_down = sem("c_down")
        c_down_evac = sem("c_down_evac")
        stored = sem("stored")

        A_KV = 8
        A_KV_EVAC = 10

        def a_kv_read(n):
            return 2 + (0, 1, 2, 3, 4, 6, 8, 9, 10)[n + 1]

        KQ = 16 * 2 * len(PARTS)

        x_flat = a["x"].rearrange("b s d -> (b s) d")
        out_flat = out.rearrange("b s d -> (b s) d")
        block = ctx.enter_context(nc.Block())

        def misc_banks(pair, bank):
            return [bank[3][:, :]] + [pair[i][:, j, :] for i in range(2) for j in range(2)]

        def dve_link(eng):
            count = [0]

            def link(ins):
                count[0] += 1
                ins.then_inc(chain, 1)
                eng.wait_ge(chain, count[0])
            return link

        def inverse_root(eng, k, src, scale, eps, n, result):
            v, t, y = newton_v[:, 0:n], newton_t[:, 0:n], newton_y[:, 0:n].bitcast(F32)
            if k == 0:
                return eng.tensor_scalar(v, src, scale, eps, ALU.mult, ALU.add)
            if k == 1:
                return eng.tensor_single_scalar(newton_i[:, 0:n], v.bitcast(I32), 1, ALU.logical_shift_right)
            if k == 2:
                return eng.tensor_scalar(newton_y[:, 0:n], newton_i[:, 0:n], -1.0, float(0x5F3759DF), ALU.mult, ALU.add)
            if k % 3 == 0:
                return eng.scalar_tensor_tensor(out=t, in0=y, scalar=-0.5, in1=y, op0=ALU.mult, op1=ALU.mult)
            if k % 3 == 1:
                return eng.tensor_tensor(t, t, v, ALU.mult)
            return eng.scalar_tensor_tensor(out=result if k == RMS_OPS - 1 else y, in0=t, scalar=1.5, in1=y,
                                            op0=ALU.add, op1=ALU.mult)

        def norm_stats(eng):
            link = dve_link(eng)
            for t in range(NT):
                ins = eng.bn_aggr(meanvar[:, t, :], stats[:, t, :])
            link(ins)
            for k in range(RMS_OPS):
                link(inverse_root(eng, k, meanvar[:, :, 1], 1.0, LN_EPS, NT, rstd[:, :]))
            eng.sem_clear(chain)

        @block.sync
        def _(sp):
            def load_tiles(i):
                t0, t1 = X_LOADS[i]
                sp.dma_start(X[:, t0:t1, :], x_flat[P * t0:P * t1, :].rearrange("(t p) d -> p t d", p=P)).then_inc(load_x[i], 16)

            def load_heads(w, n, h0, h1, done):
                sp.dma_start(w[:, :, h0 * HD:h1 * HD],
                             a[n][:, h0 * HD:h1 * HD].rearrange("(f p) n -> p f n", p=P)).then_inc(done, 16)

            load_tiles(0)
            sp.dma_start(ident[:, :], a["c_ident"]).then_inc(load_ident, 16)
            sp.dma_start(maskf[:, :, :], a["c_mask"]).then_inc(load_mask, 16)
            load_heads(wk, "L0_attn_Wk", 0, HKV, load_k)
            load_heads(wq, "L0_attn_Wq", 0, 4, load_q[0])
            load_heads(wv, "L0_attn_Wv", 0, HKV, load_v)
            for q in range(1, 4):
                load_heads(wq, "L0_attn_Wq", 4 * q, 4 * q + 4, load_q[q])
            load_tiles(1)
            sp.dma_start(wo_raw, a["L0_attn_Wo"].rearrange("(h p) n -> p h n", p=P)).then_inc(load_o, 16)
            for i in range(2, len(X_LOADS)):
                load_tiles(i)

            def wt(name):
                return a[name].rearrange("(f p) n -> p f n", p=P)
            sp.dma_start(xq_w[:, :, :], wt("wT_q")).then_inc(load_b, 16)
            for i, s in enumerate(("", "_img")):
                sp.dma_start(xkv_w[i][:, :, 0:D], wt(f"wT_k{s}")).then_inc(load_b, 16)
                sp.dma_start(xkv_w[i][:, :, D:2 * D], wt(f"wT_v{s}")).then_inc(load_b, 16)
                sp.dma_start(xkv_b[i][:, 0:D], a[f"L0_xattn_k{s}_b"].partition_broadcast(P)).then_inc(load_b, 16)
                sp.dma_start(xkv_b[i][:, D:2 * D], a[f"L0_xattn_v{s}_b"].partition_broadcast(P)).then_inc(load_b, 16)
            sp.dma_start(xo_w[:, :, :], wt("wT_o")).then_inc(load_b, 16)
            sp.dma_start(xq_b[:, :], a["L0_xattn_q_b"].partition_broadcast(P)).then_inc(load_b, 16)
            sp.dma_start(xo_b[:, :], a["L0_xattn_o_b"].partition_broadcast(P)).then_inc(load_b, 16)
            for i, n in enumerate(("q", "k", "k_img")):
                for f in range(FT):
                    sp.dma_start(norm_w[:, i, f:f + 1],
                                 a[f"L0_xattn_norm_{n}_w"][f * P:(f + 1) * P].unsqueeze(1)).then_inc(load_b, 16)

            c_ = a["ctx_2048"]

            def load_ctx(c):
                cc = c_[bass.ds(c, 1)].rearrange("o k d -> (o k) d")
                sp.dma_start(ctxk[:, 0:MIX, :],
                             cc[N_IMG:N_IMG + MIX * P, :].rearrange("(t p) d -> p t d", p=P)).then_inc(ctx_loaded, 16)
                sp.dma_start(ctxk[0:HALF, MIX, :], cc[N_IMG + MIX * P:NKEY, :]).then_inc(ctx_loaded, 16)
                sp.dma_start(ctxk[HALF:P, MIX, :], cc[0:P - HALF, :]).then_inc(ctx_loaded, 16)
                sp.dma_start(ctxk[:, MIX + 1, :], cc[P - HALF:2 * P - HALF, :]).then_inc(ctx_loaded, 16)
                sp.dma_start(ctxk[0:LAST, MIX + 2, :], cc[2 * P - HALF:N_IMG, :]).then_inc(ctx_loaded, 16)

            def turn(name, b):
                c = b + 1
                events, place = numbered(name, b)
                for e, m, n in events:
                    if e[0] == "ctx":
                        m, n = place[("kt", NCH - 1)]
                        sp.wait_ge(misc_full[m], n + 1)
                        sp.sem_inc(gone_ahead, 1)
                        if name != "near":
                            load_ctx(c + 1)
                    elif e[0] in ("qp", "kq"):
                        g = e[1]
                        sp.wait_ge(split_done, (NCH + 1) * c + 1 if e[0] == "qp" else (NCH + 1) * (c + 1))
                        sp.sem_inc(gone_ahead, 1)
                        if name != "first":
                            sp.wait_ge(st_made, XSTEP * b + KT_TILES * (g + 1))
                            sp.sem_inc(gone_ahead, 1)
                        else:
                            sp.wait_ge(kind_ready, 1)
                        half, r = divmod(g, 2)
                        for i, (pk, pq) in enumerate(PARTS):
                            if e[0] == "kq":
                                sp.dma_start(KS[16 * i:16 * i + 16, g, :, :],
                                             kp[64 * r:64 * r + 64, pk, half, :]).then_inc(kq_loaded[g], 16)
                            if g or e[0] == "qp":
                                sp.dma_start(QS[16 * i:16 * i + 16, g, :, :],
                                             qp[64 * r:64 * r + 64, pq, half, :]).then_inc(kq_loaded[g], 16)
                    elif e[0] == "mpost":
                        g = e[1]
                        sp.wait_ge(mT_ready, NG * b + g + 1)
                        sp.sem_inc(gone_ahead, 1)
                        sp.dma_start(QS[KROWS:KROWS + 2, g % NG, :, :], mT[:, :]).then_inc(m_rows, 16)

            sp.wait_ge(o_split, 2)
            load_ctx(0)
            sp.wait_ge(a_kv_evac, 2 + A_KV_EVAC * B)
            sp.dma_start(kindf, a["c_kind"]).then_inc(load_kind, 16)
            sp.wait_ge(kind_ready, 1)
            sp.wait_ge(zero_rows, 1)
            for g in range(NG):
                for h in range(4):
                    sp.dma_start(KS[KROWS:KROWS + 2, g, h, :], kind).then_inc(kind_rows, 16)
            turn("first", -1)
            turn("head", 0)
            with sp.Fori(1, B - 2) as b:
                turn("body", b)
            turn("near", B - 2)

            for g in range(NG):
                sp.wait_ge(kq_loaded[g], KQ * B)
            sp.wait_ge(split_done, (NCH + 1) * B)
            sp.dma_start(wr[:, :, :], a["L0_ffn_Wr"].rearrange("(f p) n -> p f n", p=P)).then_inc(load_r, 16)
            sp.dma_start(tri[:, :, :], a["c_tri"]).then_inc(load_r, 16)

            def load_expert(e, i):
                for j, n in enumerate(("L0_ffn_Wg", "L0_ffn_Wu", "L0_ffn_Wd")):
                    sp.dma_start(w3[:, i, j, :, :],
                                 a[n][bass.ds(e, 1)].rearrange("o (f p) n -> p (o f) n", p=P)).then_inc(load_w[i], 16)

            load_expert(0, 0)
            load_expert(1, 1)
            turn("foot", B - 1)

            with sp.Fori(1, E // 2) as k:
                for i in range(2):
                    sp.wait_ge(w_lo, 2 * k + i - 1)
                    sp.sem_inc(gone_ahead, 1)
                    load_expert(2 * k + i, i)
            for g in range(TG):
                sp.wait_ge(c_down_evac, 2 + 2 * (TG * (E - 1) + g + 1))
                sp.dma_start(out_flat[512 * g:512 * g + 512, :].rearrange("(t p) d -> p t d", p=P),
                             X[:, 4 * g:4 * g + 4, :]).then_inc(stored, 16)
            sp.wait_ge(stored, 16 * TG)

        @block.tensor
        def _(pe):
            def product(dst, stationary, moving, first, last):
                for k, (s_, m_) in enumerate(((0, 0), (0, 1), (1, 0))):
                    mm = pe.matmul(dst, stationary(s_), moving(m_), start=first and k == 0, stop=last and k == 2)
                return mm

            def turn_x(b):
                pe.wait_ge(xn_ready, b + 1)
                for f in range(FT):
                    for u in range(2):
                        mm = pe.transpose(pair[0][:, 0, f * S + u * P:f * S + (u + 1) * P], XN[:, u, f * P:(f + 1) * P],
                                          ident[:, :])
                mm.then_inc(xt_made, 1)

            pe.wait_ge(load_ident, 16)
            turn_x(0)

            def batch(b, last):
                pe.wait_ge(xt_ready, b + 1)

                def project(dst, w, head):
                    for f in range(FT):
                        mm = pe.matmul(dst, w[:, f, head * HD:(head + 1) * HD], XT[:, f, :],
                                       start=(f == 0), stop=(f == FT - 1))
                    return mm

                def kv_bank(n):
                    if n >= 2:
                        pe.wait_ge(a_kv_evac, A_KV_EVAC * b + a_kv_read(n - 2))
                    else:
                        pe.wait_ge(a_kv_evac, A_KV_EVAC * b + n + 1)
                    return bank[2 + n % 2]

                def kv_heads(k):
                    w = wk if k < 2 else wv
                    pe.wait_ge(load_k if k < 2 else load_v, 16)
                    dst = kv_bank(k)
                    for u in range(2):
                        mm = project(dst[:, u * S:(u + 1) * S], w, 2 * (k % 2) + u)
                    mm.then_inc(a_kv, 1)

                def q_heads(k):
                    pe.wait_ge(load_q[k // 2], 16)
                    pe.wait_ge(a_q_evac, 8 * b + k + 1)
                    for u in range(2):
                        mm = project(bank[k % 2][:, u * S:(u + 1) * S], wq, 2 * k + u)
                    mm.then_inc(a_q, 1)

                def v_turn(t):
                    dst = kv_bank(4 + t)
                    pe.wait_ge(a_kv_evac, A_KV_EVAC * b + a_kv_read(3))
                    for g in range(HKV):
                        mm = pe.transpose(dst[:, g * P:(g + 1) * P], VT[:, g, t * P:(t + 1) * P], ident[:, :])
                    mm.then_inc(a_kv, 1)

                def output(t, heads):
                    if heads[0] == 0:
                        pe.wait_ge(o_split, 2)
                        kv_bank(6 + t)
                        pe.wait_ge(a_o_evac, 2 + NSTEP * b + NSTEP // 2 * (t + 1))
                    for h in heads:
                        mm = product(bank[2 + t][:, 0:D], lambda p: OT[:, p, h, t * P:(t + 1) * P],
                                     lambda p: wo[:, p, h, :], h == 0, h == HQ - 1)
                    if heads[-1] == HQ - 1:
                        mm.then_inc(a_kv, 1)

                def scores(i):
                    blk, j = divmod(i, 2)
                    if i < 2:
                        pe.wait_ge(a_kv_evac, A_KV_EVAC * b + a_kv_read(1))
                        pe.wait_ge(a_q_evac, 2 + 8 * b + 4 * (j + 1))
                    pe.wait_ge(a_exp, NSTEP * b + i + 1)
                    sbank = pair[0][:, i % 2, :]
                    if i == 0:
                        pe.wait_ge(const_ready, 1)
                    pe.matmul(sbank, identb[:, :], mask[:, (0, 1, 2, 1)[blk], :, :], start=True, stop=False,
                              skip_group_check=True)
                    if blk == 2:
                        spans = [(0, 128, 64), (64, 64, 64)]
                    else:
                        spans = [(0, 128 if blk == 3 else 0, 128)]
                    for gg in range(2):
                        g = 2 * j + gg
                        for p2 in range(2):
                            h = 4 * g + 2 * p2
                            for c, k0, n in spans:
                                o = (2 * gg + p2) * P + c
                                mm = pe.matmul(sbank[:, o:o + n], QT[:, blk, h:h + 2, :].rearrange("p h q -> p (h q)"),
                                               KT[:, g, k0:k0 + n], start=False, stop=True, skip_group_check=True)
                    mm.then_inc(a_score, 1)

                def turn_probs(i):
                    pe.wait_ge(a_norm, NSTEP * b + i + 1)
                    pe.wait_ge(a_pt, NSTEP * b + i + 1)
                    for q in range(4):
                        mm = pe.transpose(pair[1][:, i % 2, q * P:(q + 1) * P], PA[:, i % P_RING, q * P:(q + 1) * P],
                                          ident[:, :])
                    mm.then_inc(a_turned, 1)

                def values(i):
                    blk, j = divmod(i, 2)
                    if i == 0:
                        pe.wait_ge(a_kv_evac, A_KV_EVAC * b + a_kv_read(5))
                    pe.wait_ge(a_pt, 2 + NSTEP * b + i + 1)
                    pe.wait_ge(a_o_evac, NSTEP * b + i + 1)
                    for gg in range(2):
                        g = 2 * j + gg
                        mm = pe.matmul(bank[i % 2][:, gg * 256:(gg + 1) * 256], V[:, (0, 0, 2, 1)[blk], g * HD:(g + 1) * HD],
                                       PT[:, i % 2, gg * 256:(gg + 1) * 256], start=True, stop=True)
                    mm.then_inc(a_pv, 1)

                for k in range(4):
                    kv_heads(k)
                    q_heads(k)
                q_heads(4)
                v_turn(0)
                scores(0)
                for k in range(5, 8):
                    q_heads(k)
                v_turn(1)
                for i in range(1, NSTEP + 3):
                    if i < NSTEP:
                        scores(i)
                    if 2 <= i < NSTEP + 2:
                        turn_probs(i - 2)
                    if i == NSTEP:
                        output(0, range(0, 5))
                    if i == NSTEP + 1:
                        output(0, range(5, 10))
                    if i >= 3:
                        values(i - 3)
                output(0, range(10, HQ))
                if not last:
                    pe.wait_ge(a_exp, 2 + NSTEP * b + NSTEP - 1)
                    turn_x(b + 1)
                output(1, range(HQ))

            with pe.Fori(0, B - 1) as b:
                batch(b, False)
            batch(B - 1, True)

            ST, SM, OB = pair, (bank[0], bank[1]), bank[2]
            misc = misc_banks(pair, bank)

            def router(g):
                for f in range(FT):
                    mm = product(pair[g // 2][:, g % 2, :], lambda p: wrp[:, p, f, :],
                                 lambda p: XT3[:, p, f, 512 * g:512 * (g + 1)], f == 0, f == FT - 1)
                if g % 2:
                    mm.then_inc(c_router, 1)

            OBv = OB[:, :].rearrange("p (k q) -> p k q", k=2)
            pe.wait_ge(load_b, 16 * 18)
            pe.wait_ge(b_init, 2)

            def turn(name, b):
                c = b + 1
                events, place = numbered(name, b)
                for e, m, n in events:
                    kind_, arg = e[0], e[1:]
                    MB = misc[m]
                    if kind_ in MISC and not (name == "first" and n == 0):
                        pe.wait_ge(misc_free[m], n)
                    if kind_ == "st":
                        s = arg[0]
                        g, t = divmod(s, KT_TILES)
                        kn = key_count(t)
                        if t == 0:
                            pe.wait_ge(m_rows, 16 * (NG * b + g + 1))
                        pe.wait_ge(exp_done, XSTEP * b + s + 1)
                        for h in range(4):
                            mm = pe.matmul(ST[s % 2][0:kn, h // 2, (h % 2) * S:(h % 2 + 1) * S],
                                           KS[:, g, h, t * P:t * P + kn], QS[:, g, h, :], start=True, stop=True)
                        mm.then_inc(st_made, 1)
                    elif kind_ == "mx":
                        g, u = arg
                        h, r = divmod(u, 8)
                        qt, ch = divmod(r, 4)
                        k0, kn = MAX_CHUNKS[ch]
                        if u == 0:
                            pe.wait_ge(kq_loaded[g % NG], KQ * (b + 1 + g // NG))
                        pe.wait_ge(smax_done, UNITS * (NG * b + g) + u + 1)
                        pe.matmul(SM[u % 2][:, 0:kn], QS[0:KROWS, g % NG, h, qt * P:(qt + 1) * P],
                                  KS[0:KROWS, g % NG, h, k0:k0 + kn], start=True, stop=True).then_inc(smax_made, 1)
                    elif kind_ == "pv":
                        db, s = arg
                        bb = b + db
                        g, t = divmod(s, KT_TILES)
                        kn = key_count(t)
                        pe.wait_ge(exp_done, 2 + XSTEP * bb + s + 1)
                        if g == 0:
                            pe.wait_ge(v_copied, (KT_TILES + 1) * bb + v_slots(t)[-1] + 1)
                        if t == 0:
                            pe.wait_ge(o_evac, 1 + NG * bb + g)
                        for v in v_slots(t):
                            for h in range(4):
                                mm = pe.matmul(OBv[32 * h:32 * h + VW, v // (MIX + 1), :], Vc[0:kn, v, 4 * g + h, :],
                                               PX[0:kn, s % XP_RING, h // 2, (h % 2) * S:(h % 2 + 1) * S],
                                               start=v in (0, MIX + 1), stop=v in (MIX, KT_TILES),
                                               tile_position=(0, 32 * h))
                        mm.then_inc(pv_done, 1)
                    elif kind_ == "otr":
                        bb, g = b + arg[0], arg[1]
                        pe.wait_ge(o_evac, 1 + NG * bb + g + 1)
                        for kd in range(2):
                            for qt in range(2):
                                o = (2 * kd + qt) * P
                                mm = pe.transpose(MB[:, o:o + P], Osb[:, kd, qt * P:(qt + 1) * P], ident[:, :])
                        mm.then_inc(misc_full[m], 1)
                    elif kind_ == "atr":
                        pe.wait_ge(attn_part, NG * b)
                        for f in range(FT):
                            for qt in range(2):
                                o = f * S + qt * P
                                mm = pe.transpose(MB[:, o:o + P], attn[:, qt, f * P:(f + 1) * P], ident[:, :])
                        mm.then_inc(misc_full[m], 1)
                    elif kind_ == "oproj":
                        for qt in range(2):
                            for f in range(FT):
                                mm = pe.matmul(MB[:, qt * D:(qt + 1) * D], attnT[:, f, qt * P:(qt + 1) * P], xo_w[:, f, :],
                                               start=(f == 0), stop=(f == FT - 1))
                        mm.then_inc(misc_full[m], 1)
                    elif kind_ == "mpost":
                        pe.wait_ge(mneg_ready, NG * b + arg[0] + 1)
                        for qt in range(2):
                            mm = pe.transpose(MB[0:8, qt * P:(qt + 1) * P], mneg[:, qt, :], ident[:, :])
                        mm.then_inc(misc_full[m], 1)
                    elif kind_ == "cT":
                        p = arg[0]
                        if p == B - 1:
                            pe.wait_ge(wr_split, 2)
                            for g in range(TG - 1):
                                router(g)
                        pe.wait_ge(xn_ready, NT // 2 + p + 1)
                        for f in range(FT):
                            for u in range(2):
                                o = f * S + u * P
                                mm = pe.transpose(MB[:, o:o + P], XN3[:, 2 * p + u, f * P:(f + 1) * P], ident[:, :])
                        mm.then_inc(misc_full[m], 1)
                    elif kind_ == "xT":
                        pe.wait_ge(b_xn, b + arg[0] + 1)
                        for f in range(FT):
                            for u in range(2):
                                o = f * S + u * P
                                mm = pe.transpose(MB[:, o:o + P], xn[:, u, f * P:(f + 1) * P], ident[:, :])
                        mm.then_inc(misc_full[m], 1)
                    elif kind_ == "q":
                        if name == "first":
                            mx, n_xt = place[("xT", arg[0])]
                            pe.wait_ge(misc_free[mx], n_xt + 1)
                        for u in range(2):
                            for f in range(FT):
                                mm = pe.matmul(MB[:, u * D:(u + 1) * D], xT[:, f, u * P:(u + 1) * P], xq_w[:, f, :],
                                               start=(f == 0), stop=(f == FT - 1))
                        mm.then_inc(misc_full[m], 1)
                    elif kind_ == "ct":
                        j = arg[1]
                        if j == 0:
                            pe.wait_ge(ctx_loaded, 80 * (b + arg[0] + 1))
                        for f in range(FT):
                            for i, t in enumerate(range(*CHUNKS[j])):
                                kn = key_count(t)
                                o = f * 2 * P + i * P
                                mm = pe.transpose(MB[:, o:o + kn], ctxk[0:kn, t, f * P:(f + 1) * P],
                                                  ident[0:kn, 0:kn])
                        mm.then_inc(misc_full[m], 1)
                    elif kind_ == "kv":
                        t = arg[1]
                        j, i0 = chunk_of(t)
                        if name == "first":
                            mc, n_ct = place[("ct", arg[0], j)]
                            pe.wait_ge(misc_free[mc], n_ct + 1)
                        for i, r0, r1 in kinds_of(t):
                            for f in range(FT):
                                mm = pe.matmul(MB[r0:r1, :], ctxT[:, j % 2, f, i0 * P + r0:i0 * P + r1], xkv_w[i][:, f, :],
                                               start=(f == 0), stop=(f == FT - 1))
                        mm.then_inc(misc_full[m], 1)
                    elif kind_ == "qt":
                        pe.wait_ge(scaled, (NCH + 1) * c + 1)
                        for f in range(FT):
                            for u in range(2):
                                o = f * S + u * P
                                mm = pe.transpose(MB[:, o:o + P], qraw[:, u, f * P:(f + 1) * P], ident[:, :])
                        mm.then_inc(misc_full[m], 1)
                    elif kind_ == "kt":
                        j = arg[0]
                        pe.wait_ge(scaled, (NCH + 1) * c + j + 2)
                        t0, t1 = CHUNKS[j]
                        for f in range(FT):
                            for t in range(t0, t1):
                                kn = key_count(t)
                                o = f * 256 + (t - t0) * P
                                mm = pe.transpose(MB[:, o:o + kn], ctxk[0:kn, t, f * P:(f + 1) * P], ident[0:kn, 0:kn])
                        mm.then_inc(misc_full[m], 1)

            turn("first", -1)
            for i in range(1, MISC_BANKS):
                pe.wait_ge(misc_free[i], FIRST_COUNT[i])
            pe.wait_ge(kind_rows, 16 * NH)
            turn("head", 0)
            with pe.Fori(1, B - 2) as b:
                turn("body", b)
            turn("near", B - 2)
            turn("foot", B - 1)
            turn("last", B)

            pe.wait_ge(misc_free[0], sum(MISC_COUNT[name] for name in TURNS) + (B - 4) * MISC_COUNT["body"])
            router(TG - 1)
            for t in range(NT):
                if t % (NT // 2) == 0:
                    pe.wait_ge(c_router_evac, 2 * t // NT + 1)
                mm = pe.transpose(bank[2][:, t * E:(t + 1) * E], logitT[:, t * P:(t + 1) * P], ident[0:E, 0:E])
            mm.then_inc(c_logit, 1)

            def gate_up(i, e, g):
                n = TG * e + g
                for m in range(FT):
                    pe.wait_ge(c_h, 2 * n + m + 1)
                    for j in range(2):
                        for f in range(FT):
                            mm = product(pair[m][:, j, :], lambda p: w3p[:, i, p, j, f, m * P:(m + 1) * P],
                                         lambda p: XT3[:, p, f, 512 * g:512 * (g + 1)], f == 0, f == FT - 1)
                    mm.then_inc(c_gu, 1)

            def down(i, e, g):
                n = TG * e + g
                pe.wait_ge(c_hlo, 2 + 2 * n + 2)
                for u in range(2):
                    pe.wait_ge(c_down_evac, 2 * n + u + 1)
                    for t in range(2):
                        for m in range(FT):
                            o = (2 * u + t) * P
                            mm = product(bank[u][:, t * D:(t + 1) * D], lambda p: hT[:, g % 2, p, m, o:o + P],
                                         lambda p: w3p[:, i, p, 2, m, :], m == 0, m == FT - 1)
                    mm.then_inc(c_down, 1)

            with pe.Fori(0, E, 2) as e2:
                for i in range(2):
                    e = e2 + i
                    pe.wait_ge(w_lo, e + 1)
                    gate_up(i, e, 0)
                    for g in range(TG):
                        if g + 1 < TG:
                            gate_up(i, e, g + 1)
                        down(i, e, g)

        @block.scalar
        def _(act):
            act.sem_inc(a_q_evac, 2)
            act.sem_inc(a_exp, 2)
            act.sem_inc(a_pt, 2)

            def move_x(b):
                act.wait_ge(xt_made, b + 1)
                act.activation(XT[:, :, :], pair[0][:, 0, :].rearrange("p (f n) -> p f n", f=FT), ACT.Copy).then_inc(xt_ready, 1)

            move_x(0)

            def batch(b, last):
                def move_q(k):
                    act.wait_ge(a_q, 8 * b + k + 1)
                    act.activation(QT[:, :, 2 * k:2 * k + 2, :].rearrange("p b h q -> p h b q"),
                                   bank[k % 2][:, :].rearrange("p (h b q) -> p h b q", h=2, b=NBLK),
                                   ACT.Copy).then_inc(a_q_evac, 1)

                for k in range(5):
                    move_q(k)
                for i in range(NSTEP + 2):
                    if i < NSTEP:
                        act.wait_ge(a_negmax, NSTEP * b + i + 1)
                        act.wait_ge(a_turned, NSTEP * b + i + 1)
                        for q in range(4):
                            ins = act.activation(PA[:, i % P_RING, q * P:(q + 1) * P], pair[0][:, i % 2, q * P:(q + 1) * P],
                                                 ACT.Exp, bias=negmax[:, i % P_RING, q:q + 1], scale=1.0 / HD,
                                                 accum_out=rowsum[:, i % P_RING, q:q + 1])
                        ins.then_inc(a_exp, 1)
                    if i == 0:
                        for k in range(5, 8):
                            move_q(k)
                    if i >= 2:
                        k = i - 2
                        act.wait_ge(a_turned, P_RING + NSTEP * b + k + 1)
                        act.wait_ge(a_pv, NSTEP * b + k + 1)
                        act.activation(PT[:, k % 2, :], pair[1][:, k % 2, :], ACT.Copy).then_inc(a_pt, 1)

                if not last:
                    move_x(b + 1)

            with act.Fori(0, B - 1) as b:
                batch(b, False)
            batch(B - 1, True)

            def split(e, i):
                act.wait_ge(load_w[i], 24 * (e - i) + 48)
                act.activation(w3p[:, i, 0, :, :, :], w3[:, i, :, :, :], ACT.Copy).then_inc(w_hi, 1)

            ST, OB = pair, bank[2]
            misc = misc_banks(pair, bank)
            act.sem_inc(exp_done, 2)
            act.sem_inc(o_evac, 1)
            act.wait_ge(a_kv_evac, 2 + A_KV_EVAC * B)
            act.wait_ge(b_init, 2)
            act.wait_ge(load_b, 16 * 18)

            def turn(name, b):
                c = b + 1
                events, place = numbered(name, b)
                rows_made = {("sq",) + q[1:]: place[e] for e in place if e[0] in ("q", "kv") for q in squares(e)}
                for e, m, n in events:
                    kind_, arg = e[0], e[1:]
                    MB3 = misc[m].rearrange("p (f n) -> p f n", f=FT)
                    if kind_ == "st":
                        s = arg[0]
                        kn = key_count(s % KT_TILES)
                        act.wait_ge(st_made, XSTEP * b + s + 1)
                        act.wait_ge(pv_done, XSTEP * b + s + 1)
                        act.activation(PX[0:kn, s % XP_RING, :, :], ST[s % 2][0:kn, :, :], ACT.Exp,
                                       scale=float(XD) ** -0.5).then_inc(exp_done, 1)
                    elif kind_ == "cT":
                        p = arg[0]
                        if p == 0:
                            act.wait_ge(split_done, (NCH + 1) * B)
                            for g in range(NG):
                                act.wait_ge(kq_loaded[g], KQ * B)
                        if p == B - 1:
                            act.wait_ge(x_added, B)
                            act.wait_ge(load_r, 32)
                            act.wait_ge(wr_zeros, 1)
                            act.activation(wrp[:, 0, :, 0:E], wr[:, :, :], ACT.Copy).then_inc(wr_split, 1)
                            split(0, 0)
                        act.wait_ge(misc_full[m], n + 1)
                        act.activation(XT3[:, 0, :, 256 * p:256 * (p + 1)], MB3, ACT.Copy).then_inc(c_xhi, 1)
                    elif kind_ == "kinds":
                        act.wait_ge(load_kind, 16)
                        act.activation(kind, kindf, ACT.Copy).then_inc(kind_ready, 1)
                    elif kind_ == "oev":
                        bb, g = b + arg[0], arg[1]
                        act.wait_ge(pv_done, XP_RING + XSTEP * bb + KT_TILES * (g + 1))
                        act.wait_ge(attn_part, NG * bb + g)
                        act.activation(Osb[:, :, :], OB[:, :].rearrange("p (k q) -> p k q", k=2), ACT.Copy)\
                           .then_inc(o_evac, 1)
                    elif kind_ in ("xT", "atr"):
                        act.wait_ge(misc_full[m], n + 1)
                        act.activation((xT if kind_ == "xT" else attnT)[:, :, :], MB3, ACT.Copy).then_inc(misc_free[m], 1)
                    elif kind_ == "ct":
                        j = arg[1]
                        kn = min(CHUNKS[j][1] * P, NKEY) - CHUNKS[j][0] * P
                        act.wait_ge(misc_full[m], n + 1)
                        act.activation(ctxT[:, j % 2, :, 0:kn], MB3[:, :, 0:kn], ACT.Copy).then_inc(misc_free[m], 1)
                    elif kind_ in ("qt", "kt"):
                        act.wait_ge(misc_full[m], n + 1)
                        if kind_ == "qt":
                            if name != "first":
                                act.wait_ge(split_done, (NCH + 1) * c)
                            segs = [(0, 0, S)]
                            k0, dst, part = 0, qw, qp
                            for g in range(NG):
                                act.wait_ge(kq_loaded[g], KQ * c)
                        else:
                            j = arg[0]
                            k0 = CHUNKS[j][0] * P
                            k1 = min(CHUNKS[j][1] * P, NKEY)
                            segs = [(1, k0, min(k1, N_TXT))] if k0 < N_TXT else []
                            segs += [(2, max(k0, N_TXT), k1)] if k1 > N_TXT else []
                            act.wait_ge(split_done, (NCH + 1) * c + (j + 2 - KW_RING if j >= KW_RING else 0))
                            dst, part = kw[:, j % KW_RING, :, :], kp
                        todo = [(w, s0, s1, f, o) for w, s0, s1 in segs for f in range(FT) for o in range(2)]
                        for w, s0, s1, f, o in todo:
                            to = dst[:, f, s0 - k0:s1 - k0] if o == 0 else part[:, 0, f, s0:s1]
                            ins = act.activation(to, MB3[:, f, s0 - k0:s1 - k0], ACT.Copy, scale=norm_w[:, w, f:f + 1])
                        ins.then_inc(misc_free[m], 1)
                    elif kind_ == "k2":
                        j = arg[0]
                        act.wait_ge(r1_done, (NCH + 1) * c + j + 1)
                        if j == 0:
                            act.activation(qp[:, 1, :, :], qw[:, :, :], ACT.Copy).then_inc(k2_done, 1)
                        else:
                            k0 = CHUNKS[j - 1][0] * P
                            k1 = min(CHUNKS[j - 1][1] * P, NKEY)
                            act.activation(kp[:, 1, :, k0:k1], kw[:, (j - 1) % KW_RING, :, 0:k1 - k0], ACT.Copy).then_inc(k2_done, 1)
                    if kind_ == "sq":
                        t = arg[1]
                        kn = P if t >= KT_TILES else key_count(t)
                        src = qraw[:, t - KT_TILES, :] if t >= KT_TILES else ctxk[0:kn, t, :]
                        m, n = rows_made[e]
                        act.wait_ge(misc_free[m], n + 1)
                        act.wait_ge(sq_done, (KT_TILES + 2) * (b + arg[0]) + (t - KT_TILES if t >= KT_TILES else t + 2))
                        act.activation(junk[0:kn, :], src, ACT.Square, accum_out=sumsq[0:kn, t:t + 1])\
                           .then_inc(sq_done, 1)
                    elif kind_ == "vc":
                        cb, t = b + arg[0], arg[1]
                        if name == "first" and t == 0:
                            act.wait_ge(v_init, 3)
                        if not (name in ("first", "head") and cb in (0,)):
                            act.wait_ge(pv_done, XP_RING + XSTEP * (cb - 1) + (NG - 1) * KT_TILES + t + 1)
                        for v, (i, r0, r1) in zip(v_slots(t), kinds_of(t)):
                            act.activation(Vc[r0:r1, v, :, 0:XD], Vn[r0:r1, t, :].rearrange("p (h d) -> p h d", d=XD),
                                           ACT.Copy).then_inc(v_copied, 1)

            turn("first", -1)
            turn("head", 0)
            with act.Fori(1, B - 2) as b:
                turn("body", b)
            turn("near", B - 2)
            turn("foot", B - 1)
            turn("last", B)

            act.wait_ge(x_added, B)
            for i in range(2):
                act.wait_ge(c_router, i + 1)
                act.activation(logitT[:, 1024 * i:1024 * (i + 1)], pair[i][0:E, :, :].rearrange("p a n -> p (a n)"),
                               ACT.Copy).then_inc(c_router_evac, 1)
            act.wait_ge(c_shift, 1)
            act.activation(prob[:, :, :], logit[:, :, :], ACT.Exp).then_inc(c_exp, 1)

            def experts(e2, last):
                for i in range(2):
                    e = e2 + i
                    for g in range(TG):
                        n = TG * e + g
                        for m in range(FT):
                            act.wait_ge(c_gu, 2 * n + m + 1)
                            act.wait_ge(c_h, 2 * n + m + 1)
                            act.activation(silu[:, m, :], pair[m][:, 0, :], ACT.Silu).then_inc(c_silu, 1)
                            if g == 0 and m == 0 and not (last and i):
                                split(e + 1, 1 - i)
                            act.wait_ge(c_h, 2 + 2 * n + m + 1)
                            act.activation(hT[:, g % 2, 0, m, :], hf[:, m, :], ACT.Copy).then_inc(c_hhi, 1)

            with act.Fori(0, E - 2, 2) as e2:
                experts(e2, False)
            experts(E - 2, True)

        @block.vector
        def _(dve):
            dve.sem_inc(a_kv_evac, 2)
            dve.sem_inc(a_o_evac, 2)

            def norm_x(b, link):
                for u in range(2):
                    xv = X[:, bass.ds(2 * b + u, 1), :].rearrange("p o d -> p (o d)")
                    ins = dve.bn_stats(XS[:, u, :], xv)
                link(ins)
                for u in range(2):
                    ins = dve.bn_aggr(XMV[:, u, :], XS[:, u, :])
                link(ins)
                for k in range(RMS_OPS):
                    link(inverse_root(dve, k, XMV[:, :, 1], 1.0, LN_EPS, 2, XR[:, :]))
                for u in range(2):
                    xv = X[:, bass.ds(2 * b + u, 1), :].rearrange("p o d -> p (o d)")
                    ins = dve.tensor_scalar(XN[:, u, :], xv, XMV[:, u, 0:1], XR[:, u:u + 1], ALU.subtract, ALU.mult)
                ins.then_inc(xn_ready, 1)

            dve.wait_ge(load_x[0], 16)
            norm_x(0, dve_link(dve))
            dve.sem_clear(chain)
            dve.wait_ge(load_ident, 16)
            dve.wait_ge(load_mask, 16)
            dve.tensor_copy(identb[:, :], ident[:, :])
            for m in range(4):
                ins = dve.tensor_copy(mask[:, :, m, :], maskf[:, :, :])
            ins.then_inc(const_ready, 1)


            def batch(b, last):
                link = dve_link(dve)

                for k in range(4):
                    dve.wait_ge(a_kv, A_KV * b + k + 1)
                    dve.tensor_copy((KT if k < 2 else VT)[:, 2 * (k % 2):2 * (k % 2) + 2, :],
                                    bank[2 + k % 2][:, :].rearrange("p (h n) -> p h n", h=2)).then_inc(a_kv_evac, 1)

                def move_v(t):
                    dve.wait_ge(a_kv, A_KV * b + 5 + t)
                    dve.tensor_copy(V[:, t, :], bank[2 + t][:, :]).then_inc(a_kv_evac, 1)
                    lo, hi = (64, 128) if t == 0 else (0, 64)
                    dve.tensor_copy(V[lo:hi, 2, :], bank[2 + t][lo:hi, :]).then_inc(a_kv_evac, 1)

                def add_output(t):
                    dve.wait_ge(a_kv, A_KV * b + 7 + t)
                    xv = X[:, bass.ds(2 * b + t, 1), :].rearrange("p o d -> p (o d)")
                    dve.tensor_tensor(xv, xv, bank[2 + t][:, 0:D], ALU.add).then_inc(a_kv_evac, 1)
                    dve.wait_ge(a_kv_evac, A_KV_EVAC * b + a_kv_read(6 + t))
                    link(dve.bn_stats(stats[:, bass.ds(2 * b + t, 1), :].rearrange("p o s -> p (o s)"), xv))

                move_v(0)
                for i in range(NSTEP + 3):
                    if i < NSTEP:
                        r = i % P_RING
                        dve.wait_ge(a_score, NSTEP * b + i + 1)
                        link(dve.tensor_reduce(rowmax[:, r, :], pair[0][:, i % 2, :].rearrange("p (q k) -> p q k", q=4),
                                               X_AXIS, ALU.max))
                        dve.tensor_scalar(negmax[:, r, :], rowmax[:, r, :], -1.0 / HD, None, ALU.mult).then_inc(a_negmax, 1)
                    if i == 0:
                        if not last:
                            for q in range(1, len(X_LOADS)):
                                dve.wait_ge(load_x[q], 16)
                            norm_x(b + 1, link)
                        move_v(1)
                    if 1 <= i < NSTEP + 1:
                        r = (i - 1) % P_RING
                        dve.wait_ge(a_exp, 2 + NSTEP * b + i)
                        link(dve.reciprocal(rowinv[:, r, :], rowsum[:, r, :]))
                        pv = PA[:, r, :].rearrange("p (q k) -> p q k", q=4)
                        dve.tensor_tensor(pv, pv, rowinv[:, r, :].unsqueeze(2).to_broadcast([P, 4, P]), ALU.mult)\
                           .then_inc(a_norm, 1)
                    if i >= 3:
                        k = i - 3
                        blk, j = divmod(k, 2)
                        dve.wait_ge(a_pv, 2 + NSTEP * b + k + 1)
                        heads, tokens = slice(8 * j, 8 * j + 8), slice(blk * WIN, (blk + 1) * WIN)
                        ov = bank[k % 2][:, :].rearrange("p (h n) -> p h n", h=8)
                        link(dve.tensor_copy(OT[:, 0, heads, tokens], ov))
                        dve.tensor_tensor(OT[:, 1, heads, tokens], ov, OT[:, 0, heads, tokens].bitcast(F32), ALU.subtract)\
                           .then_inc(a_o_evac, 1)
                for t in range(2):
                    add_output(t)
                dve.sem_clear(chain)

            with dve.Fori(0, B - 1) as b:
                batch(b, False)
            batch(B - 1, True)

            SM, OB = (bank[0], bank[1]), bank[2]
            misc = misc_banks(pair, bank)
            dve.sem_inc(smax_done, 2)
            dve.wait_ge(a_kv_evac, 2 + A_KV_EVAC * B)
            dve.memset(sumsq[:, :], 1.0).then_inc(b_init, 1)
            dve.memset(OB[:, :], 0.0).then_inc(b_init, 1)
            dve.wait_ge(b_init, 2)
            norm_stats(dve)
            dve.wait_ge(load_b, 16 * 18)

            def turn(name, b):
                c = b + 1
                events, place = numbered(name, b)
                link = dve_link(dve)
                for e, m, n in events:
                    kind_, arg = e[0], e[1:]
                    MB, MB2 = misc[m], misc[m].rearrange("p (u n) -> p u n", u=2)
                    if kind_ == "mx":
                        g, u = arg
                        h, r = divmod(u, 8)
                        qt, ch = divmod(r, 4)
                        dve.wait_ge(smax_made, UNITS * (NG * b + g) + u + 1)
                        dve.tensor_reduce(xmax[:, qt, h, ch:ch + 1], SM[u % 2][:, 0:MAX_CHUNKS[ch][1]], X_AXIS, ALU.max)\
                           .then_inc(smax_done, 1)
                    elif kind_ == "mred":
                        g = arg[0]
                        dve.wait_ge(smax_done, 2 + UNITS * (NG * b + g + 1))
                        dve.tensor_reduce(m8[:, :, 0, :], xmax[:, :, :, 0:3], X_AXIS, ALU.max)
                        link(dve.tensor_copy(m8[:, :, 1, :], xmax[:, :, :, 3]))
                        dve.tensor_scalar(mneg[:, :, :], m8[:, :, :, :].rearrange("p a k h -> p a (k h)"), -1.0, None,
                                          ALU.mult).then_inc(mneg_ready, 1)
                    elif kind_ == "mpost":
                        dve.wait_ge(misc_full[m], n + 1)
                        dve.wait_ge(m_rows, 16 * (NG * b + arg[0]))
                        dve.tensor_copy(mT[:, :], MB[0:8, 0:S]).then_inc(misc_free[m], 1)
                        dve.wait_ge(misc_free[m], n + 1)
                        dve.sem_inc(mT_ready, 1)
                    elif kind_ == "otr":
                        bb, g = b + arg[0], arg[1]
                        dve.wait_ge(misc_full[m], n + 1)
                        ov = MB[:, :].rearrange("p (k q h d) -> p k q h d", k=2, q=2, h=4)
                        link(dve.reciprocal(oinv[:, :, :, :], ov[:, :, :, :, XD]))
                        for kd in range(2):
                            ins = dve.tensor_tensor(otmp[:, kd, :, :].rearrange("p q (h d) -> p q h d", h=4),
                                                    ov[:, kd, :, :, 0:XD],
                                                    oinv[:, kd, :, :].unsqueeze(3).to_broadcast([P, 2, 4, XD]), ALU.mult)
                        ins.then_inc(misc_free[m], 1)
                        dve.wait_ge(misc_free[m], n + 1)
                        dve.tensor_tensor(attn[:, :, 64 * g:64 * g + 64], otmp[:, 0, :, :], otmp[:, 1, :, :], ALU.add)\
                           .then_inc(attn_part, 1)
                    elif kind_ == "oproj":
                        dve.wait_ge(misc_full[m], n + 1)
                        dve.tensor_tensor(oproj[:, :, :], MB2, xo_b[:, :].unsqueeze(1).to_broadcast([P, 2, D]), ALU.add)\
                           .then_inc(misc_free[m], 1)
                        dve.wait_ge(misc_free[m], n + 1)
                        xv = X[:, bass.ds(2 * (b - 1), 2), :]
                        dve.tensor_tensor(xv, xv, oproj[:, :, :], ALU.add).then_inc(x_added, 1)
                    elif kind_ == "cs":
                        dve.wait_ge(x_added, arg[0] + 1)
                        for t in (2 * arg[0], 2 * arg[0] + 1):
                            ins = dve.bn_stats(stats[:, t, :], X[:, t, :])
                        link(ins)
                    elif kind_ == "ca":
                        for t in range(*arg):
                            ins = dve.bn_aggr(meanvar[:, t, :], stats[:, t, :])
                        link(ins)
                    elif kind_ == "cr":
                        t0, t1, k = arg
                        link(inverse_root(dve, k, meanvar[:, t0:t1, 1], 1.0, LN_EPS, t1 - t0, rstd[:, t0:t1]))
                    elif kind_ == "cw":
                        if arg[0] == 0:
                            dve.wait_ge(v_copied, (KT_TILES + 1) * B)
                        for t in (2 * arg[0], 2 * arg[0] + 1):
                            ins = dve.tensor_scalar(XN3[:, t, :], X[:, t, :], meanvar[:, t, 0:1], rstd[:, t:t + 1],
                                                    ALU.subtract, ALU.mult)
                        ins.then_inc(xn_ready, 1)
                    elif kind_ == "cT":
                        p = arg[0]
                        dve.wait_ge(c_xhi, p + 1)
                        dve.tensor_tensor(XT3[:, 1, :, 256 * p:256 * (p + 1)], MB.rearrange("p (f n) -> p f n", f=FT),
                                          XT3[:, 0, :, 256 * p:256 * (p + 1)].bitcast(F32), ALU.subtract)\
                           .then_inc(misc_free[m], 1)
                    elif kind_ == "ln":
                        c2 = b + arg[0]
                        if arg[0] == 2:
                            m, n = place[("qt",)]
                            dve.wait_ge(misc_full[m], n + 1)
                        for u in range(2):
                            ins = dve.tensor_scalar(xn[:, u, :], X[:, bass.ds(2 * c2 + u, 1), :].rearrange("p o d -> p (o d)"),
                                                    meanvar[:, bass.ds(2 * c2 + u, 1), 0:1].rearrange("p o d -> p (o d)"),
                                                    rstd[:, bass.ds(2 * c2 + u, 1)], ALU.subtract, ALU.mult)
                        ins.then_inc(b_xn, 1)
                    elif kind_ == "q":
                        dve.wait_ge(misc_full[m], n + 1)
                        dve.tensor_tensor(qraw[:, :, :], MB2, xq_b[:, :].unsqueeze(1).to_broadcast([P, 2, D]), ALU.add)\
                           .then_inc(misc_free[m], 1)
                    elif kind_ == "kv":
                        t = arg[1]
                        dve.wait_ge(misc_full[m], n + 1)
                        if not (name == "first" and arg[0] == 1):
                            dve.wait_ge(v_copied, (KT_TILES + 1) * (b + arg[0] - 1) + v_slots(t)[-1] + 1)
                        for i, r0, r1 in kinds_of(t):
                            ins = dve.tensor_tensor(kv[r0:r1, t, :], MB[r0:r1, :], xkv_b[i][r0:r1, :], ALU.add)
                        ins.then_inc(misc_free[m], 1)
                    elif kind_ == "rms":
                        if arg[0] == 0:
                            dve.wait_ge(sq_done, (KT_TILES + 2) * (c + 1))
                        else:
                            dve.wait_ge(rms_step, RMS_OPS * c + arg[0])
                        inverse_root(dve, arg[0], sumsq[:, :], 1.0 / D, RMS_EPS, KT_TILES + 2, kq_rstd[:, :])\
                            .then_inc(rms_step, 1)
                    elif kind_ == "sc":
                        j = arg[0]
                        dve.wait_ge(rms_step, RMS_OPS * (c + 1))
                        if j == 0:
                            for u in range(2):
                                ins = dve.tensor_scalar(qraw[:, u, :], qraw[:, u, :], kq_rstd[:, KT_TILES + u:KT_TILES + u + 1],
                                                        None, ALU.mult)
                        else:
                            for t in range(*CHUNKS[j - 1]):
                                kn = key_count(t)
                                ins = dve.tensor_scalar(ctxk[0:kn, t, :], ctxk[0:kn, t, :], kq_rstd[0:kn, t:t + 1], None,
                                                        ALU.mult)
                        ins.then_inc(scaled, 1)
                dve.sem_clear(chain)

            turn("first", -1)
            turn("head", 0)
            with dve.Fori(1, B - 2) as b:
                turn("body", b)
            turn("near", B - 2)
            turn("foot", B - 1)
            turn("last", B)

            dve.sem_inc(c_h, 2)
            dve.sem_inc(c_down_evac, 2)
            dve.wait_ge(x_added, B)
            link = dve_link(dve)
            dve.wait_ge(c_logit, 1)
            lv = bank[2][:, 0:NT * E].rearrange("p (t e) -> p t e", e=E)
            link(dve.tensor_reduce(top[:, :], lv, X_AXIS, ALU.max))
            dve.tensor_tensor(logit[:, :, :], lv, top[:, :].unsqueeze(2).to_broadcast([P, NT, E]), ALU.subtract)\
               .then_inc(c_shift, 1)
            def hidden(e, g):
                n = TG * e + g
                for m in range(FT):
                    dve.wait_ge(c_silu, 2 * n + m + 1)
                    dve.wait_ge(c_hlo, 2 * n + m + 1)
                    dve.tensor_tensor(hf[:, m, :], silu[:, m, :], pair[m][:, 1, :], ALU.mult).then_inc(c_h, 1)

            def add(e, g):
                n = TG * e + g
                for u in range(2):
                    dve.wait_ge(c_down, 2 * n + u + 1)
                    for t in range(2):
                        tile = 4 * g + 2 * u + t
                        ins = dve.scalar_tensor_tensor(out=X[:, tile, :], in0=bank[u][:, t * D:(t + 1) * D],
                                                       scalar=gate[:, tile, bass.ds(e, 1)], in1=X[:, tile, :],
                                                       op0=ALU.mult, op1=ALU.add)
                    ins.then_inc(c_down_evac, 1)

            hidden(0, 0)
            dve.wait_ge(c_exp, 1)
            dve.wait_ge(load_r, 32)
            pj = prob[:, :, :].unsqueeze(2).to_broadcast([P, NT, E, E])
            pi = prob[:, :, :].unsqueeze(3).to_broadcast([P, NT, E, E])
            dve.tensor_tensor(beats[:, :, :, :], pj, pi, ALU.is_gt)
            link(dve.tensor_tensor(ties[:, :, :, :], pj, pi, ALU.is_equal))
            link(dve.tensor_tensor(ties[:, :, :, :], ties[:, :, :, :],
                                   tri[:, :, :].unsqueeze(1).to_broadcast([P, NT, E, E]), ALU.mult))
            link(dve.tensor_tensor(beats[:, :, :, :], beats[:, :, :, :], ties[:, :, :, :], ALU.add))
            link(dve.tensor_reduce(rank[:, :, :], beats[:, :, :, :], X_AXIS, ALU.add))
            link(dve.scalar_tensor_tensor(out=gate[:, :, :], in0=rank[:, :, :], scalar=1.5, in1=prob[:, :, :],
                                          op0=ALU.is_lt, op1=ALU.mult))
            link(dve.tensor_reduce(topsum[:, :], gate[:, :, :], X_AXIS, ALU.add))
            link(dve.reciprocal(top[:, :], topsum[:, :]))
            link(dve.tensor_tensor(gate[:, :, :], gate[:, :, :], top[:, :].unsqueeze(2).to_broadcast([P, NT, E]), ALU.mult))
            dve.sem_clear(chain)

            def expert(e, last):
                for g in range(TG):
                    if g + 1 < TG:
                        hidden(e, g + 1)
                    elif not last:
                        hidden(e + 1, 0)
                    add(e, g)

            with dve.Fori(0, E - 1) as e:
                expert(e, False)
            expert(E - 1, True)

        @block.gpsimd
        def _(pool):
            pool.sem_inc(a_turned, P_RING)
            pool.sem_inc(a_pv, 2)
            pool.sem_inc(pv_done, XP_RING)

            pool.wait_ge(load_o, 16)
            pool.tensor_copy(wo[:, 0, :, :], wo_raw).then_inc(o_split, 1)
            pool.wait_ge(o_split, 1)
            pool.tensor_tensor(wo[:, 1, :, :], wo_raw, wo[:, 0, :, :].bitcast(F32), ALU.subtract).then_inc(o_split, 1)

            def turn(name, b):
                c = b + 1
                events, place = numbered(name, b)
                for e, m, n in events:
                    kind_, arg = e[0], e[1:]
                    if kind_ in ("qt", "kt"):
                        pool.wait_ge(misc_free[m], n + 1)
                        if kind_ == "qt":
                            pool.tensor_tensor(qw[:, :, :], qw[:, :, :], qp[:, 0, :, :], ALU.subtract).then_inc(r1_done, 1)
                        else:
                            j = arg[0]
                            k0 = CHUNKS[j][0] * P
                            k1 = min(CHUNKS[j][1] * P, NKEY)
                            kv = kw[:, j % KW_RING, :, 0:k1 - k0]
                            pool.tensor_tensor(kv, kv, kp[:, 0, :, k0:k1], ALU.subtract).then_inc(r1_done, 1)
                    elif kind_ == "k2":
                        j = arg[0]
                        pool.wait_ge(k2_done, (NCH + 1) * c + j + 1)
                        if j == 0:
                            pool.tensor_tensor(qp[:, 2, :, :], qw[:, :, :], qp[:, 1, :, :], ALU.subtract).then_inc(split_done, 1)
                        else:
                            k0 = CHUNKS[j - 1][0] * P
                            k1 = min(CHUNKS[j - 1][1] * P, NKEY)
                            pool.tensor_tensor(kp[:, 2, :, k0:k1], kw[:, (j - 1) % KW_RING, :, 0:k1 - k0], kp[:, 1, :, k0:k1],
                                               ALU.subtract).then_inc(split_done, 1)

            pool.wait_ge(a_kv_evac, 2 + A_KV_EVAC * B)
            pool.memset(KS[96:P, :, :, :], 0.0)
            pool.memset(QS[96:P, :, :, :], 0.0).then_inc(zero_rows, 1)
            pool.wait_ge(zero_rows, 1)
            pool.memset(Vc[:, :, :, :], 1.0).then_inc(v_init, 1)
            pool.wait_ge(v_init, 1)
            pool.memset(Vc[HALF:P, MIX, :, :], 0.0).then_inc(v_init, 1)
            pool.wait_ge(v_init, 2)
            pool.memset(Vc[0:HALF, MIX + 1, :, :], 0.0).then_inc(v_init, 1)
            turn("first", -1)
            turn("head", 0)
            with pool.Fori(1, B - 2) as b:
                turn("body", b)
            turn("near", B - 2)
            turn("foot", B - 1)

            def split(e, i):
                pool.wait_ge(w_hi, e + 1)
                pool.tensor_tensor(w3p[:, i, 1, :, :, :], w3[:, i, :, :, :], w3p[:, i, 0, :, :, :].bitcast(F32),
                                   ALU.subtract).then_inc(w_lo, 1)

            def experts(e2, last):
                for i in range(2):
                    e = e2 + i
                    for g in range(TG):
                        n = TG * e + g
                        for m in range(FT):
                            pool.wait_ge(c_hhi, 2 * n + m + 1)
                            pool.tensor_tensor(hT[:, g % 2, 1, m, :], hf[:, m, :], hT[:, g % 2, 0, m, :].bitcast(F32),
                                               ALU.subtract).then_inc(c_hlo, 1)
                        if g == 1 and not (last and i):
                            split(e + 1, 1 - i)

            pool.sem_inc(c_hlo, 2)
            pool.wait_ge(x_added, B)
            pool.memset(wrp[:, :, :, :].bitcast(F32), 0.0).then_inc(wr_zeros, 1)
            pool.wait_ge(wr_zeros, 1)
            pool.wait_ge(wr_split, 1)
            pool.tensor_tensor(wrp[:, 1, :, 0:E], wr[:, :, :], wrp[:, 0, :, 0:E].bitcast(F32), ALU.subtract).then_inc(wr_split, 1)
            split(0, 0)
            with pool.Fori(0, E - 2, 2) as e2:
                experts(e2, False)
            experts(E - 2, True)


def kernel(**inputs):
    import numpy as _np
    import concourse.bacc as _bacc
    from concourse.bass_utils import run_bass_kernel_spmd as _run

    def constants():
        r = _np.arange(P)[:, None] % WIN
        k = _np.arange(P)[None, :]
        own = (k < WIN) & (k <= r)
        std = (k >= r + 1) & (k <= r + WIN)
        swap = ((k < WIN) & (k <= r)) | ((k >= WIN) & (k - WIN >= r + 1))
        mask = _np.stack([_np.where(m, 0.0, -1e30) for m in (own, std, swap)], 1).astype(_np.float32)
        tri = _np.broadcast_to(_np.tril(_np.ones((E, E), _np.float32), -1), (P, E, E))
        kinds = _np.zeros((2, NKEY), _np.float32)
        kinds[0, :N_TXT] = 1.0
        kinds[1, N_TXT:] = 1.0
        return {"c_ident": _np.eye(P, dtype=_np.float32), "c_mask": mask, "c_tri": _np.ascontiguousarray(tri), "c_kind": kinds}

    data = {n: _np.asarray(v) for n, v in inputs.items()}
    for n in ("q_w", "q_b", "k_w", "k_b", "k_img_w", "k_img_b", "norm_q_w", "norm_k_w", "norm_k_img_w"):
        v = data[f"L0_xattn_{n}"]
        data[f"L0_xattn_{n}"] = v.reshape(NG, 4, XD, -1).transpose(0, 2, 1, 3).reshape(v.shape)
    for n in ("q", "k", "v", "k_img", "v_img", "o"):
        data[f"wT_{n}"] = _np.ascontiguousarray(data.pop(f"L0_xattn_{n}_w").T)
    data.update(constants())
    nc = _bacc.Bacc("TRN2", target_bir_lowering=False, num_devices=1)
    arrays, aps = {}, {}
    for name, v in data.items():
        v = _np.ascontiguousarray(v)
        arrays[f"in_{name}"] = v
        aps[name] = nc.dram_tensor(f"in_{name}", v.shape, mybir.dt.from_np(v.dtype), kind="ExternalInput").ap()
    out = nc.dram_tensor("out_x", (B, S, D), F32, kind="ExternalOutput").ap()
    decoder_layer(nc, aps, out)
    r = _run(nc, [arrays], core_ids=[0])
    return r.results[0]["out_x"]
```
